# Optimizing a Trainium2 kernel written in Bass

```python
import numpy as np
import jax
import jax.numpy as jnp

def _softmax(x, axis=-1):
    return jax.nn.softmax(x, axis=axis)

def _gelu(x):
    return jax.nn.gelu(x, approximate=True)

def _silu(x):
    return jax.nn.silu(x)

def _sigmoid(x):
    return jax.nn.sigmoid(x)

def _layernorm(x, axis=-1, eps=1e-05):
    m = jnp.mean(x, axis=axis, keepdims=True)
    v = jnp.var(x, axis=axis, keepdims=True)
    return (x - m) / jnp.sqrt(v + eps)

def _scatter_add(tgt, idx, src, axis=0):
    return tgt.at[idx].add(src)

def _segment_sum(src, seg, n):
    return jax.ops.segment_sum(src, seg, n)
kernel_name = 'mk_adj_ffn_d1_adj_r2_3376a8'

def setup_inputs(seed: int=0):
    np.random.seed(seed)
    _w = jnp.asarray

    def _rec_inputs():
        import jax
        import jax.numpy as jnp
        _gk = jax.random.key(seed)
        x = -0.0005207 + 1.001 * jax.random.normal(jax.random.fold_in(_gk, 1), (128, 128, 128), jnp.float32)
        _w = (1.0 + jnp.arange(128, dtype=jnp.float32)) ** (-0.5)
        _w = _w / _w.mean()
        _pij = jnp.clip(0.0625 * _w[:, None] * _w[None, :], 0.0, 1.0)
        _a = jax.random.uniform(jax.random.fold_in(_gk, 2), (128, 128)) < _pij
        _a = jnp.logical_or(_a, jnp.eye(128, dtype=bool))
        adj = _a
        return (x, adj)
    x, adj = _rec_inputs()

    def _L0_gnn_setup():
        import jax, jax.numpy as jnp
        import numpy as np
        T_WAKE = 0.1
        SIGMA_GRAV = 1.0
        EPS = 1e-08
        B, N, D = (2, 2048, 128)

        def _zero_diag(A):
            n = A.shape[-1]
            eye = jnp.eye(n, dtype=A.dtype)
            return A * (1.0 - eye)

        def _cosine_adjacency(z):
            norm = jnp.maximum(jnp.linalg.norm(z, axis=-1, keepdims=True), EPS)
            zn = z / norm
            A = jnp.maximum(jnp.einsum('bnd,bmd->bnm', zn, zn), 0.0)
            return _zero_diag(A)

        def _rbf_adjacency(z, sigma):
            sq = jnp.sum(z * z, axis=-1, keepdims=True)
            d2 = sq + jnp.swapaxes(sq, -1, -2) - 2.0 * jnp.einsum('bnd,bmd->bnm', z, z)
            d2 = jnp.maximum(d2, 0.0)
            A = jnp.exp(-d2 / (2.0 * sigma * sigma))
            return _zero_diag(A)

        def _row_stochastic_causal(A, causal_mask):
            A = A * causal_mask.astype(A.dtype)
            deg = jnp.maximum(jnp.sum(A, axis=-1, keepdims=True), EPS)
            return A / deg
        key = jax.random.key(seed)
        ks = jax.random.split(key, 5)
        s = 1.0 / np.sqrt(D)
        return {'h': jax.random.normal(ks[0], (B, N, D), dtype=jnp.float32), 'causal_mask': jnp.tril(jnp.ones((N, N), dtype=bool)), 'Wl': jax.random.normal(ks[1], (D, D), dtype=jnp.float32) * s, 'Wg': jax.random.normal(ks[2], (D, D), dtype=jnp.float32) * s, 'Wv': jax.random.normal(ks[3], (D, D), dtype=jnp.float32) * s, 'Wo': jax.random.normal(ks[4], (D, D), dtype=jnp.float32) * s}
    _L0_gnn_all = _L0_gnn_setup()
    _L0_gnn_in = {k: v for k, v in _L0_gnn_all.items() if k in ('Wl', 'Wg', 'Wv', 'Wo')}
    del _L0_gnn_all

    def _L0_ffn_setup():
        import jax, jax.numpy as jnp
        import numpy as np
        B, T, C = (64, 192, 128)
        NH, NKV = (4, 2)
        HD = C // NH
        NREP = NH // NKV
        NE, TOPK = (8, 2)
        HID = int(8 / 3 * C)
        EPS_RMS = 1e-06

        def _rope_tables(t_len):
            inv_freq = 1.0 / 10000.0 ** (np.arange(0, HD, 2, dtype=np.float32) / HD)
            t = np.arange(t_len, dtype=np.float32)
            freqs = np.outer(t, inv_freq)
            emb = np.concatenate([freqs, freqs], axis=-1)
            return (jnp.asarray(np.cos(emb)), jnp.asarray(np.sin(emb)))

        def _rotate_half(x):
            h = x.shape[-1] // 2
            return jnp.concatenate([-x[..., h:], x[..., :h]], axis=-1)

        def _rmsnorm(v, w):
            return v * jax.lax.rsqrt(jnp.mean(v * v, axis=-1, keepdims=True) + EPS_RMS) * w
        key = jax.random.key(seed)
        ks = jax.random.split(key, 10)
        s = lambda k, shape: jax.random.normal(k, shape, jnp.float32) * 0.02
        return {'x': jax.random.normal(ks[0], (B, T, C), jnp.float32), 'ln1_w': jnp.ones((C,), jnp.float32), 'ln2_w': jnp.ones((C,), jnp.float32), 'wq': s(ks[1], (NH * HD, C)), 'wk': s(ks[2], (NKV * HD, C)), 'wv': s(ks[3], (NKV * HD, C)), 'wo': s(ks[4], (C, C)), 'router_w': s(ks[5], (NE, C)), 'w1': s(ks[6], (NE, HID, C)), 'w2': s(ks[7], (NE, C, HID)), 'w3': s(ks[8], (NE, HID, C))}
    _L0_ffn_all = _L0_ffn_setup()
    _L0_ffn_in = {k: v for k, v in _L0_ffn_all.items() if k in ('ln1_w', 'ln2_w', 'wq', 'wk', 'wv', 'wo', 'router_w', 'w1', 'w2', 'w3')}
    del _L0_ffn_all
    return {'x': x, 'adj': adj, 'L0_gnn_Wl': _L0_gnn_in['Wl'], 'L0_gnn_Wg': _L0_gnn_in['Wg'], 'L0_gnn_Wv': _L0_gnn_in['Wv'], 'L0_gnn_Wo': _L0_gnn_in['Wo'], 'L0_ffn_ln1_w': _L0_ffn_in['ln1_w'], 'L0_ffn_ln2_w': _L0_ffn_in['ln2_w'], 'L0_ffn_wq': _L0_ffn_in['wq'], 'L0_ffn_wk': _L0_ffn_in['wk'], 'L0_ffn_wv': _L0_ffn_in['wv'], 'L0_ffn_wo': _L0_ffn_in['wo'], 'L0_ffn_router_w': _L0_ffn_in['router_w'], 'L0_ffn_w1': _L0_ffn_in['w1'], 'L0_ffn_w2': _L0_ffn_in['w2'], 'L0_ffn_w3': _L0_ffn_in['w3']}

def reference(x, adj, L0_gnn_Wl, L0_gnn_Wg, L0_gnn_Wv, L0_gnn_Wo, L0_ffn_ln1_w, L0_ffn_ln2_w, L0_ffn_wq, L0_ffn_wk, L0_ffn_wv, L0_ffn_wo, L0_ffn_router_w, L0_ffn_w1, L0_ffn_w2, L0_ffn_w3):
    import jax
    import jax.numpy as jnp

    def _L0_gnn_ref(h, causal_mask, Wl, Wg, Wv, Wo):
        import jax, jax.numpy as jnp
        import numpy as np
        T_WAKE = 0.1
        SIGMA_GRAV = 1.0
        EPS = 1e-08
        B, N, D = (2, 2048, 128)

        def _zero_diag(A):
            n = A.shape[-1]
            eye = jnp.eye(n, dtype=A.dtype)
            return A * (1.0 - eye)

        def _cosine_adjacency(z):
            norm = jnp.maximum(jnp.linalg.norm(z, axis=-1, keepdims=True), EPS)
            zn = z / norm
            A = jnp.maximum(jnp.einsum('bnd,bmd->bnm', zn, zn), 0.0)
            return _zero_diag(A)

        def _rbf_adjacency(z, sigma):
            sq = jnp.sum(z * z, axis=-1, keepdims=True)
            d2 = sq + jnp.swapaxes(sq, -1, -2) - 2.0 * jnp.einsum('bnd,bmd->bnm', z, z)
            d2 = jnp.maximum(d2, 0.0)
            A = jnp.exp(-d2 / (2.0 * sigma * sigma))
            return _zero_diag(A)

        def _row_stochastic_causal(A, causal_mask):
            A = A * causal_mask.astype(A.dtype)
            deg = jnp.maximum(jnp.sum(A, axis=-1, keepdims=True), EPS)
            return A / deg
        z_l = h @ Wl
        z_g = h @ Wg
        v = h @ Wv
        A_l = _cosine_adjacency(z_l)
        A_g = _rbf_adjacency(z_g, SIGMA_GRAV)
        K_l = _row_stochastic_causal(A_l, causal_mask)
        K_g = _row_stochastic_causal(A_g, causal_mask)
        w_l, w_g = (1.0 - T_WAKE, T_WAKE)
        K = w_l * K_l + w_g * K_g
        return jnp.einsum('bnm,bmd->bnd', K, v) @ Wo

    def _L0_ffn_ref(x, ln1_w, ln2_w, wq, wk, wv, wo, router_w, w1, w2, w3):
        import jax, jax.numpy as jnp
        import numpy as np
        B, T, C = (64, 192, 128)
        NH, NKV = (4, 2)
        HD = C // NH
        NREP = NH // NKV
        NE, TOPK = (8, 2)
        HID = int(8 / 3 * C)
        EPS_RMS = 1e-06

        def _rope_tables(t_len):
            inv_freq = 1.0 / 10000.0 ** (np.arange(0, HD, 2, dtype=np.float32) / HD)
            t = np.arange(t_len, dtype=np.float32)
            freqs = np.outer(t, inv_freq)
            emb = np.concatenate([freqs, freqs], axis=-1)
            return (jnp.asarray(np.cos(emb)), jnp.asarray(np.sin(emb)))

        def _rotate_half(x):
            h = x.shape[-1] // 2
            return jnp.concatenate([-x[..., h:], x[..., :h]], axis=-1)

        def _rmsnorm(v, w):
            return v * jax.lax.rsqrt(jnp.mean(v * v, axis=-1, keepdims=True) + EPS_RMS) * w
        Bx, Tx, Cx = x.shape
        h = _rmsnorm(x, ln1_w)
        q = (h @ wq.T).reshape(Bx, Tx, NH, HD).transpose(0, 2, 1, 3)
        k = (h @ wk.T).reshape(Bx, Tx, NKV, HD).transpose(0, 2, 1, 3)
        v = (h @ wv.T).reshape(Bx, Tx, NKV, HD).transpose(0, 2, 1, 3)
        cos, sin = _rope_tables(Tx)
        cos, sin = (cos[None, None], sin[None, None])
        q = q * cos + _rotate_half(q) * sin
        k = k * cos + _rotate_half(k) * sin
        k = jnp.repeat(k, NREP, axis=1)
        v = jnp.repeat(v, NREP, axis=1)
        scores = jnp.einsum('bhtd,bhsd->bhts', q, k) / jnp.sqrt(jnp.float32(HD))
        causal = jnp.tril(jnp.ones((Tx, Tx), dtype=bool))
        scores = jnp.where(causal[None, None], scores, jnp.float32(-1e+30))
        att = jax.nn.softmax(scores, axis=-1)
        y = jnp.einsum('bhts,bhsd->bhtd', att, v).transpose(0, 2, 1, 3).reshape(Bx, Tx, Cx)
        x = x + y @ wo.T
        flat = _rmsnorm(x, ln2_w).reshape(-1, Cx)
        probs = jax.nn.softmax(flat @ router_w.T, axis=-1)
        tp, ti = jax.lax.top_k(probs, TOPK)
        tp = tp / (jnp.sum(tp, axis=-1, keepdims=True) + 1e-09)
        weights = jnp.sum(tp[..., None] * jax.nn.one_hot(ti, NE, dtype=flat.dtype), axis=1)
        out = jnp.zeros_like(flat)
        for e in range(NE):
            hh = jax.nn.silu(flat @ w1[e].T) * (flat @ w3[e].T)
            out = out + weights[:, e:e + 1] * (hh @ w2[e].T)
        return x + out.reshape(Bx, Tx, Cx)
    x = x + _L0_gnn_ref(_layernorm(x, axis=-1), adj, L0_gnn_Wl, L0_gnn_Wg, L0_gnn_Wv, L0_gnn_Wo)
    x = x + _L0_ffn_ref(_layernorm(x, axis=-1), L0_ffn_ln1_w, L0_ffn_ln2_w, L0_ffn_wq, L0_ffn_wk, L0_ffn_wv, L0_ffn_wo, L0_ffn_router_w, L0_ffn_w1, L0_ffn_w2, L0_ffn_w3)
    return x

_drawn_inputs = setup_inputs


def setup_inputs(seed=0):
    import zlib

    import numpy as np

    out = dict(_drawn_inputs(seed))
    spreads = {'L0_ffn_ln1_w': (1.0, 0.6), 'L0_ffn_ln2_w': (1.0, 0.6)}
    factors = {'L0_ffn_wq': 8.0,
     'L0_ffn_wk': 8.0,
     'L0_ffn_wv': 8.0,
     'L0_ffn_wo': 8.0,
     'L0_ffn_router_w': 8.0,
     'L0_ffn_w1': 8.0,
     'L0_ffn_w2': 8.0,
     'L0_ffn_w3': 8.0}
    for name, (base, spread) in spreads.items():
        noise = np.random.default_rng([zlib.crc32(name.encode()), seed]).standard_normal(out[name].shape)
        drawn = base * np.exp(spread * noise) if base else spread * noise
        out[name] = jnp.asarray(drawn.astype(out[name].dtype))
    for name, factor in factors.items():
        out[name] = (out[name] * factor).astype(out[name].dtype)
    return out
```

```python
from contextlib import ExitStack

import numpy as np

import concourse.bass as bass
from concourse import mybir

ALU = mybir.AluOpType
ACT = mybir.ActivationFunctionType
F32 = mybir.dt.float32
BF16 = mybir.dt.bfloat16
I32 = mybir.dt.int32
U32 = mybir.dt.uint32
U8 = mybir.dt.uint8
AX_X = mybir.AxisListType.X

P = 128
NB = 128
D = 128
G = 4
NG = NB // G
NH, NKV, HD = 4, 2, 32
NREP = NH // NKV
QK = (NH + NKV) * HD
QKV = QK + NKV * HD
NE, HID = 8, int(8 / 3 * D)
N_TOK = NB * P
HEADS = [k * NREP + r for r in range(NREP) for k in range(NKV)]
T_WAKE = 0.1
EPS = 1e-8
EPS_LN = 1e-5
EPS_RMS = 1e-6
NEG = -1e30
SCALE = float(HD) ** -0.5

ROWS = 512
SUB = ROWS // P
REGION = N_TOK + ROWS
ROW_W = D + 4
COL_ID, COL_EXPERT, COL_GATE = D, D + 1, D + 2
N_TILES = 2 * N_TOK // ROWS + NE
CHUNKS = [(c, min(P, HID - c)) for c in range(0, HID, P)]
NC = len(CHUNKS)
W_COLS = 2 * HID + NC * D
FINAL = 16

C_IDENT, C_CAUSAL, C_UPPER, C_COS, C_SIN, C_TOKEN, C_BASE, C_IOTA, C_UPTO, C_STEP, C_TILE, C_PAD = np.cumsum(
    [0, P, P, P, QK, QK, G, NE, NE, NE * NE, N_TOK // ROWS, N_TILES]).tolist()
C_END = C_PAD + SUB


def constants():
    t = np.zeros((P, C_END), np.float32)
    i = np.arange(P)
    t[:, C_IDENT:C_CAUSAL] = np.eye(P)
    t[:, C_CAUSAL:C_UPPER] = np.where(i[None, :] <= i[:, None], 0.0, NEG)
    t[:, C_UPPER:C_COS] = i[:, None] < i[None, :]
    inv_freq = 1.0 / 10000.0 ** (np.arange(0, HD, 2, dtype=np.float32) / HD)
    freqs = np.outer(i.astype(np.float32), inv_freq)
    cos = np.cos(np.concatenate([freqs, freqs], -1))
    sin = np.sin(np.concatenate([-freqs, freqs], -1))
    t[:, C_COS:C_SIN] = np.tile(cos, (1, NH + NKV))
    t[:, C_SIN:C_TOKEN] = np.tile(sin, (1, NH + NKV))
    t[:, C_TOKEN:C_BASE] = i[:, None] * NB + np.arange(G)[None, :]
    t[:, C_BASE:C_IOTA] = np.arange(NE) * REGION
    t[:, C_IOTA:C_UPTO] = np.arange(NE)
    t[:, C_UPTO:C_STEP] = np.tril(np.ones((NE, NE))).reshape(-1)
    t[:, C_STEP:C_TILE] = np.arange(N_TOK // ROWS) * ROWS
    t[:, C_TILE:C_PAD] = np.arange(N_TILES)
    t[:, C_PAD:C_END] = N_TOK + i[:, None] * SUB + np.arange(SUB)[None, :]
    return t


def later(g):
    return not isinstance(g, int) or g > 0


def build(nc, x, adj_t, wl, wg, wv_t, wo_gnn, ln1, ln2, wqkv_t, wo_t, router_t, w1_t, w2_t, w3_t, table, out):
    with ExitStack() as ctx:
        def sb(name, shape, dt=F32):
            return ctx.enter_context(nc.sbuf_tensor(name, shape, dt))

        def sem(name):
            return ctx.enter_context(nc.semaphore(name))

        bank_a = [ctx.enter_context(nc.psum_tensor(f"bank_a{i}", [P, 512], F32)) for i in range(3)]
        bank_b = [ctx.enter_context(nc.psum_tensor(f"bank_b{i}", [P, 512], F32)) for i in range(3)]
        bank_c = [ctx.enter_context(nc.psum_tensor(f"bank_c{i}", [P, 512], F32)) for i in range(2)]

        def tiles(bank, n=G):
            return bank[:].rearrange("p (t d) -> p t d", t=n)

        tab = sb("tab", [P, C_END])
        ident = tab[:, C_IDENT:C_CAUSAL]
        bank_in, bank_up, bank_gate, bank_down = bank_a[0], bank_a[1:3], bank_b[0:2], [bank_b[2], bank_c[0]]
        ident_b = sb("ident_b", [P, P], BF16)
        causal_b = sb("causal_b", [P, P], BF16)
        upper_b = sb("upper_b", [P, P], BF16)
        ones_b = sb("ones_b", [P, P], BF16)
        minus_half = sb("minus_half", [P, P])
        adj_bytes = sb("adj_bytes", [P, P // 4], I32)
        adj_f = sb("adj_f", [P, P])
        mask_l = sb("mask_l", [P, P])
        mask_g = sb("mask_g", [P, P])
        w_l = sb("w_l", [P, D])
        w_g = sb("w_g", [P, D])
        w_v_t = sb("w_v_t", [P, D])
        w_o_gnn = sb("w_o_gnn", [P, D])
        w_vo = sb("w_vo", [P, D])
        ln1_col = sb("ln1_col", [P, 1])
        ln2_row = sb("ln2_row", [P, D])
        w_qkv_raw = sb("w_qkv_raw", [P, QKV])
        w_qkv = sb("w_qkv", [P, QKV])
        w_o = sb("w_o", [P, D])
        w_router = sb("w_router", [P, NE])

        resid = sb("resid", [P, NB, D])

        w_all = sb("w_all", [P, NE, W_COLS])
        w_buf = sb("w_buf", [P, 2, W_COLS])
        in_rows = sb("in_rows", [P, 2, SUB, ROW_W])
        pad_rows = sb("pad_rows", [P, SUB, ROW_W])
        filled = sb("filled", [P, NE])
        region_end_i = sb("region_end_i", [P, NE], I32)

        lasting, ctx = ctx, ExitStack()

        a_st = sb("a_st", [P, G, 6])
        a_mv = sb("a_mv", [P, G, 2])
        a_var = sb("a_var", [P, G])
        a_rstd = sb("a_rstd", [P, G])
        a_h = sb("a_h", [P, G, D])
        a_hT = sb("a_hT", [P, G, P])
        zl = sb("zl", [P, G, P])
        zg = sb("zg", [P, G, P])
        zl2 = sb("zl2", [P, G, P])
        zg2 = sb("zg2", [P, G, P])
        sq_l = sb("sq_l", [P, G])
        inv_norm = sb("inv_norm", [P, G])
        guard = sb("guard", [P, G])
        v_l = sb("v_l", [P, G, D + 1])
        v_g = sb("v_g", [P, G, D + 1])
        adj_l = sb("adj_l", [P, G, P])
        arg_g = sb("arg_g", [P, G, P])
        adj_g = sb("adj_g", [P, G, P])
        den_l = sb("den_l", [P, G])
        den_g = sb("den_g", [P, G])
        rec_l = sb("rec_l", [P, G])
        rec_g = sb("rec_g", [P, G])
        out_l = sb("out_l", [P, G, D])
        out_g = sb("out_g", [P, G, D])

        b_st = sb("b_st", [P, G, 6])
        b_mv = sb("b_mv", [P, G, 2])
        b_var = sb("b_var", [P, 2, G])
        b_rs = sb("b_rs", [P, 2, G])
        b_rec = sb("b_rec", [P, G])
        b_ratio = sb("b_ratio", [P, G])
        b_h = sb("b_h", [P, G, D])
        h2 = sb("h2", [P, G, D])
        b_hT = sb("b_hT", [P, G, P])
        rope_c = sb("rope_c", [P, G, QK])
        swapped = sb("swapped", [P, G, QK])
        rope_s = sb("rope_s", [P, G, QK])
        roped = sb("roped", [P, G, QK])
        v1 = sb("v1", [P, G, NKV, HD + 1])
        qT = sb("qT", [P, G, P])
        kT = sb("kT", [P, G, P])
        row_max = sb("row_max", [P, NH, G])
        shifted = sb("shifted", [P, 2, G, P])
        probs = sb("probs", [P, NH, G, P])

        probs_t = sb("probs_t", [P, NH, G, P])
        y_rec = sb("y_rec", [P, G * NH])
        y = sb("y", [P, G, D])
        yT = sb("yT", [P, G, P])
        xf = sb("xf", [P, G, D])
        sq_junk = sb("sq_junk", [P, G, D], BF16)
        sum_sq = sb("sum_sq", [P, G])
        ms = sb("ms", [P, G])
        rms = sb("rms", [P, G])
        half_col = sb("half_col", [P, 2 * G])

        flat_rows = sb("flat_rows", [P, G, ROW_W])
        flatT = sb("flatT", [P, G, P])
        token_id = sb("token_id", [P, G])
        best = sb("best", [P, G, NE])
        best_at = sb("best_at", [P, G, NE], U32)
        choice = sb("choice", [P, G * 2])
        pick = sb("pick", [P, G, 2, NE])
        chosen_b = sb("chosen_b", [P, G, NE], BF16)
        below = sb("below", [P, G, NE])
        weight = sb("weight", [P, G, NE])
        total = sb("total", [P, G])
        pair = sb("pair", [P, G])
        denom = sb("denom", [P, G])
        denom_rec = sb("denom_rec", [P, G])
        place = sb("place", [P, G + 1, NE])
        picked = sb("picked", [P, G, 2, NE])
        place_f = sb("place_f", [P, G * 2])
        place_i = sb("place_i", [P, G * 2], I32)

        ctx.close()
        ctx = lasting
        counts = sb("counts", [P, NE])
        over = sb("over", [P, NE, N_TOK // ROWS])
        n_tiles = sb("n_tiles", [P, NE])
        upto = sb("upto", [P, NE, NE])
        tiles_upto = sb("tiles_upto", [P, NE])
        passed = sb("passed", [P, N_TILES, NE])
        passed_n = sb("passed_n", [P, N_TILES, NE])
        tile_expert = sb("tile_expert", [P, N_TILES])
        tile_first = sb("tile_first", [P, N_TILES])
        tile_at = sb("tile_at", [P, N_TILES])
        tile_row = sb("tile_row", [P, N_TILES])
        tile_row_i = sb("tile_row_i", [P, N_TILES], I32)
        tile_weights_i = sb("tile_weights_i", [P, N_TILES], I32)
        in_t = sb("in_t", [P, 2, ROWS])
        silu = sb("silu", [P, 2, ROWS])
        hidden = sb("hidden", [P, 2, NC, ROWS])
        second = sb("second", [P, 2, SUB])
        gate_diff = sb("gate_diff", [P, 2, SUB])
        gate_step = sb("gate_step", [P, 2, SUB])
        gate = sb("gate", [P, 2, SUB])
        dest_f = sb("dest_f", [P, 2, SUB])
        dest_i = sb("dest_i", [P, 2, SUB], I32)
        out_rows = sb("out_rows", [P, 2, SUB, D])
        final_in = sb("final_in", [P, 2, 2, FINAL, D])

        grouped = nc.dram_tensor("grouped", (NE * REGION + ROWS, ROW_W), F32, kind="Internal").ap()
        expert_out = nc.dram_tensor("expert_out", (2 * N_TOK + ROWS, D), F32, kind="Internal").ap()

        def sems(names):
            return [sem(name) for name in names.split()]

        const_loaded, adj_loaded, w_loaded, consts_set, adj_set, mask_set, w_qkv_set, wvo_ps = sems(
            "const_loaded adj_loaded w_loaded consts_set adj_set mask_set w_qkv_set wvo_ps")
        wvo_set, ones_set = sems("wvo_set ones_set")
        x_loaded = sem("x_loaded")
        a_stats, a_aggr, a_var_set, a_rstd_set, a_norm, a_hT_ps, a_hT_set, zl_ps = sems(
            "a_stats a_aggr a_var_set a_rstd_set a_norm a_hT_ps a_hT_set zl_ps")
        zg_ps, zl_set, zg_set, zl_sq, zg_sq = sems("zg_ps zl_set zg_set zl_sq zg_sq")
        sql_ps, sql_set, inv_set, guard_set, v_ps, vg_set, vl_set, vl_col_set = sems(
            "sql_ps sql_set inv_set guard_set v_ps vg_set vl_set vl_col_set")
        gl_ps, adj_l_set, gg_ps, arg_g_set, adj_g_set = sems("gl_ps adj_l_set gg_ps arg_g_set adj_g_set")
        outl_ps0, outl_ps1, outg_ps0, outg_ps1, denl_set, recl_set, outl_set0, outl_set1 = sems(
            "outl_ps0 outl_ps1 outg_ps0 outg_ps1 denl_set recl_set outl_set0 outl_set1")
        deng_set, recg_set, outg_set0, outg_set1 = sems("deng_set recg_set outg_set0 outg_set1")
        x1_half, x1_set = sems("x1_half x1_set")
        b_stats, b_aggr, b_var_set, b_rs_set, b_rec_set, b_ratio_set, b_norm, h2_set = sems(
            "b_stats b_aggr b_var_set b_rs_set b_rec_set b_ratio_set b_norm h2_set")
        b_hT_ps, b_hT_set, qkv_ps0, qkv_ps1 = sems("b_hT_ps b_hT_set qkv_ps0 qkv_ps1")
        swap_set0, swap_set1, v1_set, rope_c_set, rope_s_set, roped_set, qT_ps, kT_ps = sems(
            "swap_set0 swap_set1 v1_set rope_c_set rope_s_set roped_set qT_ps kT_ps")
        qT_set, kT_set = sems("qT_set kT_set")
        s_ps, max_set, shift_set = sems("s_ps max_set shift_set")
        prob_set = sem("prob_set")
        pT_ps, pT_set, y_ps0, y_ps1, y_rec0, y_rec1, y_set0, y_set1 = sems("pT_ps pT_set y_ps0 y_ps1 y_rec0 y_rec1 y_set0 y_set1")
        yT_ps, yT_set = sems("yT_ps yT_set")
        attn_ps, xf_set, sq_set, ms_set, rms_set, resid_set, out_stored = sems(
            "attn_ps xf_set sq_set ms_set rms_set resid_set out_stored")
        flat_set, id_set, id_next, flat_ps, flatT_set, router_ps, best_set, best_at_set = sems(
            "flat_set id_set id_next flat_ps flatT_set router_ps best_set best_at_set")
        choice_set, expert_set, pick_set, chosen_set = sems("choice_set expert_set pick_set chosen_set")
        rank_ps, below_set, weight_set, total_set, pair_set, denom_set, denom_rec_set, gates_set = sems(
            "rank_ps below_set weight_set total_set pair_set denom_set denom_rec_set gates_set")
        place_set, filled_set, picked_set = sems("place_set filled_set picked_set")
        place_f_set, place_i_set, scattered = sems("place_f_set place_i_set scattered")
        wall_loaded, pad_zero, pad_set, pad_stored, table_step, table_set = sems(
            "wall_loaded pad_zero pad_set pad_stored table_step table_set")
        wbuf_loaded0, wbuf_loaded1, rows_loaded0, rows_loaded1, inT_ps, inT_set, up_ps, gate_ps = sems(
            "wbuf_loaded0 wbuf_loaded1 rows_loaded0 rows_loaded1 inT_ps inT_set up_ps gate_ps")
        silu_set, hidden_set, down_ps = sems("silu_set hidden_set down_ps")
        second_set, gdiff_set, gstep_set, gate_set, destf_set, dest_set, outrows_set, placed0 = sems(
            "second_set gdiff_set gstep_set gate_set destf_set dest_set outrows_set placed0")
        placed1 = sem("placed1")
        final_loaded0, final_loaded1, sum_half, sum_set = sems("final_loaded0 final_loaded1 sum_half sum_set")

        block = ctx.enter_context(nc.Block())

        @block.sync
        def _(sp):
            sp.dma_start(tab[:], table).then_inc(const_loaded, 16)
            sp.dma_start(adj_bytes[:], adj_t).then_inc(adj_loaded, 16)
            for dst, src in ((w_l, wl), (w_g, wg), (w_v_t, wv_t), (w_o_gnn, wo_gnn), (ln1_col, ln1), (w_qkv_raw, wqkv_t),
                             (w_o, wo_t), (w_router, router_t)):
                sp.dma_start(dst[:], src).then_inc(w_loaded, 16)
            sp.dma_start(ln2_row[:], ln2.partition_broadcast(P)).then_inc(w_loaded, 16)
            sp.dma_start(resid[:, 0:G, :], x[:, 0:G, :]).then_inc(x_loaded, 16)
            with sp.Fori(1, NG) as g:
                sp.wait_ge(x_loaded, g * 16)
                sp.dma_start(resid[:, bass.ds(g * G, G), :], x[:, bass.ds(g * G, G), :]).then_inc(x_loaded, 16)
            sp.wait_ge(ones_set, 1)
            sp.dma_start(w_all[:, :, 0:HID], w1_t).then_inc(wall_loaded, 16)
            sp.dma_start(w_all[:, :, HID:2 * HID], w3_t).then_inc(wall_loaded, 16)
            for c, (c0, cn) in enumerate(CHUNKS):
                w2_at = 2 * HID + c * D
                sp.dma_start(w_all[0:cn, :, w2_at:w2_at + D], w2_t[c0:c0 + cn]).then_inc(wall_loaded, 16)
            pads = grouped.rearrange("n w -> n w")
            sp.wait_ge(pad_set, 1)
            sp.dma_start(pads[NE * REGION:NE * REGION + ROWS].rearrange("(p i) w -> p i w", i=SUB), pad_rows[:]).then_inc(
                pad_stored, 16)
            sp.wait_ge(table_set, 1)
            for e in range(NE):
                end = sp.value_load(region_end_i[0:1, e:e + 1], min_val=0, max_val=NE * REGION - ROWS)
                sp.dma_start(pads[bass.ds(end, ROWS)].rearrange("(p i) w -> p i w", i=SUB), pad_rows[:]).then_inc(pad_stored, 16)
            sp.wait_ge(scattered, NG * G * 2 * 16)
            sp.wait_ge(pad_stored, (NE + 1) * 16)
            sp.wait_ge(wall_loaded, (2 + NC) * 16)

            def load_tile(pair_no, u):
                j = pair_no * 2 + u
                if later(pair_no):
                    sp.wait_ge(down_ps, j - 1)
                    sp.wait_ge(inT_ps, j - 1)
                    sp.wait_ge(gate_set, j - 1)
                    sp.wait_ge(destf_set, j - 1)
                    sp.wait_ge(gdiff_set, j - 1)
                row = sp.value_load(tile_row_i[0:1, bass.ds(j, 1)], min_val=0, max_val=NE * REGION)
                sp.dma_start(in_rows[:, u, :, :], grouped[bass.ds(row, ROWS)].rearrange("(p i) w -> p i w", i=SUB)).then_inc(
                    [rows_loaded0, rows_loaded1][u], 16)
                e = sp.value_load(tile_weights_i[0:1, bass.ds(j, 1)], min_val=0, max_val=NE - 1)
                sp.dma_start(w_buf[:, u, :], w_all[:, bass.ds(e, 1), :].rearrange("p a w -> p (a w)")).then_inc(
                    [wbuf_loaded0, wbuf_loaded1][u], 16)

            load_tile(0, 0)
            load_tile(0, 1)
            with sp.Fori(1, N_TILES // 2) as k:
                load_tile(k, 0)
                load_tile(k, 1)

            sp.wait_ge(placed0, N_TILES // 2 * SUB * 16)
            sp.wait_ge(placed1, N_TILES // 2 * SUB * 16)
            halves = [expert_out[i * N_TOK:(i + 1) * N_TOK].rearrange("(p b) d -> p b d", b=NB) for i in range(2)]
            for i in range(NB // FINAL):
                if i >= 2:
                    sp.wait_ge(sum_set, i - 1)
                for n in range(2):
                    sp.dma_start(final_in[:, i % 2, n, :, :], halves[n][:, i * FINAL:(i + 1) * FINAL, :]).then_inc(
                        [final_loaded0, final_loaded1][i % 2], 16)

        W_LOADED = 16 * 9

        @block.gpsimd
        def _(pool):
            nc.gpsimd.memset(half_col[:], -0.5)
            nc.gpsimd.memset(minus_half[:], -0.5)
            nc.gpsimd.memset(v_g[:], 1.0)
            nc.gpsimd.memset(v1[:], 1.0)
            nc.gpsimd.memset(w_all[:, :, 2 * HID + (NC - 1) * D:], 0.0)
            nc.gpsimd.memset(ones_b[:], 1.0).then_inc(ones_set, 1)
            nc.gpsimd.memset(pad_rows[:], 0.0).then_inc(pad_zero, 1)
            pool.wait_ge(adj_set, 1)
            nc.gpsimd.affine_select(out=mask_l[:], in_=adj_f[:], compare_op=ALU.not_equal, fill=0.0, base=0,
                                    pattern=[[-1, P]], channel_multiplier=1).then_inc(mask_set, 1)
            pool.wait_ge(mask_set, 1)
            nc.gpsimd.tensor_scalar(mask_g[:], mask_l[:], 1.0, -NEG, ALU.subtract, ALU.mult).then_inc(mask_set, 1)

            def a_rstd_pow(g):
                pool.wait_ge(a_var_set, g + 1)
                if later(g):
                    pool.wait_ge(a_norm, g)
                nc.gpsimd.tensor_tensor(a_rstd[:], a_var[:], half_col[:, 0:G], ALU.pow).then_inc(a_rstd_set, 1)

            def a_squares(g):
                pool.wait_ge(zg_set, g + 1)
                if later(g):
                    pool.wait_ge(gg_ps, g)
                nc.gpsimd.tensor_tensor(zg2[:], zg[:], zg[:], ALU.mult).then_inc(zg_sq, 1)

            def a_squares_l(g):
                pool.wait_ge(zl_set, g + 1)
                if later(g):
                    pool.wait_ge(sql_ps, g)
                nc.gpsimd.tensor_tensor(zl2[:], zl[:], zl[:], ALU.mult).then_inc(zl_sq, 1)

            def a_inverse_norms(g):
                pool.wait_ge(sql_set, g + 1)
                if later(g):
                    pool.wait_ge(vl_set, g)
                nc.gpsimd.tensor_tensor(inv_norm[:], sq_l[:], half_col[:, 0:G], ALU.pow).then_inc(inv_set, 1)
                pool.wait_ge(inv_set, g + 1)
                if later(g):
                    pool.wait_ge(denl_set, g)
                nc.gpsimd.tensor_tensor(guard[:], sq_l[:], inv_norm[:], ALU.mult).then_inc(guard_set, 1)
                if later(g):
                    pool.wait_ge(outl_ps1, g)
                pool.nop(nofuse=True)
                nc.gpsimd.tensor_copy(v_l[:, :, D], inv_norm[:]).then_inc(vl_col_set, 1)

            def a_add_l(g):
                pool.wait_ge(outl_set1, g + 1)
                pool.nop(nofuse=True)
                xg = resid[:, bass.ds(g * G, G), :]
                nc.gpsimd.tensor_tensor(xg, out_l[:], xg, ALU.add).then_inc(x1_half, 1)

            def a_add_g(g):
                pool.wait_ge(x1_half, g + 1)
                pool.wait_ge(outg_set1, g + 1)
                pool.nop(nofuse=True)
                xg = resid[:, bass.ds(g * G, G), :]
                nc.gpsimd.tensor_tensor(xg, out_g[:], xg, ALU.add).then_inc(x1_set, 1)

            def b_pow(g):
                pool.wait_ge(b_var_set, g + 1)
                if later(g):
                    pool.wait_ge(b_ratio_set, g)
                nc.gpsimd.tensor_tensor(b_rs[:].rearrange("p a b -> p (a b)"), b_var[:].rearrange("p a b -> p (a b)"),
                                        half_col[:], ALU.pow).then_inc(b_rs_set, 1)

            def b_h2(g):
                pool.wait_ge(b_rec_set, g + 1)
                nc.gpsimd.tensor_tensor(b_ratio[:], b_rs[:, 0, :], b_rec[:], ALU.mult).then_inc(b_ratio_set, 1)
                pool.wait_ge(b_ratio_set, g + 1)
                pool.wait_ge(b_norm, g + 1)
                if later(g):
                    pool.wait_ge(xf_set, g)
                nc.gpsimd.tensor_tensor(h2[:], b_h[:], b_ratio[:].unsqueeze(2).broadcast_to([P, G, D]),
                                        ALU.mult).then_inc(h2_set, 1)

            def b_rope_sin(g, half):
                pool.wait_ge([swap_set0, swap_set1][half], g + 1)
                if later(g):
                    pool.wait_ge(roped_set, g)
                t = slice(2 * half, 2 * half + 2)
                sin = tab[:, C_SIN:C_TOKEN].unsqueeze(1).broadcast_to([P, 2, QK])
                nc.gpsimd.tensor_tensor(rope_s[:, t, :], swapped[:, t, :], sin, ALU.mult).then_inc(rope_s_set, 1)

            def c_rms_pow(g):
                pool.wait_ge(ms_set, g + 1)
                nc.gpsimd.tensor_tensor(rms[:], ms[:], half_col[:, 0:G], ALU.pow).then_inc(rms_set, 1)

            def c_scatter(g):
                pool.wait_ge(flat_set, g + 1)
                pool.wait_ge(id_set, g + 1)
                pool.wait_ge(expert_set, g + 1)
                pool.wait_ge(gates_set, g + 1)
                pool.wait_ge(place_i_set, g + 1)
                pool.nop(nofuse=True)
                for t in range(G):
                    for slot in range(2):
                        nc.gpsimd.indirect_dma_start(
                            out=grouped,
                            out_offset=bass.IndirectOffsetOnAxis(ap=place_i[:, 2 * t + slot:2 * t + slot + 1].bitcast(U32), axis=0),
                            in_=flat_rows[:, t, :], in_offset=None).then_inc(scattered, 16)

            def c_resid(g):
                pool.wait_ge(xf_set, g + 1)
                pool.nop(nofuse=True)
                rg = resid[:, bass.ds(g * G, G), :]
                nc.gpsimd.tensor_tensor(rg, xf[:], rg, ALU.add).then_inc(resid_set, 1)

            def step(a, b, c):
                if a is not None:
                    a_rstd_pow(a)
                if b is not None:
                    b_pow(b)
                    b_h2(b)
                if a is not None:
                    a_squares_l(a)
                    a_squares(a)
                if b is not None:
                    b_rope_sin(b, 0)
                    b_rope_sin(b, 1)
                if a is not None:
                    a_inverse_norms(a)
                if c is not None:
                    c_resid(c)
                    c_rms_pow(c)
                if a is not None:
                    a_add_l(a)
                    a_add_g(a)
                if c is not None:
                    c_scatter(c)

            step(0, None, None)
            step(1, 0, None)
            step(2, 1, 0)
            with pool.Fori(1, NG - 2) as k:
                step(k + 2, k + 1, k)
            step(None, NG - 1, NG - 2)
            step(None, None, NG - 1)

            def place_tile(pair_no, u):
                j = pair_no * 2 + u
                pool.wait_ge(dest_set, j + 1)
                pool.wait_ge(outrows_set, j + 1)
                if u == 1:
                    pool.wait_ge(placed0, pair_no * (SUB * 16) + SUB * 16)
                elif later(pair_no):
                    pool.wait_ge(placed1, pair_no * (SUB * 16))
                pool.nop(nofuse=True)
                for i in range(SUB):
                    nc.gpsimd.indirect_dma_start(
                        out=expert_out, out_offset=bass.IndirectOffsetOnAxis(ap=dest_i[:, u, i:i + 1].bitcast(U32), axis=0),
                        in_=out_rows[:, u, i, :], in_offset=None).then_inc([placed0, placed1][u], 16)

            place_tile(0, 0)
            place_tile(0, 1)
            with pool.Fori(1, N_TILES // 2) as k:
                place_tile(k, 0)
                place_tile(k, 1)

        @block.vector
        def _(dve):
            dve.wait_ge(const_loaded, 16)
            nc.vector.tensor_copy(ident_b[:], ident)
            nc.vector.tensor_copy(causal_b[:], tab[:, C_CAUSAL:C_UPPER])
            nc.vector.tensor_copy(upper_b[:], tab[:, C_UPPER:C_COS]).then_inc(consts_set, 1)
            dve.wait_ge(adj_loaded, 16)
            nc.vector.tensor_copy(adj_f[:], adj_bytes[:].bitcast(U8)).then_inc(adj_set, 1)
            dve.wait_ge(w_loaded, W_LOADED)
            nc.vector.tensor_scalar(w_qkv[:], w_qkv_raw[:], ln1_col[:, 0:1], None, ALU.mult).then_inc(w_qkv_set, 1)
            dve.wait_ge(wvo_ps, 1)
            nc.vector.tensor_copy(w_vo[:], bank_a[0][:, 0:D]).then_inc(wvo_set, 1)
            nc.vector.tensor_copy(token_id[:], tab[:, C_TOKEN:C_BASE]).then_inc(id_next, 1)
            nc.vector.tensor_copy(filled[:], tab[:, C_BASE:C_IOTA]).then_inc(filled_set, 1)
            dve.wait_ge(pad_zero, 1)
            nc.vector.tensor_copy(pad_rows[:, :, COL_ID], tab[:, C_PAD:C_END])
            nc.vector.memset(pad_rows[:, :, COL_EXPERT], -1.0).then_inc(pad_set, 1)
            dve.wait_ge(mask_set, 2)

            def a_statistics(g):
                dve.wait_ge(x_loaded, g * 16 + 16)
                dve.nop(nofuse=True)
                for t in range(G):
                    last = nc.vector.bn_stats(a_st[:, t, :], resid[:, bass.ds(g * G + t, 1), :].rearrange("p a d -> p (a d)"))
                last.then_inc(a_stats, 1)
                dve.wait_ge(a_stats, g + 1)
                dve.nop(nofuse=True)
                for t in range(G):
                    last = nc.vector.bn_aggr(a_mv[:, t, :], a_st[:, t, :])
                last.then_inc(a_aggr, 1)
                dve.wait_ge(a_aggr, g + 1)
                nc.vector.tensor_scalar(a_var[:], a_mv[:, :, 1], EPS_LN, None, ALU.add).then_inc(a_var_set, 1)

            def a_normalise(g):
                dve.wait_ge(a_rstd_set, g + 1)
                if later(g):
                    dve.wait_ge(a_hT_ps, g)
                dve.nop(nofuse=True)
                for t in range(G):
                    last = nc.vector.tensor_scalar(
                        a_h[:, t, :], resid[:, bass.ds(g * G + t, 1), :].rearrange("p a d -> p (a d)"),
                        a_mv[:, t, 0:1], a_rstd[:, t:t + 1], ALU.subtract, ALU.mult)
                last.then_inc(a_norm, 1)

            def a_floor(g):
                dve.wait_ge(sql_ps, g + 1)
                if later(g):
                    dve.wait_ge(guard_set, g)
                nc.vector.tensor_scalar(sq_l[:], bank_a[2][:, 0:G], EPS * EPS, None, ALU.max).then_inc(sql_set, 1)

            def a_adj_l(g):
                dve.wait_ge(gl_ps, g + 1)
                if later(g):
                    dve.wait_ge(outl_ps1, g)
                nc.vector.scalar_tensor_tensor(adj_l[:], tiles(bank_a[1]), 0.0, mask_l[:].unsqueeze(1).broadcast_to([P, G, P]),
                                               ALU.max, ALU.mult).then_inc(adj_l_set, 1)

            def a_values_l(g):
                dve.wait_ge(v_ps, g + 1)
                dve.wait_ge(vg_set, g + 1)
                dve.wait_ge(inv_set, g + 1)
                if later(g):
                    dve.wait_ge(outl_ps1, g)
                nc.vector.tensor_tensor(v_l[:, :, 0:D], tiles(bank_a[0]), inv_norm[:].unsqueeze(2).broadcast_to([P, G, D]),
                                        ALU.mult).then_inc(vl_set, 1)

            def a_arg_g(g):
                dve.wait_ge(gg_ps, g + 1)
                if later(g):
                    dve.wait_ge(adj_g_set, g)
                nc.vector.tensor_tensor(arg_g[:], tiles(bank_a[2]), mask_g[:].unsqueeze(1).broadcast_to([P, G, P]),
                                        ALU.min).then_inc(arg_g_set, 1)

            def halves(bank):
                return bank[:, 0:2 * (D + 1)].rearrange("p (t d) -> p t d", t=2)

            def a_scale_l(g):
                for h in range(2):
                    dve.wait_ge([outl_ps0, outl_ps1][h], g + 1)
                    if h == 0:
                        dve.wait_ge(guard_set, g + 1)
                    last = nc.vector.scalar_tensor_tensor(
                        den_l[:, 2 * h:2 * h + 2], guard[:, 2 * h:2 * h + 2], EPS, halves(bank_a[h])[:, :, D],
                        ALU.mult, ALU.max)
                last.then_inc(denl_set, 1)
                dve.wait_ge(denl_set, g + 1)
                nc.vector.reciprocal(rec_l[:], den_l[:]).then_inc(recl_set, 1)
                dve.wait_ge(recl_set, g + 1)
                if later(g):
                    dve.wait_ge(x1_half, g)
                for h in range(2):
                    nc.vector.scalar_tensor_tensor(
                        out_l[:, 2 * h:2 * h + 2, :], halves(bank_a[h])[:, :, 0:D], 1.0 - T_WAKE,
                        rec_l[:, 2 * h:2 * h + 2].unsqueeze(2).broadcast_to([P, 2, D]),
                        ALU.mult, ALU.mult).then_inc([outl_set0, outl_set1][h], 1)

            def a_scale_g(g):
                for h in range(2):
                    dve.wait_ge([outg_ps0, outg_ps1][h], g + 1)
                    last = nc.vector.tensor_scalar(den_g[:, 2 * h:2 * h + 2], halves(bank_a[2 - 2 * h])[:, :, D], EPS, None,
                                                   ALU.max)
                last.then_inc(deng_set, 1)
                dve.wait_ge(deng_set, g + 1)
                nc.vector.reciprocal(rec_g[:], den_g[:]).then_inc(recg_set, 1)
                dve.wait_ge(recg_set, g + 1)
                if later(g):
                    dve.wait_ge(x1_set, g)
                for h in range(2):
                    nc.vector.scalar_tensor_tensor(
                        out_g[:, 2 * h:2 * h + 2, :], halves(bank_a[2 - 2 * h])[:, :, 0:D], T_WAKE,
                        rec_g[:, 2 * h:2 * h + 2].unsqueeze(2).broadcast_to([P, 2, D]),
                        ALU.mult, ALU.mult).then_inc([outg_set0, outg_set1][h], 1)

            def b_statistics(g):
                dve.wait_ge(x1_set, g + 1)
                dve.nop(nofuse=True)
                for t in range(G):
                    last = nc.vector.bn_stats(b_st[:, t, :], resid[:, bass.ds(g * G + t, 1), :].rearrange("p a d -> p (a d)"))
                last.then_inc(b_stats, 1)
                dve.wait_ge(b_stats, g + 1)
                dve.nop(nofuse=True)
                for t in range(G):
                    last = nc.vector.bn_aggr(b_mv[:, t, :], b_st[:, t, :])
                last.then_inc(b_aggr, 1)
                dve.wait_ge(b_aggr, g + 1)
                nc.vector.tensor_scalar(b_var[:, 0, :], b_mv[:, :, 1], EPS_LN, None, ALU.add)
                nc.vector.tensor_scalar(b_var[:, 1, :], b_mv[:, :, 1], 1.0 + EPS_RMS, EPS_RMS * EPS_LN,
                                        ALU.mult, ALU.add).then_inc(b_var_set, 1)

            def b_normalise(g):
                dve.wait_ge(b_rs_set, g + 1)
                if later(g):
                    dve.wait_ge(b_ratio_set, g)
                nc.vector.reciprocal(b_rec[:], b_rs[:, 1, :]).then_inc(b_rec_set, 1)
                if later(g):
                    dve.wait_ge(b_hT_ps, g)
                    dve.wait_ge(h2_set, g)
                dve.nop(nofuse=True)
                for t in range(G):
                    last = nc.vector.tensor_scalar(
                        b_h[:, t, :], resid[:, bass.ds(g * G + t, 1), :].rearrange("p a d -> p (a d)"),
                        b_mv[:, t, 0:1], b_rs[:, 1, t:t + 1], ALU.subtract, ALU.mult)
                last.then_inc(b_norm, 1)

            def b_rope_cos(g, half):
                dve.wait_ge([qkv_ps0, qkv_ps1][half], g + 1)
                dve.wait_ge([swap_set0, swap_set1][half], g + 1)
                qk = tiles(bank_b[1 + half], 2)[:, :, 0:QK]
                cos = tab[:, C_COS:C_SIN].unsqueeze(1).broadcast_to([P, 2, QK])
                last = nc.vector.tensor_tensor(rope_c[:, 2 * half:2 * half + 2, :], qk, cos, ALU.mult)
                last.then_inc(rope_c_set, 1)

            def b_rope_add(g):
                dve.wait_ge(rope_c_set, g * 2 + 2)
                dve.wait_ge(rope_s_set, g * 2 + 2)
                if later(g):
                    dve.wait_ge(kT_ps, g)
                nc.vector.tensor_tensor(roped[:], rope_c[:], rope_s[:], ALU.add).then_inc(roped_set, 1)

            def b_softmax_shift(g, h):
                bank = tiles(bank_b[(2 + h) % 3])
                dve.wait_ge(s_ps, g * NH + h + 1)
                nc.vector.tensor_reduce(row_max[:, h, :], bank, AX_X, ALU.max).then_inc(max_set, 1)
                dve.wait_ge(max_set, g * NH + h + 1)
                if h >= 2:
                    dve.wait_ge(prob_set, g * NH + h - 1)
                elif later(g):
                    dve.wait_ge(prob_set, g * NH + h - 1)
                nc.vector.tensor_tensor(shifted[:, h % 2, :, :], bank, row_max[:, h, :].unsqueeze(2).broadcast_to([P, G, P]),
                                        ALU.subtract).then_inc(shift_set, 1)

            def c_normalise_y(g, half):
                yp = bank_c[half][:, 0:2 * NH * (HD + 1)].rearrange("p (a d) -> p a d", d=HD + 1)
                dve.wait_ge([y_ps0, y_ps1][half], g + 1)
                n = 2 * NH
                nc.vector.reciprocal(y_rec[:, half * n:half * n + n], yp[:, :, HD]).then_inc([y_rec0, y_rec1][half], 1)
                dve.wait_ge([y_rec0, y_rec1][half], g + 1)
                if later(g):
                    dve.wait_ge(yT_ps, g)
                nc.vector.tensor_tensor(
                    y[:, 2 * half:2 * half + 2, :].rearrange("p t (h d) -> p (t h) d", h=NH), yp[:, :, 0:HD],
                    y_rec[:, half * n:half * n + n].unsqueeze(2).broadcast_to([P, n, HD]),
                    ALU.mult).then_inc([y_set0, y_set1][half], 1)

            def c_block_input(g):
                dve.wait_ge(attn_ps, g + 1)
                dve.wait_ge(h2_set, g + 1)
                if later(g):
                    dve.wait_ge(resid_set, g)
                    dve.wait_ge(sq_set, g)
                nc.vector.tensor_tensor(xf[:], tiles(bank_c[1]), h2[:], ALU.add).then_inc(xf_set, 1)

            def c_mean_square(g):
                dve.wait_ge(sq_set, g + 1)
                if later(g):
                    dve.wait_ge(rms_set, g)
                nc.vector.tensor_scalar(ms[:], sum_sq[:], 1.0 / D, EPS_RMS, ALU.mult, ALU.add).then_inc(ms_set, 1)

            def c_flat(g):
                dve.wait_ge(rms_set, g + 1)
                if later(g):
                    dve.wait_ge(scattered, g * (G * 2 * 16))
                    dve.wait_ge(flat_ps, g)
                dve.nop(nofuse=True)
                for t in range(G):
                    last = nc.vector.scalar_tensor_tensor(flat_rows[:, t, 0:D], xf[:, t, :], rms[:, t:t + 1], ln2_row[:],
                                                          ALU.mult, ALU.mult)
                last.then_inc(flat_set, 1)
                dve.wait_ge(id_next, g + 1)
                nc.vector.tensor_copy(flat_rows[:, :, COL_ID], token_id[:]).then_inc(id_set, 1)
                dve.wait_ge(id_set, g + 1)
                nc.vector.tensor_scalar(token_id[:], token_id[:], float(G), None, ALU.add).then_inc(id_next, 1)

            def c_choose(g):
                logits = bank_c[1][:, 0:G * NE].rearrange("p (t e) -> p t e", t=G)
                dve.wait_ge(router_ps, g + 1)
                dve.nop(nofuse=True)
                for t in range(G):
                    last = nc.vector.max(best[:, t, :], logits[:, t, :])
                last.then_inc(best_set, 1)
                dve.wait_ge(best_set, g + 1)
                dve.nop(nofuse=True)
                for t in range(G):
                    last = nc.vector.max_index(best_at[:, t, :], best[:, t, :], logits[:, t, :])
                last.then_inc(best_at_set, 1)
                dve.wait_ge(best_at_set, g + 1)
                nc.vector.tensor_copy(choice[:].rearrange("p (t n) -> p t n", n=2), best_at[:, :, 0:2]).then_inc(choice_set, 1)
                dve.wait_ge(choice_set, g + 1)
                nc.vector.tensor_tensor(
                    pick[:].rearrange("p t n e -> p (t n) e"), tab[:, C_IOTA:C_UPTO].unsqueeze(1).broadcast_to([P, 2 * G, NE]),
                    choice[:].unsqueeze(2).broadcast_to([P, 2 * G, NE]), ALU.is_equal).then_inc(pick_set, 1)
                nc.vector.tensor_copy(flat_rows[:, :, COL_EXPERT], choice[:].rearrange("p (t n) -> p t n", n=2)[:, :, 0]).then_inc(
                    expert_set, 1)
                dve.wait_ge(pick_set, g + 1)
                if later(g):
                    dve.wait_ge(rank_ps, g)
                nc.vector.tensor_tensor(chosen_b[:], pick[:, :, 0, :], pick[:, :, 1, :], ALU.add).then_inc(chosen_set, 1)
                if later(g):
                    dve.wait_ge(weight_set, g)
                nc.vector.tensor_tensor(below[:], best[:], best[:, :, 0:1].broadcast_to([P, G, NE]), ALU.subtract).then_inc(
                    below_set, 1)

            def c_gates(g):
                dve.wait_ge(weight_set, g + 1)
                nc.vector.tensor_reduce(total[:], weight[:], AX_X, ALU.add).then_inc(total_set, 1)
                nc.vector.tensor_tensor(pair[:], weight[:, :, 0], weight[:, :, 1], ALU.add).then_inc(pair_set, 1)
                dve.wait_ge(total_set, g + 1)
                dve.wait_ge(pair_set, g + 1)
                nc.vector.scalar_tensor_tensor(denom[:], total[:], 1e-9, pair[:], ALU.mult, ALU.add).then_inc(denom_set, 1)
                dve.wait_ge(denom_set, g + 1)
                nc.vector.reciprocal(denom_rec[:], denom[:]).then_inc(denom_rec_set, 1)
                dve.wait_ge(denom_rec_set, g + 1)
                nc.vector.tensor_tensor(flat_rows[:, :, COL_GATE:COL_GATE + 2], weight[:, :, 0:2],
                                        denom_rec[:].unsqueeze(2).broadcast_to([P, G, 2]), ALU.mult).then_inc(gates_set, 1)

            def c_places(g):
                dve.wait_ge(rank_ps, g + 1)
                dve.wait_ge(filled_set, g + 1)
                nc.vector.tensor_tensor(place[:], bank_c[0][:, 0:(G + 1) * NE].rearrange("p (t e) -> p t e", e=NE),
                                        filled[:].unsqueeze(1).broadcast_to([P, G + 1, NE]), ALU.add).then_inc(place_set, 1)
                dve.wait_ge(place_set, g + 1)
                nc.vector.tensor_copy(filled[:], place[:, G, :]).then_inc(filled_set, 1)
                nc.vector.tensor_tensor(picked[:], pick[:], place[:, 0:G, :].unsqueeze(2).broadcast_to([P, G, 2, NE]),
                                        ALU.mult).then_inc(picked_set, 1)
                dve.wait_ge(picked_set, g + 1)
                nc.vector.tensor_reduce(place_f[:], picked[:].rearrange("p t n e -> p (t n) e"), AX_X, ALU.add).then_inc(
                    place_f_set, 1)
                dve.wait_ge(place_f_set, g + 1)
                nc.vector.tensor_copy(place_i[:], place_f[:]).then_inc(place_i_set, 1)

            def step(a, b, c):
                if b is not None:
                    b_statistics(b)
                if a is not None:
                    a_statistics(a)
                if b is not None:
                    b_normalise(b)
                if a is not None:
                    a_normalise(a)
                if c is not None:
                    c_normalise_y(c, 0)
                    c_normalise_y(c, 1)
                if b is not None:
                    b_rope_cos(b, 0)
                    b_rope_cos(b, 1)
                if c is not None:
                    c_block_input(c)
                if a is not None:
                    a_floor(a)
                    a_adj_l(a)
                if b is not None:
                    b_rope_add(b)
                if a is not None:
                    a_values_l(a)
                if c is not None:
                    c_mean_square(c)
                if b is not None:
                    b_softmax_shift(b, 0)
                if a is not None:
                    a_arg_g(a)
                if b is not None:
                    b_softmax_shift(b, 1)
                if a is not None:
                    a_scale_l(a)
                if b is not None:
                    b_softmax_shift(b, 2)
                    b_softmax_shift(b, 3)
                if a is not None:
                    a_scale_g(a)
                if c is not None:
                    c_flat(c)
                    c_choose(c)
                    c_gates(c)
                    c_places(c)

            step(0, None, None)
            step(1, 0, None)
            step(2, 1, 0)
            with dve.Fori(1, NG - 2) as k:
                step(k + 2, k + 1, k)
            step(None, NG - 1, NG - 2)
            step(None, None, NG - 1)

            dve.wait_ge(filled_set, NG + 1)
            nc.vector.tensor_tensor(counts[:], filled[:], tab[:, C_BASE:C_IOTA], ALU.subtract).then_inc(table_step, 1)
            nc.vector.tensor_copy(region_end_i[:], filled[:])
            dve.wait_ge(table_step, 1)
            n_steps = N_TOK // ROWS
            nc.vector.tensor_tensor(over[:], counts[:].unsqueeze(2).broadcast_to([P, NE, n_steps]),
                                    tab[:, C_STEP:C_TILE].unsqueeze(1).broadcast_to([P, NE, n_steps]), ALU.is_gt).then_inc(
                table_step, 1)
            dve.wait_ge(table_step, 2)
            nc.vector.tensor_reduce(n_tiles[:], over[:], AX_X, ALU.add).then_inc(table_step, 1)
            dve.wait_ge(table_step, 3)
            nc.vector.tensor_tensor(upto[:], tab[:, C_UPTO:C_STEP].rearrange("p (e j) -> p e j", e=NE),
                                    n_tiles[:].unsqueeze(1).broadcast_to([P, NE, NE]), ALU.mult).then_inc(table_step, 1)
            dve.wait_ge(table_step, 4)
            nc.vector.tensor_reduce(tiles_upto[:], upto[:], AX_X, ALU.add).then_inc(table_step, 1)
            dve.wait_ge(table_step, 5)
            numbers = tab[:, C_TILE:C_PAD]
            nc.vector.tensor_tensor(passed[:], numbers.unsqueeze(2).broadcast_to([P, N_TILES, NE]),
                                    tiles_upto[:].unsqueeze(1).broadcast_to([P, N_TILES, NE]), ALU.is_ge).then_inc(table_step, 1)
            dve.wait_ge(table_step, 6)
            nc.vector.tensor_reduce(tile_expert[:], passed[:], AX_X, ALU.add).then_inc(table_step, 1)
            nc.vector.tensor_tensor(passed_n[:], passed[:], n_tiles[:].unsqueeze(1).broadcast_to([P, N_TILES, NE]),
                                    ALU.mult).then_inc(table_step, 1)
            dve.wait_ge(table_step, 8)
            nc.vector.tensor_reduce(tile_first[:], passed_n[:], AX_X, ALU.add).then_inc(table_step, 1)
            dve.wait_ge(table_step, 9)
            nc.vector.tensor_tensor(tile_at[:], numbers, tile_first[:], ALU.subtract).then_inc(table_step, 1)
            dve.wait_ge(table_step, 10)
            nc.vector.tensor_scalar(tile_first[:], tile_expert[:], float(REGION), None, ALU.mult).then_inc(table_step, 1)
            dve.wait_ge(table_step, 11)
            nc.vector.scalar_tensor_tensor(tile_row[:], tile_at[:], float(ROWS), tile_first[:], ALU.mult, ALU.add).then_inc(
                table_step, 1)
            dve.wait_ge(table_step, 12)
            nc.vector.tensor_scalar(tile_weights_i[:], tile_expert[:], float(NE - 1), None, ALU.min)
            nc.vector.tensor_scalar(tile_row_i[:], tile_row[:], float(NE * REGION), None, ALU.min).then_inc(table_set, 1)

            def gates_and_places(pair_no, u):
                j = pair_no * 2 + u
                rows = in_rows[:, u, :, :]
                dve.wait_ge([rows_loaded0, rows_loaded1][u], pair_no * 16 + 16)
                dve.nop(nofuse=True)
                nc.vector.tensor_scalar(second[:, u, :], rows[:, :, COL_EXPERT], tile_expert[:, bass.ds(j, 1)], None,
                                        ALU.not_equal).then_inc(second_set, 1)
                nc.vector.tensor_tensor(gate_diff[:, u, :], rows[:, :, COL_GATE + 1], rows[:, :, COL_GATE],
                                        ALU.subtract).then_inc(gdiff_set, 1)
                dve.wait_ge(second_set, j + 1)
                if later(pair_no):
                    dve.wait_ge(dest_set, j - 1)
                nc.vector.scalar_tensor_tensor(dest_f[:, u, :], second[:, u, :], float(N_TOK), rows[:, :, COL_ID],
                                               ALU.mult, ALU.add).then_inc(destf_set, 1)
                dve.wait_ge(gdiff_set, j + 1)
                nc.vector.tensor_tensor(gate_step[:, u, :], second[:, u, :], gate_diff[:, u, :], ALU.mult).then_inc(gstep_set, 1)
                dve.wait_ge(gstep_set, j + 1)
                nc.vector.tensor_tensor(gate[:, u, :], gate_step[:, u, :], rows[:, :, COL_GATE], ALU.add).then_inc(gate_set, 1)
                dve.wait_ge(destf_set, j + 1)
                if later(pair_no):
                    dve.wait_ge([placed0, placed1][u], pair_no * (SUB * 16))
                nc.vector.tensor_copy(dest_i[:, u, :], dest_f[:, u, :]).then_inc(dest_set, 1)

            def hidden_chunk(pair_no, u, c):
                j = pair_no * 2 + u
                n = CHUNKS[c][1]
                dve.wait_ge(gate_ps, j * NC + c + 1)
                dve.wait_ge(silu_set, j * NC + c + 1)
                if later(pair_no):
                    dve.wait_ge(down_ps, j - 1)
                nc.vector.tensor_tensor(hidden[0:n, u, c, :], bank_gate[(u * NC + c) % 2][0:n, :], silu[0:n, (u * NC + c) % 2, :],
                                        ALU.mult).then_inc(hidden_set, 1)

            def scale_rows(pair_no, u):
                j = pair_no * 2 + u
                dve.wait_ge(down_ps, j + 1)
                dve.wait_ge(gate_set, j + 1)
                if later(pair_no):
                    dve.wait_ge([placed0, placed1][u], pair_no * (SUB * 16))
                nc.vector.tensor_tensor(out_rows[:, u, :, :], tiles(bank_down[u]), gate[:, u, :].unsqueeze(2).broadcast_to([P, SUB, D]),
                                        ALU.mult).then_inc(outrows_set, 1)

            def expert_pair(pair_no):
                for u in range(2):
                    gates_and_places(pair_no, u)
                    for c in range(NC):
                        hidden_chunk(pair_no, u, c)
                    scale_rows(pair_no, u)

            expert_pair(0)
            with dve.Fori(1, N_TILES // 2) as k:
                expert_pair(k)

            for i in range(NB // FINAL):
                r = resid[:, i * FINAL:(i + 1) * FINAL, :]
                dve.wait_ge([final_loaded0, final_loaded1][i % 2], (i // 2 + 1) * 32)
                if i == 0:
                    dve.wait_ge(resid_set, NG)
                nc.vector.tensor_tensor(r, r, final_in[:, i % 2, 0, :, :], ALU.add).then_inc(sum_half, 1)
                dve.wait_ge(sum_half, i + 1)
                nc.vector.tensor_tensor(r, r, final_in[:, i % 2, 1, :, :], ALU.add).then_inc(sum_set, 1)

        @block.scalar
        def _(act):
            act.wait_ge(ones_set, 1)

            def copy_bank(dst, bank):
                return nc.scalar.activation(dst, bank, ACT.Copy)

            def a_copy_hT(g):
                act.wait_ge(a_hT_ps, g + 1)
                if later(g):
                    act.wait_ge(v_ps, g)
                copy_bank(a_hT[:], tiles(bank_a[0])).then_inc(a_hT_set, 1)

            def a_copy_z(g):
                act.wait_ge(zl_ps, g + 1)
                if later(g):
                    act.wait_ge(gl_ps, g)
                    act.wait_ge(zl_sq, g)
                copy_bank(zl[:], tiles(bank_a[1])).then_inc(zl_set, 1)
                act.wait_ge(zg_ps, g + 1)
                if later(g):
                    act.wait_ge(gg_ps, g)
                    act.wait_ge(zg_sq, g)
                copy_bank(zg[:], tiles(bank_a[2])).then_inc(zg_set, 1)

            def a_copy_values(g):
                act.wait_ge(v_ps, g + 1)
                if later(g):
                    act.wait_ge(outg_ps1, g)
                copy_bank(v_g[:, :, 0:D], tiles(bank_a[0])).then_inc(vg_set, 1)

            def a_exp(g):
                act.wait_ge(arg_g_set, g + 1)
                if later(g):
                    act.wait_ge(outg_ps1, g)
                nc.scalar.activation(adj_g[:], arg_g[:], ACT.Exp).then_inc(adj_g_set, 1)

            def b_copy_hT(g):
                act.wait_ge(b_hT_ps, g + 1)
                if later(g):
                    act.wait_ge(qkv_ps1, g)
                copy_bank(b_hT[:], tiles(bank_b[0])).then_inc(b_hT_set, 1)

            def b_copy_qkv(g, half):
                qkv = tiles(bank_b[1 + half], 2)
                t = slice(2 * half, 2 * half + 2)
                act.wait_ge([qkv_ps0, qkv_ps1][half], g + 1)
                if later(g):
                    act.wait_ge(rope_s_set, g * 2)
                    act.wait_ge(y_ps1, g)
                src = qkv[:, :, 0:QK].rearrange("p t (h two e) -> p t h two e", two=2, e=HD // 2)
                dst = swapped[:, t, :].rearrange("p t (h two e) -> p t h two e", two=2, e=HD // 2)
                for part in range(2):
                    copy_bank(dst[:, :, :, part, :], src[:, :, :, 1 - part, :])
                copy_bank(v1[:, t, :, 0:HD], qkv[:, :, QK:QKV].rearrange("p t (k d) -> p t k d", k=NKV)).then_inc(
                    [swap_set0, swap_set1][half], 1)

            def b_copy_qk(g):
                act.wait_ge(qT_ps, g + 1)
                if later(g):
                    act.wait_ge(s_ps, g * NH)
                copy_bank(qT[:], tiles(bank_b[0])).then_inc(qT_set, 1)
                act.wait_ge(kT_ps, g + 1)
                for r in range(NREP):
                    last = copy_bank(kT[r * NKV * HD:(r + 1) * NKV * HD, :, :], tiles(bank_b[1])[0:NKV * HD, :, :])
                last.then_inc(kT_set, 1)

            def b_exp(g, h):
                act.wait_ge(shift_set, g * NH + h + 1)
                if later(g):
                    act.wait_ge(pT_ps, g * NH - NH + h + 1)
                nc.scalar.activation(probs[:, h, :, :], shifted[:, h % 2, :, :], ACT.Exp, scale=SCALE).then_inc(prob_set, 1)

            def c_copy_probs(g, h):
                act.wait_ge(pT_ps, g * NH + h + 1)
                if later(g):
                    act.wait_ge(y_ps1, g)
                copy_bank(probs_t[:, h, :, :], tiles(bank_c[h % 2])).then_inc(pT_set, 1)

            def c_copy_yT(g):
                act.wait_ge(yT_ps, g + 1)
                if later(g):
                    act.wait_ge(attn_ps, g)
                copy_bank(yT[:], tiles(bank_c[0])).then_inc(yT_set, 1)

            def c_square(g):
                act.wait_ge(xf_set, g + 1)
                if later(g):
                    act.wait_ge(ms_set, g)
                for t in range(G):
                    last = nc.scalar.activation(sq_junk[:, t, :], xf[:, t, :], ACT.Square, accum_out=sum_sq[:, t:t + 1])
                last.then_inc(sq_set, 1)

            def c_copy_flatT(g):
                act.wait_ge(flat_ps, g + 1)
                if later(g):
                    act.wait_ge(router_ps, g)
                copy_bank(flatT[:], tiles(bank_c[0])).then_inc(flatT_set, 1)

            def c_weights(g):
                act.wait_ge(below_set, g + 1)
                if later(g):
                    act.wait_ge(gates_set, g)
                nc.scalar.activation(weight[:], below[:], ACT.Exp).then_inc(weight_set, 1)

            def step(a, b, c):
                if c is not None:
                    for h in range(NH):
                        c_copy_probs(c, h)
                if b is not None:
                    b_copy_hT(b)
                if a is not None:
                    a_copy_hT(a)
                if b is not None:
                    b_copy_qkv(b, 0)
                    b_copy_qkv(b, 1)
                if c is not None:
                    c_copy_yT(c)
                if a is not None:
                    a_copy_z(a)
                    a_copy_values(a)
                if c is not None:
                    c_square(c)
                if b is not None:
                    b_copy_qk(b)
                    b_exp(b, 0)
                if a is not None:
                    a_exp(a)
                if b is not None:
                    b_exp(b, 1)
                    b_exp(b, 2)
                    b_exp(b, 3)
                if c is not None:
                    c_copy_flatT(c)
                    c_weights(c)

            step(0, None, None)
            step(1, 0, None)
            step(2, 1, 0)
            with act.Fori(1, NG - 2) as k:
                step(k + 2, k + 1, k)
            step(None, NG - 1, NG - 2)
            step(None, None, NG - 1)

            def expert_pair(pair_no):
                for u in range(2):
                    j = pair_no * 2 + u
                    act.wait_ge(inT_ps, j + 1)
                    if later(pair_no):
                        act.wait_ge(gate_ps, j * NC - NC)
                    copy_bank(in_t[:, u, :], bank_in[:]).then_inc(inT_set, 1)
                    for c, (_, n) in enumerate(CHUNKS):
                        m = u * NC + c
                        act.wait_ge(up_ps, j * NC + c + 1)
                        if later(pair_no) or m >= 2:
                            act.wait_ge(hidden_set, j * NC + c - 1)
                        nc.scalar.activation(silu[0:n, m % 2, :], bank_up[m % 2][0:n, :], ACT.Silu).then_inc(silu_set, 1)

            expert_pair(0)
            with act.Fori(1, N_TILES // 2) as k:
                expert_pair(k)

            for i in range(NB // FINAL):
                act.wait_ge(sum_set, i + 1)
                act.dma_start(out[:, i * FINAL:(i + 1) * FINAL, :], resid[:, i * FINAL:(i + 1) * FINAL, :]).then_inc(
                    out_stored, 16)
            act.wait_ge(out_stored, NB // FINAL * 16)

        @block.tensor
        def _(pe):
            pe.wait_ge(w_loaded, W_LOADED)
            nc.tensor.matmul(bank_a[0][:, 0:D], w_v_t[:], w_o_gnn[:], start=True, stop=True).then_inc(wvo_ps, 1)
            pe.wait_ge(const_loaded, 16)
            pe.wait_ge(consts_set, 1)
            pe.wait_ge(ones_set, 1)
            pe.wait_ge(w_qkv_set, 1)
            pe.wait_ge(wvo_set, 1)

            def transposes(bank, srcs):
                for t, src in enumerate(srcs):
                    last = nc.tensor.transpose(bank[:, t * P:(t + 1) * P], src, ident)
                return last

            def a_transpose(g):
                pe.wait_ge(a_norm, g + 1)
                if later(g):
                    pe.wait_ge(outg_set1, g)
                transposes(bank_a[0], [a_h[:, t, :] for t in range(G)]).then_inc(a_hT_ps, 1)

            def a_project(g):
                pe.wait_ge(a_hT_set, g + 1)
                if later(g):
                    pe.wait_ge(outl_set1, g)
                hT = a_hT[:].rearrange("p t d -> p (t d)")
                nc.tensor.matmul(bank_a[1][:], w_l[:], hT, start=True, stop=True).then_inc(zl_ps, 1)
                if later(g):
                    pe.wait_ge(outg_set0, g)
                nc.tensor.matmul(bank_a[2][:], w_g[:], hT, start=True, stop=True).then_inc(zg_ps, 1)
                for t in range(G):
                    last = nc.tensor.matmul(bank_a[0][:, t * P:(t + 1) * P], a_hT[:, t, :], w_vo[:], start=True, stop=True)
                last.then_inc(v_ps, 1)

            def a_gram_l(g):
                pe.wait_ge(zl_set, g + 1)
                for t in range(G):
                    last = nc.tensor.matmul(bank_a[1][:, t * P:(t + 1) * P], zl[:, t, :], zl[:, t, :], start=True, stop=True)
                last.then_inc(gl_ps, 1)

            def a_norms(g):
                pe.wait_ge(zl_sq, g + 1)
                pe.wait_ge(zg_set, g + 1)
                for t in range(G):
                    last = nc.tensor.matmul(bank_a[2][:, t:t + 1], zl2[:, t, :], v_g[:, 0, D:D + 1], start=True, stop=True)
                last.then_inc(sql_ps, 1)

            def a_gram_g(g):
                pe.wait_ge(zg_sq, g + 1)
                pe.wait_ge(sql_set, g + 1)
                for t in range(G):
                    o = bank_a[2][:, t * P:(t + 1) * P]
                    nc.tensor.matmul(o, zg[:, t, :], zg[:, t, :], start=True, stop=False)
                    nc.tensor.matmul(o, minus_half[:], zg2[:, t, :], start=False, stop=False)
                    last = nc.tensor.matmul(o, zg2[:, t, :], minus_half[:], start=False, stop=True)
                last.then_inc(gg_ps, 1)

            def a_apply(g, kernel, values, banks, ready):
                for h in range(2):
                    for t in range(2):
                        last = nc.tensor.matmul(banks[h][:, t * (D + 1):(t + 1) * (D + 1)], kernel[:, 2 * h + t, :],
                                                values[:, 2 * h + t, :], start=True, stop=True)
                    last.then_inc(ready[h], 1)

            def a_apply_l(g):
                pe.wait_ge(adj_l_set, g + 1)
                pe.wait_ge(vl_set, g + 1)
                pe.wait_ge(vl_col_set, g + 1)
                a_apply(g, adj_l, v_l, [bank_a[0], bank_a[1]], [outl_ps0, outl_ps1])

            def a_apply_g(g, h):
                if h == 0:
                    pe.wait_ge(adj_g_set, g + 1)
                    pe.wait_ge(arg_g_set, g + 1)
                else:
                    pe.wait_ge(outl_set0, g + 1)
                for t in range(2):
                    last = nc.tensor.matmul(bank_a[2 - 2 * h][:, t * (D + 1):(t + 1) * (D + 1)], adj_g[:, 2 * h + t, :],
                                            v_g[:, 2 * h + t, :], start=True, stop=True)
                last.then_inc([outg_ps0, outg_ps1][h], 1)

            def b_transpose(g):
                pe.wait_ge(b_norm, g + 1)
                if later(g):
                    pe.wait_ge(shift_set, g * NH - 2)
                transposes(bank_b[0], [b_h[:, t, :] for t in range(G)]).then_inc(b_hT_ps, 1)

            def b_project(g):
                pe.wait_ge(b_hT_set, g + 1)
                for half in range(2):
                    if later(g):
                        pe.wait_ge(shift_set, g * NH - 1 + half)
                    for t in range(2):
                        last = nc.tensor.matmul(bank_b[1 + half][:, t * QKV:(t + 1) * QKV], b_hT[:, 2 * half + t, :], w_qkv[:],
                                                start=True, stop=True)
                    last.then_inc([qkv_ps0, qkv_ps1][half], 1)

            def b_transpose_qk(g):
                pe.wait_ge(roped_set, g + 1)
                pe.wait_ge(b_hT_set, g + 1)
                transposes(bank_b[0], [roped[:, t, 0:NH * HD] for t in range(G)]).then_inc(qT_ps, 1)
                for t in range(G):
                    last = nc.tensor.transpose(bank_b[1][0:NKV * HD, t * P:(t + 1) * P], roped[:, t, NH * HD:QK], ident)
                last.then_inc(kT_ps, 1)

            def b_scores(g, h):
                bank = bank_b[(2 + h) % 3]
                if h == 0:
                    pe.wait_ge(qT_set, g + 1)
                    pe.wait_ge(kT_set, g + 1)
                if h == 3:
                    pe.wait_ge(shift_set, g * NH + 1)
                nc.tensor.matmul(bank[:], ident_b[:], causal_b[:].unsqueeze(1).broadcast_to([P, G, P]), start=True, stop=False,
                                 skip_group_check=True)
                heads = slice(h * HD, (h + 1) * HD)
                for t in range(G):
                    last = nc.tensor.matmul(bank[:, t * P:(t + 1) * P], qT[heads, t, :], kT[heads, t, :], start=False, stop=True,
                                            skip_group_check=True)
                last.then_inc(s_ps, 1)

            def c_transpose_probs(g, h):
                pe.wait_ge(prob_set, g * NH + h + 1)
                if h >= 2:
                    pe.wait_ge(pT_set, g * NH + h - 1)
                elif later(g):
                    pe.wait_ge([place_set, best_at_set][h], g)
                transposes(bank_c[h % 2], [probs[:, h, t, :] for t in range(G)]).then_inc(pT_ps, 1)

            def c_values(g, half):
                if half == 0:
                    pe.wait_ge(pT_set, g * NH + NH)
                for i in range(2 * NH):
                    t, h = 2 * half + i // NH, i % NH
                    last = nc.tensor.matmul(bank_c[half][:, i * (HD + 1):(i + 1) * (HD + 1)], probs_t[:, h, t, :],
                                            v1[:, t, h % NKV, :], start=True, stop=True)
                last.then_inc([y_ps0, y_ps1][half], 1)

            def c_transpose_y(g):
                pe.wait_ge(y_set1, g + 1)
                transposes(bank_c[0], [y[:, t, :] for t in range(G)]).then_inc(yT_ps, 1)

            def c_output(g):
                pe.wait_ge(yT_set, g + 1)
                for t in range(G):
                    last = nc.tensor.matmul(bank_c[1][:, t * P:(t + 1) * P], yT[:, t, :], w_o[:], start=True, stop=True)
                last.then_inc(attn_ps, 1)

            def c_transpose_flat(g):
                pe.wait_ge(flat_set, g + 1)
                pe.wait_ge(yT_set, g + 1)
                transposes(bank_c[0], [flat_rows[:, t, 0:D] for t in range(G)]).then_inc(flat_ps, 1)

            def c_router(g):
                pe.wait_ge(flatT_set, g + 1)
                pe.wait_ge(xf_set, g + 1)
                for t in range(G):
                    last = nc.tensor.matmul(bank_c[1][:, t * NE:(t + 1) * NE], flatT[:, t, :], w_router[:], start=True, stop=True)
                last.then_inc(router_ps, 1)

            def c_rank(g):
                pe.wait_ge(chosen_set, g + 1)
                o = bank_c[0]
                last = nc.tensor.matmul(o[:, 0:G * NE], upper_b[:], chosen_b[:].rearrange("p t e -> p (t e)"), start=True,
                                        stop=False, skip_group_check=True)
                for t in range(G):
                    n = G - t
                    last = nc.tensor.matmul(o[:, (t + 1) * NE:(G + 1) * NE], ones_b[:],
                                            chosen_b[:, t:t + 1, :].broadcast_to([P, n, NE]), start=False, stop=t == G - 1,
                                            skip_group_check=True)
                last.then_inc(rank_ps, 1)

            def step(a, b, c):
                if c is not None:
                    for h in range(NH):
                        c_transpose_probs(c, h)
                if b is not None:
                    b_transpose(b)
                if a is not None:
                    a_transpose(a)
                if c is not None:
                    c_values(c, 0)
                    c_values(c, 1)
                if b is not None:
                    b_project(b)
                if a is not None:
                    a_project(a)
                if c is not None:
                    c_transpose_y(c)
                    c_output(c)
                if a is not None:
                    a_gram_l(a)
                    a_norms(a)
                if b is not None:
                    b_transpose_qk(b)
                if a is not None:
                    a_gram_g(a)
                if b is not None:
                    b_scores(b, 0)
                    b_scores(b, 1)
                if a is not None:
                    a_apply_l(a)
                if b is not None:
                    b_scores(b, 2)
                    b_scores(b, 3)
                if a is not None:
                    a_apply_g(a, 0)
                    a_apply_g(a, 1)
                if c is not None:
                    c_transpose_flat(c)
                    c_router(c)
                    c_rank(c)

            step(0, None, None)
            step(1, 0, None)
            step(2, 1, 0)
            with pe.Fori(1, NG - 2) as k:
                step(k + 2, k + 1, k)
            step(None, NG - 1, NG - 2)
            step(None, None, NG - 1)

            def turn_rows(pair_no, u):
                pe.wait_ge([rows_loaded0, rows_loaded1][u], pair_no * 16 + 16)
                if u or later(pair_no):
                    pe.wait_ge(inT_set, pair_no * 2 + u)
                for i in range(SUB):
                    last = nc.tensor.transpose(bank_in[:, i * P:(i + 1) * P], in_rows[:, u, i, 0:D], ident)
                last.then_inc(inT_ps, 1)

            def up_and_gate(pair_no, u):
                j = pair_no * 2 + u
                pe.wait_ge(inT_set, j + 1)
                pe.wait_ge([wbuf_loaded0, wbuf_loaded1][u], pair_no * 16 + 16)
                for c, (c0, n) in enumerate(CHUNKS):
                    m = u * NC + c
                    full = later(pair_no) or m >= 2
                    if full:
                        pe.wait_ge(silu_set, j * NC + c - 1)
                    nc.tensor.matmul(bank_up[m % 2][0:n, :], w_buf[:, u, c0:c0 + n], in_t[:, u, :], start=True,
                                     stop=True).then_inc(up_ps, 1)
                    if full:
                        pe.wait_ge(hidden_set, j * NC + c - 1)
                    nc.tensor.matmul(bank_gate[m % 2][0:n, :], w_buf[:, u, HID + c0:HID + c0 + n], in_t[:, u, :], start=True,
                                     stop=True).then_inc(gate_ps, 1)

            def down(pair_no, u):
                j = pair_no * 2 + u
                pe.wait_ge(hidden_set, j * NC + NC)
                if later(pair_no):
                    pe.wait_ge(outrows_set, j - 1)
                for i in range(SUB):
                    for c, (_, n) in enumerate(CHUNKS):
                        last = nc.tensor.matmul(bank_down[u][:, i * P:(i + 1) * P], hidden[0:n, u, c, i * P:(i + 1) * P],
                                                w_buf[0:n, u, 2 * HID + c * D:2 * HID + (c + 1) * D], start=c == 0, stop=c == NC - 1)
                last.then_inc(down_ps, 1)

            def expert_pair(pair_no, last_pair=False):
                up_and_gate(pair_no, 0)
                turn_rows(pair_no, 1)
                down(pair_no, 0)
                up_and_gate(pair_no, 1)
                if not last_pair:
                    turn_rows(pair_no + 1, 0)
                down(pair_no, 1)

            turn_rows(0, 0)
            expert_pair(0)
            with pe.Fori(1, N_TILES // 2 - 1) as k:
                expert_pair(k)
            expert_pair(N_TILES // 2 - 1, last_pair=True)


def kernel(**inputs):
    import numpy as _np
    import concourse.bacc as _bacc
    from concourse import mybir as _mybir
    from concourse.bass_utils import run_bass_kernel_spmd as _run

    nc = _bacc.Bacc("TRN2", target_bir_lowering=False, num_devices=1)
    f = {k: _np.asarray(v) for k, v in inputs.items()}
    wq = f["L0_ffn_wq"].reshape(NH, HD, D)[HEADS].reshape(NH * HD, D)
    wo = f["L0_ffn_wo"].reshape(D, NH, HD)[:, HEADS].reshape(D, NH * HD)
    laid = {
        "x": f["x"].transpose(1, 0, 2),
        "adj_t": _np.ascontiguousarray(f["adj"].T).view(_np.int32),
        "wl": f["L0_gnn_Wl"],
        "wg": f["L0_gnn_Wg"],
        "wv_t": f["L0_gnn_Wv"].T,
        "wo_gnn": f["L0_gnn_Wo"],
        "ln1": f["L0_ffn_ln1_w"].reshape(D, 1),
        "ln2": f["L0_ffn_ln2_w"],
        "wqkv_t": _np.concatenate([wq, f["L0_ffn_wk"], f["L0_ffn_wv"]], 0).T,
        "wo_t": wo.T,
        "router_t": f["L0_ffn_router_w"].T,
        "w1_t": f["L0_ffn_w1"].transpose(2, 0, 1),
        "w2_t": f["L0_ffn_w2"].transpose(2, 0, 1),
        "w3_t": f["L0_ffn_w3"].transpose(2, 0, 1),
        "table": constants(),
    }
    arrays, args = {}, []
    for name, a in laid.items():
        a = _np.ascontiguousarray(a)
        arrays[f"in_{name}"] = a
        args.append(nc.dram_tensor(f"in_{name}", a.shape, _mybir.dt.from_np(a.dtype), kind="ExternalInput").ap())
    args.append(nc.dram_tensor("out_0", (P, NB, D), _mybir.dt.float32, kind="ExternalOutput").ap())
    build(nc, *args)
    r = _run(nc, [arrays], core_ids=[0])
    return _np.ascontiguousarray(r.results[0]["out_0"].transpose(1, 0, 2))
```

```python
from contextlib import ExitStack

import numpy as np

import concourse.bass as bass
from concourse import mybir

ALU = mybir.AluOpType
ACT = mybir.ActivationFunctionType
F32 = mybir.dt.float32
BF16 = mybir.dt.bfloat16
I32 = mybir.dt.int32
U32 = mybir.dt.uint32
U8 = mybir.dt.uint8
AX_X = mybir.AxisListType.X

P = 128
NB = 128
D = 128
G = 4
NG = NB // G
NH, NKV, HD = 4, 2, 32
NREP = NH // NKV
QK = (NH + NKV) * HD
QKV = QK + NKV * HD
NE, HID = 8, int(8 / 3 * D)
N_TOK = NB * P
HEADS = [k * NREP + r for r in range(NREP) for k in range(NKV)]
T_WAKE = 0.1
EPS = 1e-8
EPS_LN = 1e-5
EPS_RMS = 1e-6
NEG = -1e30
SCALE = float(HD) ** -0.5

ROWS = 512
SUB = ROWS // P
REGION = N_TOK + ROWS
ROW_W = D + 4
COL_ID, COL_EXPERT, COL_GATE = D, D + 1, D + 2
N_TILES = 2 * N_TOK // ROWS + NE
CHUNKS = [(c, min(P, HID - c)) for c in range(0, HID, P)]
NC = len(CHUNKS)
W_COLS = 2 * HID + NC * D
LAG = 4
RANKS = 64
FINAL = 16

C_IDENT, C_CAUSAL, C_UPPER, C_COS, C_SIN, C_TOKEN, C_BASE, C_IOTA, C_UPTO, C_STEP, C_TILE, C_PAD = np.cumsum(
    [0, P, P, P, QK, QK, G, NE, NE, NE * NE, N_TOK // ROWS, N_TILES]).tolist()
C_END = C_PAD + SUB


def constants():
    t = np.zeros((P, C_END), np.float32)
    i = np.arange(P)
    t[:, C_IDENT:C_CAUSAL] = np.eye(P)
    t[:, C_CAUSAL:C_UPPER] = np.where(i[None, :] <= i[:, None], 0.0, -NEG)
    t[:, C_UPPER:C_COS] = i[:, None] < i[None, :]
    inv_freq = 1.0 / 10000.0 ** (np.arange(0, HD, 2, dtype=np.float32) / HD)
    freqs = np.outer(i.astype(np.float32), inv_freq)
    cos = np.cos(np.concatenate([freqs, freqs], -1))
    sin = np.sin(np.concatenate([-freqs, freqs], -1))
    scale = np.repeat([-SCALE, 1.0], [NH * HD, NKV * HD])
    t[:, C_COS:C_SIN] = np.tile(cos, (1, NH + NKV)) * scale
    t[:, C_SIN:C_TOKEN] = np.tile(sin, (1, NH + NKV)) * scale
    t[:, C_TOKEN:C_BASE] = i[:, None] * NB + np.arange(G)[None, :]
    t[:, C_BASE:C_IOTA] = np.arange(NE) * REGION
    t[:, C_IOTA:C_UPTO] = np.arange(NE)
    t[:, C_UPTO:C_STEP] = np.tril(np.ones((NE, NE))).reshape(-1)
    t[:, C_STEP:C_TILE] = np.arange(N_TOK // ROWS) * ROWS
    t[:, C_TILE:C_PAD] = np.arange(N_TILES)
    t[:, C_PAD:C_END] = N_TOK + i[:, None] * SUB + np.arange(SUB)[None, :]
    return t


def later(g):
    return not isinstance(g, int) or g > 0


def at(g, work, *args):
    if not isinstance(g, int) or 0 <= g < NG:
        work(g, *args)


def build(nc, x, adj_t, wl, wg, wv_t, wo_gnn, ln1, ln2, wqkv_t, wo_t, router_t, w1_t, w2_t, w3_t, table, out):
    with ExitStack() as ctx:
        def sb(name, shape, dt=F32):
            return ctx.enter_context(nc.sbuf_tensor(name, shape, dt))

        def sem(name):
            return ctx.enter_context(nc.semaphore(name))

        bank_a = [ctx.enter_context(nc.psum_tensor(f"bank_a{i}", [P, 512], F32)) for i in range(3)]
        bank_b = [ctx.enter_context(nc.psum_tensor(f"bank_b{i}", [P, 512], F32)) for i in range(2)]
        bank_c = [ctx.enter_context(nc.psum_tensor(f"bank_c{i}", [P, 512], F32)) for i in range(2)]
        bank_d = ctx.enter_context(nc.psum_tensor("bank_d", [P, 512], F32))

        def tiles(bank, n=G):
            return bank[:].rearrange("p (t d) -> p t d", t=n)

        tab = sb("tab", [P, C_END])
        ident = tab[:, C_IDENT:C_CAUSAL]
        bank_in, bank_up, bank_gate, bank_down = bank_a[0], bank_a[1:3], bank_b, bank_c
        ident_b = sb("ident_b", [P, P], BF16)
        causal_b = sb("causal_b", [P, P], BF16)
        upper_b = sb("upper_b", [P, P], BF16)
        ones_b = sb("ones_b", [P, P], BF16)
        minus_half = sb("minus_half", [P, P])
        adj_bytes = sb("adj_bytes", [P, P // 4], I32)
        adj_f = sb("adj_f", [P, P])
        mask_l = sb("mask_l", [P, P])
        mask_g = sb("mask_g", [P, P])
        w_l = sb("w_l", [P, D])
        w_g = sb("w_g", [P, D])
        w_v_t = sb("w_v_t", [P, D])
        w_o_gnn = sb("w_o_gnn", [P, D])
        w_vo = sb("w_vo", [P, D])
        ln1_col = sb("ln1_col", [P, 1])
        ln2_row = sb("ln2_row", [P, D])
        w_qkv_raw = sb("w_qkv_raw", [P, QKV])
        w_qkv = sb("w_qkv", [P, QKV])
        w_o = sb("w_o", [P, D])
        w_router = sb("w_router", [P, NE])

        resid = sb("resid", [P, NB, D])

        w_all = sb("w_all", [P, NE, W_COLS])
        w_buf = sb("w_buf", [P, 2, W_COLS])
        in_rows = sb("in_rows", [P, 2, SUB, ROW_W])
        pad_rows = sb("pad_rows", [P, SUB, ROW_W])
        filled = sb("filled", [P, NE])
        region_end_i = sb("region_end_i", [P, NE], I32)

        lasting, ctx = ctx, ExitStack()

        a_st = sb("a_st", [P, G, 6])
        a_mv = sb("a_mv", [P, G, 2])
        a_var = sb("a_var", [P, G])
        a_rstd = sb("a_rstd", [P, G])
        a_h = sb("a_h", [P, G, D])
        a_hT = sb("a_hT", [P, G, P])
        zl = sb("zl", [P, G, P])
        zg = sb("zg", [P, G, P])
        zl2 = sb("zl2", [P, G, P])
        zg2 = sb("zg2", [P, G, P])
        sq_l = sb("sq_l", [P, G])
        inv_norm = sb("inv_norm", [P, G])
        guard = sb("guard", [P, G])
        v_l = sb("v_l", [P, G, D + 1])
        v_g = sb("v_g", [P, G, D + 1])
        adj_l = sb("adj_l", [P, G, P])
        arg_g = sb("arg_g", [P, G, P])
        adj_g = sb("adj_g", [P, G, P])
        den_l = sb("den_l", [P, G])
        den_g = sb("den_g", [P, G])
        rec_l = sb("rec_l", [P, G])
        rec_g = sb("rec_g", [P, G])

        b_st = sb("b_st", [P, G, 6])
        b_mv = sb("b_mv", [P, G, 2])
        b_var = sb("b_var", [P, 2, G])
        b_rs = sb("b_rs", [P, 2, G])
        b_rec = sb("b_rec", [P, G])
        b_ratio = sb("b_ratio", [P, G])
        b_h = sb("b_h", [P, G, D])
        h2 = sb("h2", [P, G, D])
        b_hT = sb("b_hT", [P, G, P])
        rope_c = sb("rope_c", [P, G, QK])
        swapped = sb("swapped", [P, G, QK])
        rope_s = sb("rope_s", [P, G, QK])
        roped = sb("roped", [P, G, QK])
        v_attn = sb("v_attn", [P, G, NKV, HD])
        qT = sb("qT", [P, G, P])
        kT = sb("kT", [P, G, P])
        row_min = sb("row_min", [P, NH, G])
        sums = sb("sums", [P, NH, G])
        probs = sb("probs", [P, NH, G, P])

        probs_t = sb("probs_t", [P, NH, G, P])
        sum_rec = sb("sum_rec", [P, NH, G])
        rec_rows = sb("rec_rows", [P, G, NH, HD])
        rec_t = sb("rec_t", [P, G, P])
        yT = sb("yT", [P, G, P])
        xf = sb("xf", [P, G, D])
        sq_junk = sb("sq_junk", [P, G, D], BF16)
        sum_sq = sb("sum_sq", [P, G])
        ms = sb("ms", [P, G])
        rms = sb("rms", [P, G])
        half_col = sb("half_col", [P, 2 * G])

        flat_rows = sb("flat_rows", [P, G, ROW_W])
        flatT = sb("flatT", [P, G, P])
        token_id = sb("token_id", [P, G])
        best = sb("best", [P, G, NE])
        best_at = sb("best_at", [P, G, NE], U32)
        choice = sb("choice", [P, G * 2])
        pick = sb("pick", [P, G, 2, NE])
        chosen_b = sb("chosen_b", [P, G, NE], BF16)
        below = sb("below", [P, G, NE])
        weight = sb("weight", [P, G, NE])
        total = sb("total", [P, G])
        pair = sb("pair", [P, G])
        denom = sb("denom", [P, G])
        denom_rec = sb("denom_rec", [P, G])
        place = sb("place", [P, G + 1, NE])
        picked = sb("picked", [P, G, 2, NE])
        place_f = sb("place_f", [P, G * 2])
        place_i = sb("place_i", [P, G * 2], I32)

        ctx.close()
        ctx = lasting
        counts = sb("counts", [P, NE])
        over = sb("over", [P, NE, N_TOK // ROWS])
        n_tiles = sb("n_tiles", [P, NE])
        upto = sb("upto", [P, NE, NE])
        tiles_upto = sb("tiles_upto", [P, NE])
        passed = sb("passed", [P, N_TILES, NE])
        passed_n = sb("passed_n", [P, N_TILES, NE])
        tile_expert = sb("tile_expert", [P, N_TILES])
        tile_first = sb("tile_first", [P, N_TILES])
        tile_at = sb("tile_at", [P, N_TILES])
        tile_row = sb("tile_row", [P, N_TILES])
        tile_row_i = sb("tile_row_i", [P, N_TILES], I32)
        tile_weights_i = sb("tile_weights_i", [P, N_TILES], I32)
        in_t = sb("in_t", [P, 2, ROWS])
        silu = sb("silu", [P, 2, ROWS])
        hidden = sb("hidden", [P, 2, NC, ROWS])
        second = sb("second", [P, 2, SUB])
        gate_diff = sb("gate_diff", [P, 2, SUB])
        gate_step = sb("gate_step", [P, 2, SUB])
        gate = sb("gate", [P, 2, SUB])
        dest_f = sb("dest_f", [P, 2, SUB])
        dest_i = sb("dest_i", [P, 2, SUB], I32)
        out_rows = sb("out_rows", [P, 2, SUB, D])
        final_in = sb("final_in", [P, 2, 2, FINAL, D])

        grouped = nc.dram_tensor("grouped", (NE * REGION + ROWS, ROW_W), F32, kind="Internal").ap()
        expert_out = nc.dram_tensor("expert_out", (2 * N_TOK + ROWS, D), F32, kind="Internal").ap()

        def sems(names):
            return [sem(name) for name in names.split()]

        const_loaded, adj_loaded, w_loaded, consts_set, adj_set, mask_set, w_qkv_set, wvo_ps = sems(
            "const_loaded adj_loaded w_loaded consts_set adj_set mask_set w_qkv_set wvo_ps")
        wvo_set, ones_set = sems("wvo_set ones_set")
        x_loaded = sem("x_loaded")
        a_stats, a_aggr, a_var_set, a_rstd_set, a_norm, a_hT_ps, a_hT_set, zl_ps = sems(
            "a_stats a_aggr a_var_set a_rstd_set a_norm a_hT_ps a_hT_set zl_ps")
        zg_ps, zl_set, zg_set, zl_sq, zg_sq = sems("zg_ps zl_set zg_set zl_sq zg_sq")
        sql_ps, sql_set, inv_set, guard_set, v_ps, vg_set, vl_set, vl_col_set = sems(
            "sql_ps sql_set inv_set guard_set v_ps vg_set vl_set vl_col_set")
        gl_ps, adj_l_set, gg_ps, arg_g_set, adj_g_set = sems("gl_ps adj_l_set gg_ps arg_g_set adj_g_set")
        outl_ps0, outl_ps1, outg_ps0, outg_ps1, denl_set, recl_set, xl_set0, xl_set1 = sems(
            "outl_ps0 outl_ps1 outg_ps0 outg_ps1 denl_set recl_set xl_set0 xl_set1")
        deng_set, recg_set, x1_half, x1_set = sems("deng_set recg_set x1_half x1_set")
        b_stats, b_aggr, b_var_set, b_rs_set, b_rec_set, b_ratio_set, b_norm, h2_set = sems(
            "b_stats b_aggr b_var_set b_rs_set b_rec_set b_ratio_set b_norm h2_set")
        b_hT_ps, b_hT_set, qkv_ps0, qkv_ps1 = sems("b_hT_ps b_hT_set qkv_ps0 qkv_ps1")
        swap_set0, swap_set1, v1_set, rope_c_set, rope_s_set, roped_set, qT_ps, kT_ps = sems(
            "swap_set0 swap_set1 v1_set rope_c_set rope_s_set roped_set qT_ps kT_ps")
        qT_set, kT_set = sems("qT_set kT_set")
        s_ps, min_set = sems("s_ps min_set")
        prob_set = sem("prob_set")
        pT_ps, pT_set, y_ps, sum_rec_set, rec_rows_set, recT_ps, recT_set = sems("pT_ps pT_set y_ps sum_rec_set rec_rows_set recT_ps recT_set")
        yT_set = sem("yT_set")
        attn_ps, xf_set, sq_set, ms_set, rms_set, resid_set, out_stored = sems(
            "attn_ps xf_set sq_set ms_set rms_set resid_set out_stored")
        flat_set, id_set, id_next, flat_ps, flatT_set, router_ps, best_set, best_at_set = sems(
            "flat_set id_set id_next flat_ps flatT_set router_ps best_set best_at_set")
        choice_set, expert_set, pick_set, chosen_set = sems("choice_set expert_set pick_set chosen_set")
        rank_ps, below_set, weight_set, total_set, pair_set, denom_set, denom_rec_set, gates_set = sems(
            "rank_ps below_set weight_set total_set pair_set denom_set denom_rec_set gates_set")
        place_set, filled_set, picked_set = sems("place_set filled_set picked_set")
        place_f_set, place_i_set, scattered = sems("place_f_set place_i_set scattered")
        wall_loaded, pad_zero, pad_set, pad_stored, table_step, table_set = sems(
            "wall_loaded pad_zero pad_set pad_stored table_step table_set")
        wbuf_loaded0, wbuf_loaded1, rows_loaded0, rows_loaded1, inT_ps, inT_set, up_ps, gate_ps = sems(
            "wbuf_loaded0 wbuf_loaded1 rows_loaded0 rows_loaded1 inT_ps inT_set up_ps gate_ps")
        silu_set, hidden_set, down_ps = sems("silu_set hidden_set down_ps")
        second_set, gdiff_set, gstep_set, gate_set, destf_set, dest_set, outrows_set, placed0 = sems(
            "second_set gdiff_set gstep_set gate_set destf_set dest_set outrows_set placed0")
        placed1 = sem("placed1")
        final_loaded0, final_loaded1, sum_half, sum_set = sems("final_loaded0 final_loaded1 sum_half sum_set")

        block = ctx.enter_context(nc.Block())

        @block.sync
        def _(sp):
            sp.dma_start(tab[:], table).then_inc(const_loaded, 16)
            sp.dma_start(adj_bytes[:], adj_t).then_inc(adj_loaded, 16)
            for dst, src in ((w_l, wl), (w_g, wg), (w_v_t, wv_t), (w_o_gnn, wo_gnn), (ln1_col, ln1), (w_qkv_raw, wqkv_t),
                             (w_o, wo_t), (w_router, router_t)):
                sp.dma_start(dst[:], src).then_inc(w_loaded, 16)
            sp.dma_start(ln2_row[:], ln2.partition_broadcast(P)).then_inc(w_loaded, 16)
            sp.dma_start(resid[:, 0:G, :], x[:, 0:G, :]).then_inc(x_loaded, 16)
            with sp.Fori(1, NG) as g:
                sp.wait_ge(x_loaded, g * 16)
                sp.dma_start(resid[:, bass.ds(g * G, G), :], x[:, bass.ds(g * G, G), :]).then_inc(x_loaded, 16)
            sp.wait_ge(ones_set, 1)
            sp.dma_start(w_all[:, :, 0:HID], w1_t).then_inc(wall_loaded, 16)
            sp.dma_start(w_all[:, :, HID:2 * HID], w3_t).then_inc(wall_loaded, 16)
            for c, (c0, cn) in enumerate(CHUNKS):
                w2_at = 2 * HID + c * D
                sp.dma_start(w_all[0:cn, :, w2_at:w2_at + D], w2_t[c0:c0 + cn]).then_inc(wall_loaded, 16)
            pads = grouped.rearrange("n w -> n w")
            sp.wait_ge(pad_set, 1)
            sp.dma_start(pads[NE * REGION:NE * REGION + ROWS].rearrange("(p i) w -> p i w", i=SUB), pad_rows[:]).then_inc(
                pad_stored, 16)
            sp.wait_ge(table_set, 1)
            for e in range(NE):
                end = sp.value_load(region_end_i[0:1, e:e + 1], min_val=0, max_val=NE * REGION - ROWS)
                sp.dma_start(pads[bass.ds(end, ROWS)].rearrange("(p i) w -> p i w", i=SUB), pad_rows[:]).then_inc(pad_stored, 16)
            sp.wait_ge(scattered, NG * G * 2 * 16)
            sp.wait_ge(pad_stored, (NE + 1) * 16)
            sp.wait_ge(wall_loaded, (2 + NC) * 16)

            def load_tile(pair_no, u):
                j = pair_no * 2 + u
                if later(pair_no):
                    sp.wait_ge(down_ps, j - 1)
                    sp.wait_ge(inT_ps, j - 1)
                    sp.wait_ge(gate_set, j - 1)
                    sp.wait_ge(destf_set, j - 1)
                    sp.wait_ge(gdiff_set, j - 1)
                row = sp.value_load(tile_row_i[0:1, bass.ds(j, 1)], min_val=0, max_val=NE * REGION)
                sp.dma_start(in_rows[:, u, :, :], grouped[bass.ds(row, ROWS)].rearrange("(p i) w -> p i w", i=SUB)).then_inc(
                    [rows_loaded0, rows_loaded1][u], 16)
                e = sp.value_load(tile_weights_i[0:1, bass.ds(j, 1)], min_val=0, max_val=NE - 1)
                sp.dma_start(w_buf[:, u, :], w_all[:, bass.ds(e, 1), :].rearrange("p a w -> p (a w)")).then_inc(
                    [wbuf_loaded0, wbuf_loaded1][u], 16)

            load_tile(0, 0)
            load_tile(0, 1)
            with sp.Fori(1, N_TILES // 2) as k:
                load_tile(k, 0)
                load_tile(k, 1)

            sp.wait_ge(placed0, N_TILES // 2 * SUB * 16)
            sp.wait_ge(placed1, N_TILES // 2 * SUB * 16)
            halves = [expert_out[i * N_TOK:(i + 1) * N_TOK].rearrange("(p b) d -> p b d", b=NB) for i in range(2)]
            for i in range(NB // FINAL):
                if i >= 2:
                    sp.wait_ge(sum_set, i - 1)
                for n in range(2):
                    sp.dma_start(final_in[:, i % 2, n, :, :], halves[n][:, i * FINAL:(i + 1) * FINAL, :]).then_inc(
                        [final_loaded0, final_loaded1][i % 2], 16)

        W_LOADED = 16 * 9

        @block.gpsimd
        def _(pool):
            nc.gpsimd.memset(half_col[:], -0.5)
            nc.gpsimd.memset(minus_half[:], -0.5)
            nc.gpsimd.memset(v_g[:], 1.0)
            nc.gpsimd.memset(w_all[:, :, 2 * HID + (NC - 1) * D:], 0.0)
            nc.gpsimd.memset(ones_b[:], 1.0).then_inc(ones_set, 1)
            nc.gpsimd.memset(pad_rows[:], 0.0).then_inc(pad_zero, 1)
            pool.wait_ge(adj_set, 1)
            nc.gpsimd.affine_select(out=mask_l[:], in_=adj_f[:], compare_op=ALU.not_equal, fill=0.0, base=0,
                                    pattern=[[-1, P]], channel_multiplier=1).then_inc(mask_set, 1)
            pool.wait_ge(mask_set, 1)
            nc.gpsimd.tensor_scalar(mask_g[:], mask_l[:], 1.0, -NEG, ALU.subtract, ALU.mult).then_inc(mask_set, 1)

            def a_rstd_pow(g):
                pool.wait_ge(a_var_set, g + 1)
                if later(g):
                    pool.wait_ge(a_norm, g)
                nc.gpsimd.tensor_tensor(a_rstd[:], a_var[:], half_col[:, 0:G], ALU.pow).then_inc(a_rstd_set, 1)

            def a_inverse_norms(g):
                pool.wait_ge(sql_set, g + 1)
                if later(g):
                    pool.wait_ge(vl_set, g)
                nc.gpsimd.tensor_tensor(inv_norm[:], sq_l[:], half_col[:, 0:G], ALU.pow).then_inc(inv_set, 1)
                pool.wait_ge(inv_set, g + 1)
                if later(g):
                    pool.wait_ge(denl_set, g)
                nc.gpsimd.tensor_tensor(guard[:], sq_l[:], inv_norm[:], ALU.mult).then_inc(guard_set, 1)
                if later(g):
                    pool.wait_ge(outl_ps1, g)
                pool.nop(nofuse=True)
                nc.gpsimd.tensor_copy(v_l[:, :, D], inv_norm[:]).then_inc(vl_col_set, 1)

            def b_pow(g):
                pool.wait_ge(b_var_set, g + 1)
                if later(g):
                    pool.wait_ge(b_ratio_set, g)
                nc.gpsimd.tensor_tensor(b_rs[:].rearrange("p a b -> p (a b)"), b_var[:].rearrange("p a b -> p (a b)"),
                                        half_col[:], ALU.pow).then_inc(b_rs_set, 1)

            def b_h2(g):
                pool.wait_ge(b_rec_set, g + 1)
                nc.gpsimd.tensor_tensor(b_ratio[:], b_rs[:, 0, :], b_rec[:], ALU.mult).then_inc(b_ratio_set, 1)
                pool.wait_ge(b_ratio_set, g + 1)
                pool.wait_ge(b_norm, g + 1)
                if later(g):
                    pool.wait_ge(xf_set, g)
                nc.gpsimd.tensor_tensor(h2[:], b_h[:], b_ratio[:].unsqueeze(2).broadcast_to([P, G, D]),
                                        ALU.mult).then_inc(h2_set, 1)

            def b_rope_sin(g, half):
                pool.wait_ge([swap_set0, swap_set1][half], g + 1)
                if later(g):
                    pool.wait_ge(roped_set, g)
                t = slice(2 * half, 2 * half + 2)
                sin = tab[:, C_SIN:C_TOKEN].unsqueeze(1).broadcast_to([P, 2, QK])
                nc.gpsimd.tensor_tensor(rope_s[:, t, :], swapped[:, t, :], sin, ALU.mult).then_inc(rope_s_set, 1)

            def c_rms_pow(g):
                pool.wait_ge(ms_set, g + 1)
                if later(g):
                    pool.wait_ge(flat_set, g)
                nc.gpsimd.tensor_tensor(rms[:], ms[:], half_col[:, 0:G], ALU.pow).then_inc(rms_set, 1)

            def c_scatter(g, i):
                if i == 0:
                    pool.wait_ge(flat_set, g + 1)
                    pool.wait_ge(id_set, g + 1)
                    pool.wait_ge(expert_set, g + 1)
                    pool.wait_ge(gates_set, g + 1)
                    pool.wait_ge(place_i_set, g + 1)
                    pool.nop(nofuse=True)
                nc.gpsimd.indirect_dma_start(
                    out=grouped, out_offset=bass.IndirectOffsetOnAxis(ap=place_i[:, i:i + 1].bitcast(U32), axis=0),
                    in_=flat_rows[:, i // 2, :], in_offset=None).then_inc(scattered, 16)

            def c_resid(g):
                pool.wait_ge(xf_set, g + 1)
                pool.nop(nofuse=True)
                rg = resid[:, bass.ds(g * G, G), :]
                nc.gpsimd.tensor_tensor(rg, xf[:], rg, ALU.add).then_inc(resid_set, 1)

            def step(k):
                at(k - 4, c_scatter, 1)
                at(k - 4, c_scatter, 2)
                at(k - 4, c_scatter, 3)
                at(k - 4, c_scatter, 4)
                at(k - 4, c_scatter, 5)
                at(k - 4, c_scatter, 6)
                at(k, a_rstd_pow)
                at(k - 4, c_scatter, 7)
                at(k - 2, b_h2)
                at(k - 3, c_rms_pow)
                at(k - 3, c_resid)
                at(k - 1, b_pow)
                at(k, a_inverse_norms)
                at(k - 3, c_scatter, 0)
                at(k - 1, b_rope_sin, 0)
                at(k - 1, b_rope_sin, 1)

            for k in range(LAG + 1):
                step(k)
            with pool.Fori(LAG + 1, NG) as k:
                step(k)
            for k in range(NG, NG + LAG):
                step(k)

            def place_tile(pair_no, u):
                j = pair_no * 2 + u
                pool.wait_ge(dest_set, j + 1)
                pool.wait_ge(outrows_set, j + 1)
                if u == 1:
                    pool.wait_ge(placed0, pair_no * (SUB * 16) + SUB * 16)
                elif later(pair_no):
                    pool.wait_ge(placed1, pair_no * (SUB * 16))
                pool.nop(nofuse=True)
                for i in range(SUB):
                    nc.gpsimd.indirect_dma_start(
                        out=expert_out, out_offset=bass.IndirectOffsetOnAxis(ap=dest_i[:, u, i:i + 1].bitcast(U32), axis=0),
                        in_=out_rows[:, u, i, :], in_offset=None).then_inc([placed0, placed1][u], 16)

            place_tile(0, 0)
            place_tile(0, 1)
            with pool.Fori(1, N_TILES // 2) as k:
                place_tile(k, 0)
                place_tile(k, 1)

        @block.vector
        def _(dve):
            dve.wait_ge(const_loaded, 16)
            nc.vector.tensor_copy(ident_b[:], ident)
            nc.vector.tensor_copy(causal_b[:], tab[:, C_CAUSAL:C_UPPER])
            nc.vector.tensor_copy(upper_b[:], tab[:, C_UPPER:C_COS]).then_inc(consts_set, 1)
            dve.wait_ge(adj_loaded, 16)
            nc.vector.tensor_copy(adj_f[:], adj_bytes[:].bitcast(U8)).then_inc(adj_set, 1)
            dve.wait_ge(w_loaded, W_LOADED)
            nc.vector.tensor_scalar(w_qkv[:], w_qkv_raw[:], ln1_col[:, 0:1], None, ALU.mult).then_inc(w_qkv_set, 1)
            dve.wait_ge(wvo_ps, 1)
            nc.vector.tensor_copy(w_vo[:], bank_a[0][:, 0:D]).then_inc(wvo_set, 1)
            nc.vector.tensor_copy(token_id[:], tab[:, C_TOKEN:C_BASE]).then_inc(id_next, 1)
            nc.vector.tensor_copy(filled[:], tab[:, C_BASE:C_IOTA]).then_inc(filled_set, 1)
            dve.wait_ge(pad_zero, 1)
            nc.vector.tensor_copy(pad_rows[:, :, COL_ID], tab[:, C_PAD:C_END])
            nc.vector.memset(pad_rows[:, :, COL_EXPERT], -1.0).then_inc(pad_set, 1)
            dve.wait_ge(mask_set, 2)

            def a_statistics(g):
                dve.wait_ge(x_loaded, g * 16 + 16)
                dve.nop(nofuse=True)
                for t in range(G):
                    last = nc.vector.bn_stats(a_st[:, t, :], resid[:, bass.ds(g * G + t, 1), :].rearrange("p a d -> p (a d)"))
                last.then_inc(a_stats, 1)
                dve.wait_ge(a_stats, g + 1)
                dve.nop(nofuse=True)
                for t in range(G):
                    last = nc.vector.bn_aggr(a_mv[:, t, :], a_st[:, t, :])
                last.then_inc(a_aggr, 1)
                dve.wait_ge(a_aggr, g + 1)
                nc.vector.tensor_scalar(a_var[:], a_mv[:, :, 1], EPS_LN, None, ALU.add).then_inc(a_var_set, 1)

            def a_normalise(g):
                dve.wait_ge(a_rstd_set, g + 1)
                if later(g):
                    dve.wait_ge(a_hT_ps, g)
                dve.nop(nofuse=True)
                for t in range(G):
                    last = nc.vector.tensor_scalar(
                        a_h[:, t, :], resid[:, bass.ds(g * G + t, 1), :].rearrange("p a d -> p (a d)"),
                        a_mv[:, t, 0:1], a_rstd[:, t:t + 1], ALU.subtract, ALU.mult)
                last.then_inc(a_norm, 1)

            def a_floor(g):
                dve.wait_ge(sql_ps, g + 1)
                if later(g):
                    dve.wait_ge(guard_set, g)
                nc.vector.tensor_scalar(sq_l[:], bank_a[2][:, 0:G], EPS * EPS, None, ALU.max).then_inc(sql_set, 1)

            def a_adj_l(g):
                dve.wait_ge(gl_ps, g + 1)
                if later(g):
                    dve.wait_ge(outl_ps1, g)
                nc.vector.scalar_tensor_tensor(adj_l[:], tiles(bank_a[1]), 0.0, mask_l[:].unsqueeze(1).broadcast_to([P, G, P]),
                                               ALU.max, ALU.mult).then_inc(adj_l_set, 1)

            def a_values_l(g):
                dve.wait_ge(v_ps, g + 1)
                dve.wait_ge(vg_set, g + 1)
                dve.wait_ge(inv_set, g + 1)
                if later(g):
                    dve.wait_ge(outl_ps1, g)
                nc.vector.scalar_tensor_tensor(v_l[:, :, 0:D], tiles(bank_a[0]), 1.0 - T_WAKE,
                                               inv_norm[:].unsqueeze(2).broadcast_to([P, G, D]), ALU.mult,
                                               ALU.mult).then_inc(vl_set, 1)

            def a_arg_g(g):
                dve.wait_ge(gg_ps, g + 1)
                if later(g):
                    dve.wait_ge(adj_g_set, g)
                nc.vector.tensor_tensor(arg_g[:], tiles(bank_a[2]), mask_g[:].unsqueeze(1).broadcast_to([P, G, P]),
                                        ALU.min).then_inc(arg_g_set, 1)

            def halves(bank):
                return bank[:, 0:2 * (D + 1)].rearrange("p (t d) -> p t d", t=2)

            def a_scale_l(g):
                for h in range(2):
                    dve.wait_ge([outl_ps0, outl_ps1][h], g + 1)
                    if h == 0:
                        dve.wait_ge(guard_set, g + 1)
                    last = nc.vector.scalar_tensor_tensor(
                        den_l[:, 2 * h:2 * h + 2], guard[:, 2 * h:2 * h + 2], EPS, halves(bank_a[h])[:, :, D],
                        ALU.mult, ALU.max)
                last.then_inc(denl_set, 1)
                dve.wait_ge(denl_set, g + 1)
                nc.vector.reciprocal(rec_l[:], den_l[:]).then_inc(recl_set, 1)
                dve.wait_ge(recl_set, g + 1)
                dve.nop(nofuse=True)
                for h in range(2):
                    for t in (2 * h, 2 * h + 1):
                        x_t = resid[:, bass.ds(g * G + t, 1), :].rearrange("p a d -> p (a d)")
                        last = nc.vector.scalar_tensor_tensor(x_t, halves(bank_a[h])[:, t % 2, 0:D], rec_l[:, t:t + 1], x_t,
                                                              ALU.mult, ALU.add)
                    last.then_inc([xl_set0, xl_set1][h], 1)

            def a_scale_g(g):
                for h in range(2):
                    dve.wait_ge([outg_ps0, outg_ps1][h], g + 1)
                    last = nc.vector.tensor_scalar(den_g[:, 2 * h:2 * h + 2], halves(bank_a[2 - 2 * h])[:, :, D], EPS, None,
                                                   ALU.max)
                last.then_inc(deng_set, 1)
                dve.wait_ge(deng_set, g + 1)
                nc.vector.reciprocal(rec_g[:], den_g[:]).then_inc(recg_set, 1)
                dve.wait_ge(recg_set, g + 1)
                dve.wait_ge(xl_set1, g + 1)
                dve.nop(nofuse=True)
                for h in range(2):
                    for t in (2 * h, 2 * h + 1):
                        x_t = resid[:, bass.ds(g * G + t, 1), :].rearrange("p a d -> p (a d)")
                        last = nc.vector.scalar_tensor_tensor(x_t, halves(bank_a[2 - 2 * h])[:, t % 2, 0:D],
                                                              rec_g[:, t:t + 1], x_t, ALU.mult, ALU.add)
                    last.then_inc([x1_half, x1_set][h], 1)

            def b_statistics(g):
                dve.wait_ge(x1_set, g + 1)
                dve.nop(nofuse=True)
                for t in range(G):
                    last = nc.vector.bn_stats(b_st[:, t, :], resid[:, bass.ds(g * G + t, 1), :].rearrange("p a d -> p (a d)"))
                last.then_inc(b_stats, 1)
                dve.wait_ge(b_stats, g + 1)
                dve.nop(nofuse=True)
                for t in range(G):
                    last = nc.vector.bn_aggr(b_mv[:, t, :], b_st[:, t, :])
                last.then_inc(b_aggr, 1)
                dve.wait_ge(b_aggr, g + 1)
                nc.vector.tensor_scalar(b_var[:, 0, :], b_mv[:, :, 1], EPS_LN, None, ALU.add)
                nc.vector.tensor_scalar(b_var[:, 1, :], b_mv[:, :, 1], 1.0 + EPS_RMS, EPS_RMS * EPS_LN,
                                        ALU.mult, ALU.add).then_inc(b_var_set, 1)

            def b_normalise(g):
                dve.wait_ge(b_rs_set, g + 1)
                if later(g):
                    dve.wait_ge(b_ratio_set, g)
                nc.vector.reciprocal(b_rec[:], b_rs[:, 1, :]).then_inc(b_rec_set, 1)
                if later(g):
                    dve.wait_ge(b_hT_ps, g)
                    dve.wait_ge(h2_set, g)
                dve.nop(nofuse=True)
                for t in range(G):
                    last = nc.vector.tensor_scalar(
                        b_h[:, t, :], resid[:, bass.ds(g * G + t, 1), :].rearrange("p a d -> p (a d)"),
                        b_mv[:, t, 0:1], b_rs[:, 1, t:t + 1], ALU.subtract, ALU.mult)
                last.then_inc(b_norm, 1)

            def b_rope_cos(g, half):
                dve.wait_ge([qkv_ps0, qkv_ps1][half], g + 1)
                dve.wait_ge([swap_set0, swap_set1][half], g + 1)
                qk = tiles(bank_b[1 - half], 2)[:, :, 0:QK]
                cos = tab[:, C_COS:C_SIN].unsqueeze(1).broadcast_to([P, 2, QK])
                last = nc.vector.tensor_tensor(rope_c[:, 2 * half:2 * half + 2, :], qk, cos, ALU.mult)
                last.then_inc(rope_c_set, 1)

            def b_rope_add(g):
                dve.wait_ge(rope_c_set, g * 2 + 2)
                dve.wait_ge(rope_s_set, g * 2 + 2)
                if later(g):
                    dve.wait_ge(kT_ps, g)
                nc.vector.tensor_tensor(roped[:], rope_c[:], rope_s[:], ALU.add).then_inc(roped_set, 1)

            def b_row_min(g, h):
                dve.wait_ge(s_ps, g * NH + h + 1)
                if later(g):
                    dve.wait_ge(prob_set, g * NH - NH + h + 1)
                nc.vector.tensor_reduce(row_min[:, h, :], tiles(bank_b[1 - h % 2]), AX_X, ALU.min).then_inc(min_set, 1)

            def c_sum_rec(g):
                dve.wait_ge(prob_set, g * NH + NH)
                if later(g):
                    dve.wait_ge(rec_rows_set, g)
                nc.vector.reciprocal(sum_rec[:], sums[:]).then_inc(sum_rec_set, 1)

            def c_normalise_y(g):
                dve.wait_ge(recT_set, g + 1)
                dve.wait_ge(y_ps, g + 1)
                if later(g):
                    dve.wait_ge(attn_ps, g)
                nc.vector.tensor_tensor(yT[:], tiles(bank_c[0]), rec_t[:], ALU.mult).then_inc(yT_set, 1)

            def c_block_input(g):
                dve.wait_ge(attn_ps, g + 1)
                dve.wait_ge(h2_set, g + 1)
                if later(g):
                    dve.wait_ge(resid_set, g)
                    dve.wait_ge(sq_set, g)
                nc.vector.tensor_tensor(xf[:], tiles(bank_c[1]), h2[:], ALU.add).then_inc(xf_set, 1)

            def c_mean_square(g):
                dve.wait_ge(sq_set, g + 1)
                if later(g):
                    dve.wait_ge(rms_set, g)
                nc.vector.tensor_scalar(ms[:], sum_sq[:], 1.0 / D, EPS_RMS, ALU.mult, ALU.add).then_inc(ms_set, 1)

            def c_flat(g):
                dve.wait_ge(rms_set, g + 1)
                if later(g):
                    dve.wait_ge(scattered, g * (G * 2 * 16))
                    dve.wait_ge(flat_ps, g)
                dve.nop(nofuse=True)
                for t in range(G):
                    last = nc.vector.scalar_tensor_tensor(flat_rows[:, t, 0:D], xf[:, t, :], rms[:, t:t + 1], ln2_row[:],
                                                          ALU.mult, ALU.mult)
                last.then_inc(flat_set, 1)
                dve.wait_ge(id_next, g + 1)
                nc.vector.tensor_copy(flat_rows[:, :, COL_ID], token_id[:]).then_inc(id_set, 1)
                dve.wait_ge(id_set, g + 1)
                nc.vector.tensor_scalar(token_id[:], token_id[:], float(G), None, ALU.add).then_inc(id_next, 1)

            def c_choose(g):
                logits = bank_d[:, 0:G * NE].rearrange("p (t e) -> p t e", t=G)
                dve.wait_ge(router_ps, g + 1)
                dve.nop(nofuse=True)
                for t in range(G):
                    last = nc.vector.max(best[:, t, :], logits[:, t, :])
                last.then_inc(best_set, 1)
                dve.wait_ge(best_set, g + 1)
                dve.nop(nofuse=True)
                for t in range(G):
                    last = nc.vector.max_index(best_at[:, t, :], best[:, t, :], logits[:, t, :])
                last.then_inc(best_at_set, 1)
                dve.wait_ge(best_at_set, g + 1)
                nc.vector.tensor_copy(choice[:].rearrange("p (t n) -> p t n", n=2), best_at[:, :, 0:2]).then_inc(choice_set, 1)
                dve.wait_ge(choice_set, g + 1)
                nc.vector.tensor_tensor(
                    pick[:].rearrange("p t n e -> p (t n) e"), tab[:, C_IOTA:C_UPTO].unsqueeze(1).broadcast_to([P, 2 * G, NE]),
                    choice[:].unsqueeze(2).broadcast_to([P, 2 * G, NE]), ALU.is_equal).then_inc(pick_set, 1)
                nc.vector.tensor_copy(flat_rows[:, :, COL_EXPERT], choice[:].rearrange("p (t n) -> p t n", n=2)[:, :, 0]).then_inc(
                    expert_set, 1)
                dve.wait_ge(pick_set, g + 1)
                if later(g):
                    dve.wait_ge(rank_ps, g)
                nc.vector.tensor_tensor(chosen_b[:], pick[:, :, 0, :], pick[:, :, 1, :], ALU.add).then_inc(chosen_set, 1)
                if later(g):
                    dve.wait_ge(weight_set, g)
                nc.vector.tensor_tensor(below[:], best[:], best[:, :, 0:1].broadcast_to([P, G, NE]), ALU.subtract).then_inc(
                    below_set, 1)

            def c_gates(g):
                dve.wait_ge(weight_set, g + 1)
                nc.vector.tensor_reduce(total[:], weight[:], AX_X, ALU.add).then_inc(total_set, 1)
                nc.vector.tensor_tensor(pair[:], weight[:, :, 0], weight[:, :, 1], ALU.add).then_inc(pair_set, 1)
                dve.wait_ge(total_set, g + 1)
                dve.wait_ge(pair_set, g + 1)
                nc.vector.scalar_tensor_tensor(denom[:], total[:], 1e-9, pair[:], ALU.mult, ALU.add).then_inc(denom_set, 1)
                dve.wait_ge(denom_set, g + 1)
                nc.vector.reciprocal(denom_rec[:], denom[:]).then_inc(denom_rec_set, 1)
                dve.wait_ge(denom_rec_set, g + 1)
                nc.vector.tensor_tensor(flat_rows[:, :, COL_GATE:COL_GATE + 2], weight[:, :, 0:2],
                                        denom_rec[:].unsqueeze(2).broadcast_to([P, G, 2]), ALU.mult).then_inc(gates_set, 1)

            def c_places(g):
                dve.wait_ge(rank_ps, g + 1)
                dve.wait_ge(filled_set, g + 1)
                nc.vector.tensor_tensor(place[:], bank_d[:, RANKS:RANKS + (G + 1) * NE].rearrange("p (t e) -> p t e", e=NE),
                                        filled[:].unsqueeze(1).broadcast_to([P, G + 1, NE]), ALU.add).then_inc(place_set, 1)
                dve.wait_ge(place_set, g + 1)
                nc.vector.tensor_copy(filled[:], place[:, G, :]).then_inc(filled_set, 1)
                nc.vector.tensor_tensor(picked[:], pick[:], place[:, 0:G, :].unsqueeze(2).broadcast_to([P, G, 2, NE]),
                                        ALU.mult).then_inc(picked_set, 1)
                dve.wait_ge(picked_set, g + 1)
                nc.vector.tensor_reduce(place_f[:], picked[:].rearrange("p t n e -> p (t n) e"), AX_X, ALU.add).then_inc(
                    place_f_set, 1)
                dve.wait_ge(place_f_set, g + 1)
                nc.vector.tensor_copy(place_i[:], place_f[:]).then_inc(place_i_set, 1)

            def step(k):
                at(k, a_statistics)
                at(k - 2, b_rope_cos, 0)
                at(k - 1, a_adj_l)
                at(k - 2, b_rope_cos, 1)
                at(k - 2, b_rope_add)
                at(k - 1, a_values_l)
                at(k - 1, a_arg_g)
                at(k - 3, c_normalise_y)
                at(k - 1, a_scale_l)
                at(k - 3, c_block_input)
                at(k - 2, b_row_min, 0)
                at(k - 1, a_scale_g)
                at(k - 2, b_row_min, 1)
                at(k, a_normalise)
                at(k - 3, c_mean_square)
                at(k - 2, b_row_min, 2)
                at(k - 1, b_statistics)
                at(k - 3, c_flat)
                at(k - 2, b_row_min, 3)
                at(k - 1, b_normalise)
                at(k - 3, c_choose)
                at(k, a_floor)
                at(k - 2, c_sum_rec)
                at(k - 3, c_gates)
                at(k - 3, c_places)

            for k in range(LAG + 1):
                step(k)
            with dve.Fori(LAG + 1, NG) as k:
                step(k)
            for k in range(NG, NG + LAG):
                step(k)

            dve.wait_ge(filled_set, NG + 1)
            nc.vector.tensor_tensor(counts[:], filled[:], tab[:, C_BASE:C_IOTA], ALU.subtract).then_inc(table_step, 1)
            nc.vector.tensor_copy(region_end_i[:], filled[:])
            dve.wait_ge(table_step, 1)
            n_steps = N_TOK // ROWS
            nc.vector.tensor_tensor(over[:], counts[:].unsqueeze(2).broadcast_to([P, NE, n_steps]),
                                    tab[:, C_STEP:C_TILE].unsqueeze(1).broadcast_to([P, NE, n_steps]), ALU.is_gt).then_inc(
                table_step, 1)
            dve.wait_ge(table_step, 2)
            nc.vector.tensor_reduce(n_tiles[:], over[:], AX_X, ALU.add).then_inc(table_step, 1)
            dve.wait_ge(table_step, 3)
            nc.vector.tensor_tensor(upto[:], tab[:, C_UPTO:C_STEP].rearrange("p (e j) -> p e j", e=NE),
                                    n_tiles[:].unsqueeze(1).broadcast_to([P, NE, NE]), ALU.mult).then_inc(table_step, 1)
            dve.wait_ge(table_step, 4)
            nc.vector.tensor_reduce(tiles_upto[:], upto[:], AX_X, ALU.add).then_inc(table_step, 1)
            dve.wait_ge(table_step, 5)
            numbers = tab[:, C_TILE:C_PAD]
            nc.vector.tensor_tensor(passed[:], numbers.unsqueeze(2).broadcast_to([P, N_TILES, NE]),
                                    tiles_upto[:].unsqueeze(1).broadcast_to([P, N_TILES, NE]), ALU.is_ge).then_inc(table_step, 1)
            dve.wait_ge(table_step, 6)
            nc.vector.tensor_reduce(tile_expert[:], passed[:], AX_X, ALU.add).then_inc(table_step, 1)
            nc.vector.tensor_tensor(passed_n[:], passed[:], n_tiles[:].unsqueeze(1).broadcast_to([P, N_TILES, NE]),
                                    ALU.mult).then_inc(table_step, 1)
            dve.wait_ge(table_step, 8)
            nc.vector.tensor_reduce(tile_first[:], passed_n[:], AX_X, ALU.add).then_inc(table_step, 1)
            dve.wait_ge(table_step, 9)
            nc.vector.tensor_tensor(tile_at[:], numbers, tile_first[:], ALU.subtract).then_inc(table_step, 1)
            dve.wait_ge(table_step, 10)
            nc.vector.tensor_scalar(tile_first[:], tile_expert[:], float(REGION), None, ALU.mult).then_inc(table_step, 1)
            dve.wait_ge(table_step, 11)
            nc.vector.scalar_tensor_tensor(tile_row[:], tile_at[:], float(ROWS), tile_first[:], ALU.mult, ALU.add).then_inc(
                table_step, 1)
            dve.wait_ge(table_step, 12)
            nc.vector.tensor_scalar(tile_weights_i[:], tile_expert[:], float(NE - 1), None, ALU.min)
            nc.vector.tensor_scalar(tile_row_i[:], tile_row[:], float(NE * REGION), None, ALU.min).then_inc(table_set, 1)

            def gates_and_places(pair_no, u):
                j = pair_no * 2 + u
                rows = in_rows[:, u, :, :]
                dve.wait_ge([rows_loaded0, rows_loaded1][u], pair_no * 16 + 16)
                dve.nop(nofuse=True)
                nc.vector.tensor_scalar(second[:, u, :], rows[:, :, COL_EXPERT], tile_expert[:, bass.ds(j, 1)], None,
                                        ALU.not_equal).then_inc(second_set, 1)
                nc.vector.tensor_tensor(gate_diff[:, u, :], rows[:, :, COL_GATE + 1], rows[:, :, COL_GATE],
                                        ALU.subtract).then_inc(gdiff_set, 1)
                dve.wait_ge(second_set, j + 1)
                if later(pair_no):
                    dve.wait_ge(dest_set, j - 1)
                nc.vector.scalar_tensor_tensor(dest_f[:, u, :], second[:, u, :], float(N_TOK), rows[:, :, COL_ID],
                                               ALU.mult, ALU.add).then_inc(destf_set, 1)
                dve.wait_ge(gdiff_set, j + 1)
                nc.vector.tensor_tensor(gate_step[:, u, :], second[:, u, :], gate_diff[:, u, :], ALU.mult).then_inc(gstep_set, 1)
                dve.wait_ge(gstep_set, j + 1)
                nc.vector.tensor_tensor(gate[:, u, :], gate_step[:, u, :], rows[:, :, COL_GATE], ALU.add).then_inc(gate_set, 1)
                dve.wait_ge(destf_set, j + 1)
                if later(pair_no):
                    dve.wait_ge([placed0, placed1][u], pair_no * (SUB * 16))
                nc.vector.tensor_copy(dest_i[:, u, :], dest_f[:, u, :]).then_inc(dest_set, 1)

            def hidden_chunk(pair_no, u, c):
                j = pair_no * 2 + u
                n = CHUNKS[c][1]
                dve.wait_ge(gate_ps, j * NC + c + 1)
                dve.wait_ge(silu_set, j * NC + c + 1)
                if later(pair_no):
                    dve.wait_ge(down_ps, j - 1)
                nc.vector.tensor_tensor(hidden[0:n, u, c, :], bank_gate[(u * NC + c) % 2][0:n, :], silu[0:n, (u * NC + c) % 2, :],
                                        ALU.mult).then_inc(hidden_set, 1)

            def scale_rows(pair_no, u):
                j = pair_no * 2 + u
                dve.wait_ge(down_ps, j + 1)
                dve.wait_ge(gate_set, j + 1)
                if later(pair_no):
                    dve.wait_ge([placed0, placed1][u], pair_no * (SUB * 16))
                nc.vector.tensor_tensor(out_rows[:, u, :, :], tiles(bank_down[u]), gate[:, u, :].unsqueeze(2).broadcast_to([P, SUB, D]),
                                        ALU.mult).then_inc(outrows_set, 1)

            def expert_pair(pair_no):
                for u in range(2):
                    gates_and_places(pair_no, u)
                    for c in range(NC):
                        hidden_chunk(pair_no, u, c)
                    scale_rows(pair_no, u)

            expert_pair(0)
            with dve.Fori(1, N_TILES // 2) as k:
                expert_pair(k)

            for i in range(NB // FINAL):
                r = resid[:, i * FINAL:(i + 1) * FINAL, :]
                dve.wait_ge([final_loaded0, final_loaded1][i % 2], (i // 2 + 1) * 32)
                if i == 0:
                    dve.wait_ge(resid_set, NG)
                nc.vector.tensor_tensor(r, r, final_in[:, i % 2, 0, :, :], ALU.add).then_inc(sum_half, 1)
                dve.wait_ge(sum_half, i + 1)
                nc.vector.tensor_tensor(r, r, final_in[:, i % 2, 1, :, :], ALU.add).then_inc(sum_set, 1)

        @block.scalar
        def _(act):
            act.wait_ge(ones_set, 1)

            def copy_bank(dst, bank):
                return nc.scalar.activation(dst, bank, ACT.Copy)

            def a_copy_hT(g):
                act.wait_ge(a_hT_ps, g + 1)
                if later(g):
                    act.wait_ge(v_ps, g)
                copy_bank(a_hT[:], tiles(bank_a[0])).then_inc(a_hT_set, 1)

            def a_copy_zl(g):
                act.wait_ge(zl_ps, g + 1)
                if later(g):
                    act.wait_ge(gl_ps, g)
                copy_bank(zl[:], tiles(bank_a[1])).then_inc(zl_set, 1)

            def a_square_zl(g):
                act.wait_ge(zl_ps, g + 1)
                if later(g):
                    act.wait_ge(sql_ps, g)
                nc.scalar.activation(zl2[:], tiles(bank_a[1]), ACT.Square).then_inc(zl_sq, 1)

            def a_copy_zg(g):
                act.wait_ge(zg_ps, g + 1)
                if later(g):
                    act.wait_ge(gg_ps, g)
                copy_bank(zg[:], tiles(bank_a[2])).then_inc(zg_set, 1)

            def a_square_zg(g):
                act.wait_ge(zg_ps, g + 1)
                if later(g):
                    act.wait_ge(gg_ps, g)
                nc.scalar.activation(zg2[:], tiles(bank_a[2]), ACT.Square).then_inc(zg_sq, 1)

            def a_copy_values(g):
                act.wait_ge(v_ps, g + 1)
                if later(g):
                    act.wait_ge(outg_ps1, g)
                nc.scalar.activation(v_g[:, :, 0:D], tiles(bank_a[0]), ACT.Copy, scale=T_WAKE).then_inc(vg_set, 1)

            def a_exp(g):
                act.wait_ge(arg_g_set, g + 1)
                if later(g):
                    act.wait_ge(outg_ps1, g)
                nc.scalar.activation(adj_g[:], arg_g[:], ACT.Exp).then_inc(adj_g_set, 1)

            def b_copy_hT(g):
                act.wait_ge(b_hT_ps, g + 1)
                if later(g):
                    act.wait_ge(qkv_ps1, g)
                copy_bank(b_hT[:], tiles(bank_b[0])).then_inc(b_hT_set, 1)

            def b_copy_qkv(g, half):
                qkv = tiles(bank_b[1 - half], 2)
                t = slice(2 * half, 2 * half + 2)
                act.wait_ge([qkv_ps0, qkv_ps1][half], g + 1)
                if later(g):
                    act.wait_ge(rope_s_set, g * 2 - 1 + half)
                    act.wait_ge(y_ps, g)
                src = qkv[:, :, 0:QK].rearrange("p t (h two e) -> p t h two e", two=2, e=HD // 2)
                dst = swapped[:, t, :].rearrange("p t (h two e) -> p t h two e", two=2, e=HD // 2)
                for part in range(2):
                    copy_bank(dst[:, :, :, part, :], src[:, :, :, 1 - part, :])
                copy_bank(v_attn[:, t, :, :], qkv[:, :, QK:QKV].rearrange("p t (k d) -> p t k d", k=NKV)).then_inc(
                    [swap_set0, swap_set1][half], 1)

            def b_copy_q(g):
                act.wait_ge(qT_ps, g + 1)
                if later(g):
                    act.wait_ge(s_ps, g * NH)
                copy_bank(qT[:], tiles(bank_b[1])).then_inc(qT_set, 1)

            def b_copy_k(g):
                act.wait_ge(kT_ps, g + 1)
                if later(g):
                    act.wait_ge(s_ps, g * NH)
                for r in range(NREP):
                    last = copy_bank(kT[r * NKV * HD:(r + 1) * NKV * HD, :, :], tiles(bank_b[0])[0:NKV * HD, :, :])
                last.then_inc(kT_set, 1)

            def b_exp(g, h):
                act.wait_ge(min_set, g * NH + h + 1)
                if later(g):
                    act.wait_ge(pT_ps, g * NH - NH + h + 1)
                    act.wait_ge(sum_rec_set, g)
                act.nop(nofuse=True)
                for t in range(G):
                    last = nc.scalar.activation(probs[:, h, t, :], tiles(bank_b[1 - h % 2])[:, t, :], ACT.Exp,
                                                bias=row_min[:, h, t:t + 1], scale=-1.0, accum_out=sums[:, h, t:t + 1])
                last.then_inc(prob_set, 1)

            def c_spread_rec(g):
                act.wait_ge(sum_rec_set, g + 1)
                if later(g):
                    act.wait_ge(recT_ps, g)
                copy_bank(rec_rows[:], sum_rec[:].rearrange("p h t -> p t h").unsqueeze(3).broadcast_to(
                    [P, G, NH, HD])).then_inc(rec_rows_set, 1)

            def c_copy_rec(g):
                act.wait_ge(recT_ps, g + 1)
                if later(g):
                    act.wait_ge(yT_set, g)
                copy_bank(rec_t[:], tiles(bank_c[1])).then_inc(recT_set, 1)

            def c_copy_probs(g, h):
                act.wait_ge(pT_ps, g * NH + h + 1)
                if later(g):
                    act.wait_ge(y_ps, g)
                copy_bank(probs_t[:, h, :, :], tiles(bank_c[h % 2])).then_inc(pT_set, 1)

            def c_square(g):
                act.wait_ge(xf_set, g + 1)
                if later(g):
                    act.wait_ge(ms_set, g)
                for t in range(G):
                    last = nc.scalar.activation(sq_junk[:, t, :], xf[:, t, :], ACT.Square, accum_out=sum_sq[:, t:t + 1])
                last.then_inc(sq_set, 1)

            def c_copy_flatT(g):
                act.wait_ge(flat_ps, g + 1)
                if later(g):
                    act.wait_ge(router_ps, g)
                copy_bank(flatT[:], tiles(bank_d)).then_inc(flatT_set, 1)

            def c_weights(g):
                act.wait_ge(below_set, g + 1)
                if later(g):
                    act.wait_ge(gates_set, g)
                nc.scalar.activation(weight[:], below[:], ACT.Exp).then_inc(weight_set, 1)

            def step(k):
                at(k - 2, b_copy_q)
                at(k - 1, a_exp)
                at(k - 2, b_copy_k)
                at(k - 3, c_square)
                at(k - 2, b_exp, 0)
                at(k - 2, b_exp, 1)
                at(k, a_copy_hT)
                at(k - 2, b_exp, 2)
                at(k - 2, c_copy_probs, 0)
                at(k - 2, c_copy_probs, 1)
                at(k, a_square_zg)
                at(k - 3, c_copy_flatT)
                at(k - 2, b_exp, 3)
                at(k, a_copy_zg)
                at(k, a_square_zl)
                at(k - 1, b_copy_hT)
                at(k - 2, c_copy_probs, 2)
                at(k - 3, c_weights)
                at(k - 2, c_copy_probs, 3)
                at(k - 2, c_spread_rec)
                at(k, a_copy_zl)
                at(k - 1, b_copy_qkv, 0)
                at(k - 1, b_copy_qkv, 1)
                at(k, a_copy_values)
                at(k - 2, c_copy_rec)

            for k in range(LAG + 1):
                step(k)
            with act.Fori(LAG + 1, NG) as k:
                step(k)
            for k in range(NG, NG + LAG):
                step(k)

            def expert_pair(pair_no):
                for u in range(2):
                    j = pair_no * 2 + u
                    act.wait_ge(inT_ps, j + 1)
                    if later(pair_no):
                        act.wait_ge(gate_ps, j * NC - NC)
                    copy_bank(in_t[:, u, :], bank_in[:]).then_inc(inT_set, 1)
                    for c, (_, n) in enumerate(CHUNKS):
                        m = u * NC + c
                        act.wait_ge(up_ps, j * NC + c + 1)
                        if later(pair_no) or m >= 2:
                            act.wait_ge(hidden_set, j * NC + c - 1)
                        nc.scalar.activation(silu[0:n, m % 2, :], bank_up[m % 2][0:n, :], ACT.Silu).then_inc(silu_set, 1)

            expert_pair(0)
            with act.Fori(1, N_TILES // 2) as k:
                expert_pair(k)

            for i in range(NB // FINAL):
                act.wait_ge(sum_set, i + 1)
                act.dma_start(out[:, i * FINAL:(i + 1) * FINAL, :], resid[:, i * FINAL:(i + 1) * FINAL, :]).then_inc(
                    out_stored, 16)
            act.wait_ge(out_stored, NB // FINAL * 16)

        @block.tensor
        def _(pe):
            pe.wait_ge(w_loaded, W_LOADED)
            nc.tensor.matmul(bank_a[0][:, 0:D], w_v_t[:], w_o_gnn[:], start=True, stop=True).then_inc(wvo_ps, 1)
            pe.wait_ge(const_loaded, 16)
            pe.wait_ge(consts_set, 1)
            pe.wait_ge(ones_set, 1)
            pe.wait_ge(w_qkv_set, 1)
            pe.wait_ge(wvo_set, 1)

            def transposes(bank, srcs):
                for t, src in enumerate(srcs):
                    last = nc.tensor.transpose(bank[:, t * P:(t + 1) * P], src, ident)
                return last

            def a_transpose(g):
                pe.wait_ge(a_norm, g + 1)
                if later(g):
                    pe.wait_ge(x1_set, g)
                transposes(bank_a[0], [a_h[:, t, :] for t in range(G)]).then_inc(a_hT_ps, 1)

            def a_project(g):
                pe.wait_ge(a_hT_set, g + 1)
                if later(g):
                    pe.wait_ge(xl_set1, g)
                hT = a_hT[:].rearrange("p t d -> p (t d)")
                nc.tensor.matmul(bank_a[1][:], w_l[:], hT, start=True, stop=True).then_inc(zl_ps, 1)
                if later(g):
                    pe.wait_ge(x1_half, g)
                nc.tensor.matmul(bank_a[2][:], w_g[:], hT, start=True, stop=True).then_inc(zg_ps, 1)

            def a_project_v(g):
                pe.wait_ge(a_hT_set, g + 1)
                for t in range(G):
                    last = nc.tensor.matmul(bank_a[0][:, t * P:(t + 1) * P], a_hT[:, t, :], w_vo[:], start=True, stop=True)
                last.then_inc(v_ps, 1)

            def a_gram_l(g):
                pe.wait_ge(zl_set, g + 1)
                pe.wait_ge(zl_sq, g + 1)
                for t in range(G):
                    last = nc.tensor.matmul(bank_a[1][:, t * P:(t + 1) * P], zl[:, t, :], zl[:, t, :], start=True, stop=True)
                last.then_inc(gl_ps, 1)

            def a_norms(g):
                pe.wait_ge(zl_sq, g + 1)
                pe.wait_ge(zg_set, g + 1)
                pe.wait_ge(zg_sq, g + 1)
                for t in range(G):
                    last = nc.tensor.matmul(bank_a[2][:, t:t + 1], zl2[:, t, :], v_g[:, 0, D:D + 1], start=True, stop=True)
                last.then_inc(sql_ps, 1)

            def a_gram_g(g):
                pe.wait_ge(zg_sq, g + 1)
                pe.wait_ge(sql_set, g + 1)
                for t in range(G):
                    o = bank_a[2][:, t * P:(t + 1) * P]
                    nc.tensor.matmul(o, zg[:, t, :], zg[:, t, :], start=True, stop=False)
                    nc.tensor.matmul(o, minus_half[:], zg2[:, t, :], start=False, stop=False)
                    last = nc.tensor.matmul(o, zg2[:, t, :], minus_half[:], start=False, stop=True)
                last.then_inc(gg_ps, 1)

            def a_apply(g, kernel, values, banks, ready):
                for h in range(2):
                    for t in range(2):
                        last = nc.tensor.matmul(banks[h][:, t * (D + 1):(t + 1) * (D + 1)], kernel[:, 2 * h + t, :],
                                                values[:, 2 * h + t, :], start=True, stop=True)
                    last.then_inc(ready[h], 1)

            def a_apply_l(g):
                pe.wait_ge(adj_l_set, g + 1)
                pe.wait_ge(vl_set, g + 1)
                pe.wait_ge(vl_col_set, g + 1)
                a_apply(g, adj_l, v_l, [bank_a[0], bank_a[1]], [outl_ps0, outl_ps1])

            def a_apply_g(g, h):
                if h == 0:
                    pe.wait_ge(adj_g_set, g + 1)
                    pe.wait_ge(arg_g_set, g + 1)
                    pe.wait_ge(vg_set, g + 1)
                else:
                    pe.wait_ge(xl_set0, g + 1)
                for t in range(2):
                    last = nc.tensor.matmul(bank_a[2 - 2 * h][:, t * (D + 1):(t + 1) * (D + 1)], adj_g[:, 2 * h + t, :],
                                            v_g[:, 2 * h + t, :], start=True, stop=True)
                last.then_inc([outg_ps0, outg_ps1][h], 1)

            def b_transpose(g):
                pe.wait_ge(b_norm, g + 1)
                if later(g):
                    pe.wait_ge(prob_set, g * NH)
                transposes(bank_b[0], [b_h[:, t, :] for t in range(G)]).then_inc(b_hT_ps, 1)

            def b_project(g, half):
                pe.wait_ge(b_hT_set, g + 1)
                if half == 0 and later(g):
                    pe.wait_ge(prob_set, g * NH - 1)
                for t in range(2):
                    last = nc.tensor.matmul(bank_b[1 - half][:, t * QKV:(t + 1) * QKV], b_hT[:, 2 * half + t, :], w_qkv[:],
                                            start=True, stop=True)
                last.then_inc([qkv_ps0, qkv_ps1][half], 1)

            def b_transpose_q(g):
                pe.wait_ge(roped_set, g + 1)
                transposes(bank_b[1], [roped[:, t, 0:NH * HD] for t in range(G)]).then_inc(qT_ps, 1)

            def b_transpose_k(g):
                for t in range(G):
                    last = nc.tensor.transpose(bank_b[0][0:NKV * HD, t * P:(t + 1) * P], roped[:, t, NH * HD:QK], ident)
                last.then_inc(kT_ps, 1)

            def b_scores(g, h):
                bank = bank_b[1 - h % 2]
                if h == 0:
                    pe.wait_ge(qT_set, g + 1)
                    pe.wait_ge(kT_set, g + 1)
                if h >= 2:
                    pe.wait_ge(prob_set, g * NH + h - 1)
                nc.tensor.matmul(bank[:], ident_b[:], causal_b[:].unsqueeze(1).broadcast_to([P, G, P]), start=True, stop=False,
                                 skip_group_check=True)
                heads = slice(h * HD, (h + 1) * HD)
                for t in range(G):
                    last = nc.tensor.matmul(bank[:, t * P:(t + 1) * P], qT[heads, t, :], kT[heads, t, :], start=False, stop=True,
                                            skip_group_check=True)
                last.then_inc(s_ps, 1)

            def c_transpose_probs(g, h):
                pe.wait_ge(prob_set, g * NH + h + 1)
                if h >= 2:
                    pe.wait_ge(pT_set, g * NH + h - 1)
                elif later(g):
                    pe.wait_ge([yT_set, xf_set][h], g)
                transposes(bank_c[h % 2], [probs[:, h, t, :] for t in range(G)]).then_inc(pT_ps, 1)

            def c_transpose_rec(g):
                pe.wait_ge(rec_rows_set, g + 1)
                pe.wait_ge(pT_set, g * NH + NH)
                transposes(bank_c[1], [rec_rows[:, t, :, :].rearrange("p h d -> p (h d)") for t in range(G)]).then_inc(recT_ps, 1)

            def c_values(g):
                pe.wait_ge(pT_set, g * NH + NH)
                for t in range(G):
                    for h in range(NH):
                        last = nc.tensor.matmul(bank_c[0][h * HD:(h + 1) * HD, t * P:(t + 1) * P], v_attn[:, t, h % NKV, :],
                                                probs_t[:, h, t, :], start=True, stop=True)
                last.then_inc(y_ps, 1)

            def c_output(g):
                pe.wait_ge(yT_set, g + 1)
                for t in range(G):
                    last = nc.tensor.matmul(bank_c[1][:, t * P:(t + 1) * P], yT[:, t, :], w_o[:], start=True, stop=True)
                last.then_inc(attn_ps, 1)

            def c_transpose_flat(g):
                pe.wait_ge(flat_set, g + 1)
                if later(g):
                    pe.wait_ge(place_set, g)
                transposes(bank_d, [flat_rows[:, t, 0:D] for t in range(G)]).then_inc(flat_ps, 1)

            def c_router(g):
                pe.wait_ge(flatT_set, g + 1)
                for t in range(G):
                    last = nc.tensor.matmul(bank_d[:, t * NE:(t + 1) * NE], flatT[:, t, :], w_router[:], start=True, stop=True)
                last.then_inc(router_ps, 1)

            def c_rank(g):
                pe.wait_ge(chosen_set, g + 1)
                o = bank_d[:, RANKS:RANKS + (G + 1) * NE]
                last = nc.tensor.matmul(o[:, 0:G * NE], upper_b[:], chosen_b[:].rearrange("p t e -> p (t e)"), start=True,
                                        stop=False, skip_group_check=True)
                for t in range(G):
                    n = G - t
                    last = nc.tensor.matmul(o[:, (t + 1) * NE:(G + 1) * NE], ones_b[:],
                                            chosen_b[:, t:t + 1, :].broadcast_to([P, n, NE]), start=False, stop=t == G - 1,
                                            skip_group_check=True)
                last.then_inc(rank_ps, 1)

            def step(k):
                at(k - 1, a_gram_g)
                at(k - 2, b_transpose_q)
                at(k - 1, a_apply_l)
                at(k - 2, b_transpose_k)
                at(k - 3, c_output)
                at(k - 1, a_apply_g, 0)
                at(k - 2, b_scores, 0)
                at(k - 1, a_apply_g, 1)
                at(k - 2, b_scores, 1)
                at(k - 2, b_scores, 2)
                at(k - 2, c_transpose_probs, 0)
                at(k, a_transpose)
                at(k - 2, c_transpose_probs, 1)
                at(k - 2, b_scores, 3)
                at(k, a_project)
                at(k - 3, c_transpose_flat)
                at(k, a_project_v)
                at(k - 3, c_router)
                at(k - 2, c_transpose_probs, 2)
                at(k - 1, b_transpose)
                at(k - 2, c_transpose_probs, 3)
                at(k, a_norms)
                at(k - 3, c_rank)
                at(k - 1, b_project, 0)
                at(k - 2, c_values)
                at(k - 1, b_project, 1)
                at(k, a_gram_l)
                at(k - 2, c_transpose_rec)

            for k in range(LAG + 1):
                step(k)
            with pe.Fori(LAG + 1, NG) as k:
                step(k)
            for k in range(NG, NG + LAG):
                step(k)

            def turn_rows(pair_no, u):
                pe.wait_ge([rows_loaded0, rows_loaded1][u], pair_no * 16 + 16)
                if u or later(pair_no):
                    pe.wait_ge(inT_set, pair_no * 2 + u)
                for i in range(SUB):
                    last = nc.tensor.transpose(bank_in[:, i * P:(i + 1) * P], in_rows[:, u, i, 0:D], ident)
                last.then_inc(inT_ps, 1)

            def up_and_gate(pair_no, u):
                j = pair_no * 2 + u
                pe.wait_ge(inT_set, j + 1)
                pe.wait_ge([wbuf_loaded0, wbuf_loaded1][u], pair_no * 16 + 16)
                for c, (c0, n) in enumerate(CHUNKS):
                    m = u * NC + c
                    full = later(pair_no) or m >= 2
                    if full:
                        pe.wait_ge(silu_set, j * NC + c - 1)
                    nc.tensor.matmul(bank_up[m % 2][0:n, :], w_buf[:, u, c0:c0 + n], in_t[:, u, :], start=True,
                                     stop=True).then_inc(up_ps, 1)
                    if full:
                        pe.wait_ge(hidden_set, j * NC + c - 1)
                    nc.tensor.matmul(bank_gate[m % 2][0:n, :], w_buf[:, u, HID + c0:HID + c0 + n], in_t[:, u, :], start=True,
                                     stop=True).then_inc(gate_ps, 1)

            def down(pair_no, u):
                j = pair_no * 2 + u
                pe.wait_ge(hidden_set, j * NC + NC)
                if later(pair_no):
                    pe.wait_ge(outrows_set, j - 1)
                for i in range(SUB):
                    for c, (_, n) in enumerate(CHUNKS):
                        last = nc.tensor.matmul(bank_down[u][:, i * P:(i + 1) * P], hidden[0:n, u, c, i * P:(i + 1) * P],
                                                w_buf[0:n, u, 2 * HID + c * D:2 * HID + (c + 1) * D], start=c == 0, stop=c == NC - 1)
                last.then_inc(down_ps, 1)

            def expert_pair(pair_no, last_pair=False):
                up_and_gate(pair_no, 0)
                turn_rows(pair_no, 1)
                down(pair_no, 0)
                up_and_gate(pair_no, 1)
                if not last_pair:
                    turn_rows(pair_no + 1, 0)
                down(pair_no, 1)

            turn_rows(0, 0)
            expert_pair(0)
            with pe.Fori(1, N_TILES // 2 - 1) as k:
                expert_pair(k)
            expert_pair(N_TILES // 2 - 1, last_pair=True)


def kernel(**inputs):
    import numpy as _np
    import concourse.bacc as _bacc
    from concourse import mybir as _mybir
    from concourse.bass_utils import run_bass_kernel_spmd as _run

    nc = _bacc.Bacc("TRN2", target_bir_lowering=False, num_devices=1)
    f = {k: _np.asarray(v) for k, v in inputs.items()}
    wq = f["L0_ffn_wq"].reshape(NH, HD, D)[HEADS].reshape(NH * HD, D)
    wo = f["L0_ffn_wo"].reshape(D, NH, HD)[:, HEADS].reshape(D, NH * HD)
    laid = {
        "x": f["x"].transpose(1, 0, 2),
        "adj_t": _np.ascontiguousarray(f["adj"].T).view(_np.int32),
        "wl": f["L0_gnn_Wl"],
        "wg": f["L0_gnn_Wg"],
        "wv_t": f["L0_gnn_Wv"].T,
        "wo_gnn": f["L0_gnn_Wo"],
        "ln1": f["L0_ffn_ln1_w"].reshape(D, 1),
        "ln2": f["L0_ffn_ln2_w"],
        "wqkv_t": _np.concatenate([wq, f["L0_ffn_wk"], f["L0_ffn_wv"]], 0).T,
        "wo_t": wo.T,
        "router_t": f["L0_ffn_router_w"].T,
        "w1_t": f["L0_ffn_w1"].transpose(2, 0, 1),
        "w2_t": f["L0_ffn_w2"].transpose(2, 0, 1),
        "w3_t": f["L0_ffn_w3"].transpose(2, 0, 1),
        "table": constants(),
    }
    arrays, args = {}, []
    for name, a in laid.items():
        a = _np.ascontiguousarray(a)
        arrays[f"in_{name}"] = a
        args.append(nc.dram_tensor(f"in_{name}", a.shape, _mybir.dt.from_np(a.dtype), kind="ExternalInput").ap())
    args.append(nc.dram_tensor("out_0", (P, NB, D), _mybir.dt.float32, kind="ExternalOutput").ap())
    build(nc, *args)
    r = _run(nc, [arrays], core_ids=[0])
    return _np.ascontiguousarray(r.results[0]["out_0"].transpose(1, 0, 2))
```

```python
from contextlib import ExitStack

import numpy as np

import concourse.bass as bass
from concourse import mybir

ALU = mybir.AluOpType
ACT = mybir.ActivationFunctionType
F32 = mybir.dt.float32
F32R = mybir.dt.float32r
BF16 = mybir.dt.bfloat16
I32 = mybir.dt.int32
U32 = mybir.dt.uint32
U8 = mybir.dt.uint8
AX_X = mybir.AxisListType.X

P = 128
NB = 128
D = 128
G = 4
NG = NB // G
NH, NKV, HD = 4, 2, 32
NREP = NH // NKV
QK = (NH + NKV) * HD
QKV = QK + NKV * HD
NE, HID = 8, int(8 / 3 * D)
N_TOK = NB * P
HEADS = [k * NREP + r for r in range(NREP) for k in range(NKV)]
T_WAKE = 0.1
EPS = 1e-8
EPS_LN = 1e-5
EPS_RMS = 1e-6
NEG = -1e30
SCALE = float(HD) ** -0.5

ROWS = 512
SUB = ROWS // P
REGION = N_TOK + ROWS
ROW_W = D + 4
COL_ID, COL_EXPERT, COL_GATE = D, D + 1, D + 2
N_TILES = 2 * N_TOK // ROWS + NE
CHUNKS = [(c, min(P, HID - c)) for c in range(0, HID, P)]
NC = len(CHUNKS)
W_COLS = 2 * HID + NC * D
LAG = 4
RANKS = 64
FINAL = 16

C_IDENT, C_CAUSAL, C_UPPER, C_COS, C_SIN, C_TOKEN, C_BASE, C_IOTA, C_UPTO, C_STEP, C_TILE, C_PAD = np.cumsum(
    [0, P, P, P, QK, QK, G, NE, NE, NE * NE, N_TOK // ROWS, N_TILES]).tolist()
C_END = C_PAD + SUB


def constants():
    t = np.zeros((P, C_END), np.float32)
    i = np.arange(P)
    t[:, C_IDENT:C_CAUSAL] = np.eye(P)
    t[:, C_CAUSAL:C_UPPER] = np.where(i[None, :] <= i[:, None], 0.0, -NEG)
    t[:, C_UPPER:C_COS] = i[:, None] < i[None, :]
    inv_freq = 1.0 / 10000.0 ** (np.arange(0, HD, 2, dtype=np.float32) / HD)
    freqs = np.outer(i.astype(np.float32), inv_freq)
    cos = np.cos(np.concatenate([freqs, freqs], -1))
    sin = np.sin(np.concatenate([-freqs, freqs], -1))
    scale = np.repeat([-SCALE, 1.0], [NH * HD, NKV * HD])
    t[:, C_COS:C_SIN] = np.tile(cos, (1, NH + NKV)) * scale
    t[:, C_SIN:C_TOKEN] = np.tile(sin, (1, NH + NKV)) * scale
    t[:, C_TOKEN:C_BASE] = i[:, None] * NB + np.arange(G)[None, :]
    t[:, C_BASE:C_IOTA] = np.arange(NE) * REGION
    t[:, C_IOTA:C_UPTO] = np.arange(NE)
    t[:, C_UPTO:C_STEP] = np.tril(np.ones((NE, NE))).reshape(-1)
    t[:, C_STEP:C_TILE] = np.arange(N_TOK // ROWS) * ROWS
    t[:, C_TILE:C_PAD] = np.arange(N_TILES)
    t[:, C_PAD:C_END] = N_TOK + i[:, None] * SUB + np.arange(SUB)[None, :]
    return t


def later(g):
    return not isinstance(g, int) or g > 0


def at(g, work, *args):
    if not isinstance(g, int) or 0 <= g < NG:
        work(g, *args)


def build(nc, x, adj_t, wl, wg, wv_t, wo_gnn, ln1, ln2, wqkv_t, wo_t, router_t, w1_t, w2_t, w3_t, table, out):
    with ExitStack() as ctx:
        def sb(name, shape, dt=F32):
            return ctx.enter_context(nc.sbuf_tensor(name, shape, dt))

        def sem(name):
            return ctx.enter_context(nc.semaphore(name))

        bank_a = [ctx.enter_context(nc.psum_tensor(f"bank_a{i}", [P, 512], F32)) for i in range(3)]
        bank_b = [ctx.enter_context(nc.psum_tensor(f"bank_b{i}", [P, 512], F32)) for i in range(2)]
        bank_c = [ctx.enter_context(nc.psum_tensor(f"bank_c{i}", [P, 512], F32)) for i in range(2)]
        bank_d = ctx.enter_context(nc.psum_tensor("bank_d", [P, 512], F32))

        def tiles(bank, n=G):
            return bank[:].rearrange("p (t d) -> p t d", t=n)

        tab = sb("tab", [P, C_END])
        ident = tab[:, C_IDENT:C_CAUSAL]
        bank_in, bank_up, bank_gate, bank_down = bank_a[0], bank_a[1:3], bank_b, bank_c
        ident_b = sb("ident_b", [P, P], BF16)
        causal_b = sb("causal_b", [P, P], BF16)
        upper_b = sb("upper_b", [P, P], BF16)
        ones_b = sb("ones_b", [P, P], BF16)
        minus_half = sb("minus_half", [P, P])
        adj_bytes = sb("adj_bytes", [P, P // 4], I32)
        adj_f = sb("adj_f", [P, P])
        mask_l = sb("mask_l", [P, P])
        mask_g = sb("mask_g", [P, P])
        w_l = sb("w_l", [P, D])
        w_g = sb("w_g", [P, D])
        w_v_t = sb("w_v_t", [P, D])
        w_o_gnn = sb("w_o_gnn", [P, D])
        w_vo = sb("w_vo", [P, D])
        ln1_col = sb("ln1_col", [P, 1])
        ln2_row = sb("ln2_row", [P, D])
        w_qkv_raw = sb("w_qkv_raw", [P, QKV])
        w_qkv = sb("w_qkv", [P, QKV])
        w_o = sb("w_o", [P, D])
        w_router = sb("w_router", [P, NE])

        resid = sb("resid", [P, NB, D])

        w_all = sb("w_all", [P, NE, W_COLS])
        w13 = sb("w13", [P, 2, 2 * HID])
        w2 = sb("w2", [P, 2, NC * D])
        in_rows = sb("in_rows", [P, 2, SUB, ROW_W])
        pad_rows = sb("pad_rows", [P, SUB, ROW_W])
        filled = sb("filled", [P, NE])
        region_end_i = sb("region_end_i", [P, NE], I32)

        lasting, ctx = ctx, ExitStack()

        a_st = sb("a_st", [P, G, 6])
        a_mv = sb("a_mv", [P, G, 2])
        a_var = sb("a_var", [P, G])
        a_rstd = sb("a_rstd", [P, G])
        a_h = sb("a_h", [P, G, D])
        a_hT = sb("a_hT", [P, G, P])
        zl = sb("zl", [P, G, P])
        zg = sb("zg", [P, G, P])
        zl2 = sb("zl2", [P, G, P])
        zg2 = sb("zg2", [P, G, P])
        sq_l = sb("sq_l", [P, G])
        inv_norm = sb("inv_norm", [P, G])
        guard = sb("guard", [P, G])
        v_l = sb("v_l", [P, G, D + 1])
        v_g = sb("v_g", [P, G, D + 1])
        adj_l = sb("adj_l", [P, G, P])
        arg_g = sb("arg_g", [P, G, P])
        adj_g = sb("adj_g", [P, G, P])
        den_l = sb("den_l", [P, G])
        den_g = sb("den_g", [P, G])
        rec_l = sb("rec_l", [P, G])
        rec_g = sb("rec_g", [P, G])

        b_st = sb("b_st", [P, G, 6])
        b_mv = sb("b_mv", [P, G, 2])
        b_var = sb("b_var", [P, 2, G])
        b_rs = sb("b_rs", [P, 2, G])
        b_rec = sb("b_rec", [P, G])
        b_ratio = sb("b_ratio", [P, G])
        b_h = sb("b_h", [P, G, D])
        h2 = sb("h2", [P, G, D])
        b_hT = sb("b_hT", [P, G, P])
        rope_c = sb("rope_c", [P, G, QK])
        swapped = sb("swapped", [P, G, QK])
        rope_s = sb("rope_s", [P, G, QK])
        roped = sb("roped", [P, G, QK])
        v_attn = sb("v_attn", [P, G, NKV, HD])
        qT = sb("qT", [P, G, P])
        kT = sb("kT", [P, G, P])
        row_min = sb("row_min", [P, NH, G])
        sums = sb("sums", [P, NH, G])
        probs = sb("probs", [P, NH, G, P])

        probs_t = sb("probs_t", [P, NH, G, P])
        sum_rec = sb("sum_rec", [P, NH, G])
        rec_rows = sb("rec_rows", [P, G, NH, HD])
        rec_t = sb("rec_t", [P, G, P])
        yT = sb("yT", [P, G, P])
        xf = sb("xf", [P, G, D])
        sq_junk = sb("sq_junk", [P, G, D], BF16)
        sum_sq = sb("sum_sq", [P, G])
        ms = sb("ms", [P, G])
        rms = sb("rms", [P, G])
        half_col = sb("half_col", [P, 2 * G])

        flat_rows = sb("flat_rows", [P, G, ROW_W])
        flatT = sb("flatT", [P, G, P])
        token_id = sb("token_id", [P, G])
        best = sb("best", [P, G, NE])
        best_at = sb("best_at", [P, G, NE], U32)
        choice = sb("choice", [P, G * 2])
        pick = sb("pick", [P, G, 2, NE])
        chosen_b = sb("chosen_b", [P, G, NE], BF16)
        below = sb("below", [P, G, NE])
        weight = sb("weight", [P, G, NE])
        total = sb("total", [P, G])
        pair = sb("pair", [P, G])
        denom = sb("denom", [P, G])
        denom_rec = sb("denom_rec", [P, G])
        place = sb("place", [P, G + 1, NE])
        picked = sb("picked", [P, G, 2, NE])
        place_f = sb("place_f", [P, G * 2])
        place_i = sb("place_i", [P, G * 2], I32)

        ctx.close()
        ctx = lasting
        counts = sb("counts", [P, NE])
        over = sb("over", [P, NE, N_TOK // ROWS])
        n_tiles = sb("n_tiles", [P, NE])
        upto = sb("upto", [P, NE, NE])
        tiles_upto = sb("tiles_upto", [P, NE])
        passed = sb("passed", [P, N_TILES, NE])
        passed_n = sb("passed_n", [P, N_TILES, NE])
        tile_expert = sb("tile_expert", [P, N_TILES])
        tile_first = sb("tile_first", [P, N_TILES])
        tile_at = sb("tile_at", [P, N_TILES])
        tile_row = sb("tile_row", [P, N_TILES])
        tile_row_i = sb("tile_row_i", [P, N_TILES], I32)
        tile_weights_i = sb("tile_weights_i", [P, N_TILES], I32)
        in_hi = sb("in_hi", [P, 2, ROWS], F32R)
        in_lo = sb("in_lo", [P, 2, ROWS], F32R)
        w_hi = sb("w_hi", [P, 2, 2 * HID], F32R)
        w_lo = sb("w_lo", [P, 2, 2 * HID], F32R)
        silu = sb("silu", [P, 2, ROWS])
        hidden = sb("hidden", [P, 2, NC, ROWS])
        second = sb("second", [P, 2, SUB])
        gate_diff = sb("gate_diff", [P, 2, SUB])
        gate_step = sb("gate_step", [P, 2, SUB])
        gate = sb("gate", [P, 2, SUB])
        dest_f = sb("dest_f", [P, 2, SUB])
        dest_i = sb("dest_i", [P, 2, SUB], I32)
        out_rows = sb("out_rows", [P, 2, SUB, D])
        final_in = sb("final_in", [P, 2, 2, FINAL, D])

        grouped = nc.dram_tensor("grouped", (NE * REGION + ROWS, ROW_W), F32, kind="Internal").ap()
        expert_out = nc.dram_tensor("expert_out", (2 * N_TOK + ROWS, D), F32, kind="Internal").ap()

        def sems(names):
            return [sem(name) for name in names.split()]

        const_loaded, adj_loaded, w_loaded, consts_set, adj_set, mask_set, w_qkv_set, wvo_ps = sems(
            "const_loaded adj_loaded w_loaded consts_set adj_set mask_set w_qkv_set wvo_ps")
        wvo_set, ones_set = sems("wvo_set ones_set")
        x_loaded = sem("x_loaded")
        a_stats, a_aggr, a_var_set, a_rstd_set, a_norm, a_hT_ps, a_hT_set, zl_ps = sems(
            "a_stats a_aggr a_var_set a_rstd_set a_norm a_hT_ps a_hT_set zl_ps")
        zg_ps, zl_set, zg_set, zl_sq, zg_sq = sems("zg_ps zl_set zg_set zl_sq zg_sq")
        sql_ps, sql_set, inv_set, guard_set, v_ps, vg_set, vl_set, vl_col_set = sems(
            "sql_ps sql_set inv_set guard_set v_ps vg_set vl_set vl_col_set")
        gl_ps, adj_l_set, gg_ps, arg_g_set, adj_g_set = sems("gl_ps adj_l_set gg_ps arg_g_set adj_g_set")
        outl_ps0, outl_ps1, outg_ps0, outg_ps1, denl_set, recl_set, xl_set0, xl_set1 = sems(
            "outl_ps0 outl_ps1 outg_ps0 outg_ps1 denl_set recl_set xl_set0 xl_set1")
        deng_set, recg_set, x1_half, x1_set = sems("deng_set recg_set x1_half x1_set")
        b_stats, b_aggr, b_var_set, b_rs_set, b_rec_set, b_ratio_set, b_norm, h2_set = sems(
            "b_stats b_aggr b_var_set b_rs_set b_rec_set b_ratio_set b_norm h2_set")
        b_hT_ps, b_hT_set, qkv_ps0, qkv_ps1 = sems("b_hT_ps b_hT_set qkv_ps0 qkv_ps1")
        swap_set0, swap_set1, v1_set, rope_c_set, rope_s_set, roped_set, qT_ps, kT_ps = sems(
            "swap_set0 swap_set1 v1_set rope_c_set rope_s_set roped_set qT_ps kT_ps")
        qT_set, kT_set = sems("qT_set kT_set")
        s_ps, min_set = sems("s_ps min_set")
        prob_set = sem("prob_set")
        pT_ps, pT_set, y_ps, sum_rec_set, rec_rows_set, recT_ps, recT_set = sems("pT_ps pT_set y_ps sum_rec_set rec_rows_set recT_ps recT_set")
        yT_set = sem("yT_set")
        attn_ps, xf_set, sq_set, ms_set, rms_set, resid_set, out_stored = sems(
            "attn_ps xf_set sq_set ms_set rms_set resid_set out_stored")
        flat_set, id_set, id_next, flat_ps, flatT_set, router_ps, best_set, best_at_set = sems(
            "flat_set id_set id_next flat_ps flatT_set router_ps best_set best_at_set")
        choice_set, expert_set, pick_set, chosen_set = sems("choice_set expert_set pick_set chosen_set")
        rank_ps, below_set, weight_set, total_set, pair_set, denom_set, denom_rec_set, gates_set = sems(
            "rank_ps below_set weight_set total_set pair_set denom_set denom_rec_set gates_set")
        place_set, filled_set, picked_set = sems("place_set filled_set picked_set")
        place_f_set, place_i_set, scattered = sems("place_f_set place_i_set scattered")
        wall_loaded, pad_zero, pad_set, pad_stored, table_step, table_set = sems(
            "wall_loaded pad_zero pad_set pad_stored table_step table_set")
        w13_loaded0, w13_loaded1, rows_loaded0, rows_loaded1, inT_ps, in_hi_set, up_ps, gate_ps = sems(
            "w13_loaded0 w13_loaded1 rows_loaded0 rows_loaded1 inT_ps in_hi_set up_ps gate_ps")
        silu_set, hidden_set, down_ps = sems("silu_set hidden_set down_ps")
        second_set, gdiff_set, gstep_set, gate_set, destf_set, dest_set, outrows_set, placed0 = sems(
            "second_set gdiff_set gstep_set gate_set destf_set dest_set outrows_set placed0")
        placed1, in_lo_set, w_hi_set, w_lo_set, w2_loaded0, w2_loaded1 = sems(
            "placed1 in_lo_set w_hi_set w_lo_set w2_loaded0 w2_loaded1")
        final_loaded0, final_loaded1, sum_half, sum_set = sems("final_loaded0 final_loaded1 sum_half sum_set")

        block = ctx.enter_context(nc.Block())

        @block.sync
        def _(sp):
            sp.dma_start(tab[:], table).then_inc(const_loaded, 16)
            sp.dma_start(adj_bytes[:], adj_t).then_inc(adj_loaded, 16)
            for dst, src in ((w_l, wl), (w_g, wg), (w_v_t, wv_t), (w_o_gnn, wo_gnn), (ln1_col, ln1), (w_qkv_raw, wqkv_t),
                             (w_o, wo_t), (w_router, router_t)):
                sp.dma_start(dst[:], src).then_inc(w_loaded, 16)
            sp.dma_start(ln2_row[:], ln2.partition_broadcast(P)).then_inc(w_loaded, 16)
            sp.dma_start(resid[:, 0:G, :], x[:, 0:G, :]).then_inc(x_loaded, 16)
            with sp.Fori(1, NG) as g:
                sp.wait_ge(x_loaded, g * 16)
                sp.dma_start(resid[:, bass.ds(g * G, G), :], x[:, bass.ds(g * G, G), :]).then_inc(x_loaded, 16)
            sp.wait_ge(ones_set, 1)
            sp.dma_start(w_all[:, :, 0:HID], w1_t).then_inc(wall_loaded, 16)
            sp.dma_start(w_all[:, :, HID:2 * HID], w3_t).then_inc(wall_loaded, 16)
            for c, (c0, cn) in enumerate(CHUNKS):
                w2_at = 2 * HID + c * D
                sp.dma_start(w_all[0:cn, :, w2_at:w2_at + D], w2_t[c0:c0 + cn]).then_inc(wall_loaded, 16)
            pads = grouped.rearrange("n w -> n w")
            sp.wait_ge(pad_set, 1)
            sp.dma_start(pads[NE * REGION:NE * REGION + ROWS].rearrange("(p i) w -> p i w", i=SUB), pad_rows[:]).then_inc(
                pad_stored, 16)
            sp.wait_ge(table_set, 1)
            for e in range(NE):
                end = sp.value_load(region_end_i[0:1, e:e + 1], min_val=0, max_val=NE * REGION - ROWS)
                sp.dma_start(pads[bass.ds(end, ROWS)].rearrange("(p i) w -> p i w", i=SUB), pad_rows[:]).then_inc(pad_stored, 16)
            sp.wait_ge(scattered, NG * G * 2 * 16)
            sp.wait_ge(pad_stored, (NE + 1) * 16)
            sp.wait_ge(wall_loaded, (2 + NC) * 16)

            def expert_of(j):
                return sp.value_load(tile_weights_i[0:1, bass.ds(j, 1)], min_val=0, max_val=NE - 1)

            def load_w13(pair_no, u):
                j = pair_no * 2 + u
                e = expert_of(j)
                if later(pair_no):
                    sp.wait_ge(w_lo_set, j - 1)
                sp.dma_start(w13[:, u, :], w_all[:, bass.ds(e, 1), 0:2 * HID].rearrange("p a w -> p (a w)")).then_inc(
                    [w13_loaded0, w13_loaded1][u], 16)

            def load_w2(pair_no, u):
                j = pair_no * 2 + u
                e = expert_of(j)
                if later(pair_no):
                    sp.wait_ge(down_ps, j - 1)
                sp.dma_start(w2[:, u, :], w_all[:, bass.ds(e, 1), 2 * HID:].rearrange("p a w -> p (a w)")).then_inc(
                    [w2_loaded0, w2_loaded1][u], 16)

            def load_rows(pair_no, u):
                j = pair_no * 2 + u
                row = sp.value_load(tile_row_i[0:1, bass.ds(j, 1)], min_val=0, max_val=NE * REGION)
                if later(pair_no):
                    sp.wait_ge(inT_ps, j - 1)
                    sp.wait_ge(gate_set, j - 1)
                    sp.wait_ge(destf_set, j - 1)
                    sp.wait_ge(gdiff_set, j - 1)
                sp.dma_start(in_rows[:, u, :, :], grouped[bass.ds(row, ROWS)].rearrange("(p i) w -> p i w", i=SUB)).then_inc(
                    [rows_loaded0, rows_loaded1][u], 16)

            def load_pair(pair_no, last_pair=False):
                load_w13(pair_no, 1)
                load_w2(pair_no, 0)
                load_rows(pair_no, 1)
                if not last_pair:
                    load_w13(pair_no + 1, 0)
                load_w2(pair_no, 1)
                if not last_pair:
                    load_rows(pair_no + 1, 0)

            load_w13(0, 0)
            load_rows(0, 0)
            load_pair(0)
            with sp.Fori(1, N_TILES // 2 - 1) as k:
                load_pair(k)
            load_pair(N_TILES // 2 - 1, last_pair=True)

            sp.wait_ge(resid_set, NG)
            sp.wait_ge(placed0, N_TILES // 2 * SUB * 16)
            sp.wait_ge(placed1, N_TILES // 2 * SUB * 16)
            halves = [expert_out[i * N_TOK:(i + 1) * N_TOK].rearrange("(p b) d -> p b d", b=NB) for i in range(2)]
            for i in range(NB // FINAL):
                if i >= 2:
                    sp.wait_ge(sum_set, i - 1)
                for n in range(2):
                    sp.dma_start(final_in[:, i % 2, n, :, :], halves[n][:, i * FINAL:(i + 1) * FINAL, :]).then_inc(
                        [final_loaded0, final_loaded1][i % 2], 16)

        W_LOADED = 16 * 9

        @block.gpsimd
        def _(pool):
            nc.gpsimd.memset(half_col[:], -0.5)
            nc.gpsimd.memset(minus_half[:], -0.5)
            nc.gpsimd.memset(v_g[:], 1.0)
            nc.gpsimd.memset(w_all[:, :, 2 * HID + (NC - 1) * D:], 0.0)
            nc.gpsimd.memset(ones_b[:], 1.0).then_inc(ones_set, 1)
            nc.gpsimd.memset(pad_rows[:], 0.0).then_inc(pad_zero, 1)
            pool.wait_ge(adj_set, 1)
            nc.gpsimd.affine_select(out=mask_l[:], in_=adj_f[:], compare_op=ALU.not_equal, fill=0.0, base=0,
                                    pattern=[[-1, P]], channel_multiplier=1).then_inc(mask_set, 1)
            pool.wait_ge(mask_set, 1)
            nc.gpsimd.tensor_scalar(mask_g[:], mask_l[:], 1.0, -NEG, ALU.subtract, ALU.mult).then_inc(mask_set, 1)

            def a_rstd_pow(g):
                pool.wait_ge(a_var_set, g + 1)
                if later(g):
                    pool.wait_ge(a_norm, g)
                nc.gpsimd.tensor_tensor(a_rstd[:], a_var[:], half_col[:, 0:G], ALU.pow).then_inc(a_rstd_set, 1)

            def a_inverse_norms(g):
                pool.wait_ge(sql_set, g + 1)
                if later(g):
                    pool.wait_ge(vl_set, g)
                nc.gpsimd.tensor_tensor(inv_norm[:], sq_l[:], half_col[:, 0:G], ALU.pow).then_inc(inv_set, 1)
                pool.wait_ge(inv_set, g + 1)
                if later(g):
                    pool.wait_ge(denl_set, g)
                nc.gpsimd.tensor_tensor(guard[:], sq_l[:], inv_norm[:], ALU.mult).then_inc(guard_set, 1)
                if later(g):
                    pool.wait_ge(outl_ps1, g)
                pool.nop(nofuse=True)
                nc.gpsimd.tensor_copy(v_l[:, :, D], inv_norm[:]).then_inc(vl_col_set, 1)

            def b_pow(g):
                pool.wait_ge(b_var_set, g + 1)
                if later(g):
                    pool.wait_ge(b_ratio_set, g)
                nc.gpsimd.tensor_tensor(b_rs[:].rearrange("p a b -> p (a b)"), b_var[:].rearrange("p a b -> p (a b)"),
                                        half_col[:], ALU.pow).then_inc(b_rs_set, 1)

            def b_h2(g):
                pool.wait_ge(b_rec_set, g + 1)
                nc.gpsimd.tensor_tensor(b_ratio[:], b_rs[:, 0, :], b_rec[:], ALU.mult).then_inc(b_ratio_set, 1)
                pool.wait_ge(b_ratio_set, g + 1)
                pool.wait_ge(b_norm, g + 1)
                if later(g):
                    pool.wait_ge(xf_set, g)
                nc.gpsimd.tensor_tensor(h2[:], b_h[:], b_ratio[:].unsqueeze(2).broadcast_to([P, G, D]),
                                        ALU.mult).then_inc(h2_set, 1)

            def b_rope_sin(g, half):
                pool.wait_ge([swap_set0, swap_set1][half], g + 1)
                if later(g):
                    pool.wait_ge(roped_set, g)
                t = slice(2 * half, 2 * half + 2)
                sin = tab[:, C_SIN:C_TOKEN].unsqueeze(1).broadcast_to([P, 2, QK])
                nc.gpsimd.tensor_tensor(rope_s[:, t, :], swapped[:, t, :], sin, ALU.mult).then_inc(rope_s_set, 1)

            def c_rms_pow(g):
                pool.wait_ge(ms_set, g + 1)
                if later(g):
                    pool.wait_ge(flat_set, g)
                nc.gpsimd.tensor_tensor(rms[:], ms[:], half_col[:, 0:G], ALU.pow).then_inc(rms_set, 1)

            def c_scatter(g, i):
                if i == 0:
                    pool.wait_ge(flat_set, g + 1)
                    pool.wait_ge(id_set, g + 1)
                    pool.wait_ge(expert_set, g + 1)
                    pool.wait_ge(gates_set, g + 1)
                    pool.wait_ge(place_i_set, g + 1)
                    pool.nop(nofuse=True)
                nc.gpsimd.indirect_dma_start(
                    out=grouped, out_offset=bass.IndirectOffsetOnAxis(ap=place_i[:, i:i + 1].bitcast(U32), axis=0),
                    in_=flat_rows[:, i // 2, :], in_offset=None).then_inc(scattered, 16)

            def c_resid(g):
                pool.wait_ge(xf_set, g + 1)
                pool.nop(nofuse=True)
                rg = resid[:, bass.ds(g * G, G), :]
                nc.gpsimd.tensor_tensor(rg, xf[:], rg, ALU.add).then_inc(resid_set, 1)

            def step(k):
                at(k, a_rstd_pow)
                at(k - 4, c_resid)
                at(k - 2, b_rope_sin, 0)
                at(k - 2, b_rope_sin, 1)
                at(k - 1, a_inverse_norms)
                at(k - 4, c_scatter, 0)
                at(k - 4, c_scatter, 1)
                at(k - 4, c_scatter, 2)
                at(k - 4, c_scatter, 3)
                at(k - 4, c_scatter, 4)
                at(k - 4, c_scatter, 5)
                at(k - 4, c_scatter, 6)
                at(k - 4, c_scatter, 7)
                at(k - 2, b_h2)
                at(k - 3, c_rms_pow)
                at(k - 1, b_pow)

            for k in range(LAG + 1):
                step(k)
            with pool.Fori(LAG + 1, NG) as k:
                step(k)
            for k in range(NG, NG + LAG):
                step(k)

            def place_tile(pair_no, u):
                j = pair_no * 2 + u
                pool.wait_ge(dest_set, j + 1)
                pool.wait_ge(outrows_set, j + 1)
                if u == 1:
                    pool.wait_ge(placed0, pair_no * (SUB * 16) + SUB * 16)
                elif later(pair_no):
                    pool.wait_ge(placed1, pair_no * (SUB * 16))
                pool.nop(nofuse=True)
                for i in range(SUB):
                    nc.gpsimd.indirect_dma_start(
                        out=expert_out, out_offset=bass.IndirectOffsetOnAxis(ap=dest_i[:, u, i:i + 1].bitcast(U32), axis=0),
                        in_=out_rows[:, u, i, :], in_offset=None).then_inc([placed0, placed1][u], 16)

            place_tile(0, 0)
            place_tile(0, 1)
            with pool.Fori(1, N_TILES // 2) as k:
                place_tile(k, 0)
                place_tile(k, 1)

        @block.vector
        def _(dve):
            dve.wait_ge(const_loaded, 16)
            nc.vector.tensor_copy(ident_b[:], ident)
            nc.vector.tensor_copy(causal_b[:], tab[:, C_CAUSAL:C_UPPER])
            nc.vector.tensor_copy(upper_b[:], tab[:, C_UPPER:C_COS]).then_inc(consts_set, 1)
            dve.wait_ge(adj_loaded, 16)
            nc.vector.tensor_copy(adj_f[:], adj_bytes[:].bitcast(U8)).then_inc(adj_set, 1)
            dve.wait_ge(w_loaded, W_LOADED)
            nc.vector.tensor_scalar(w_qkv[:], w_qkv_raw[:], ln1_col[:, 0:1], None, ALU.mult).then_inc(w_qkv_set, 1)
            dve.wait_ge(wvo_ps, 1)
            nc.vector.tensor_copy(w_vo[:], bank_a[0][:, 0:D]).then_inc(wvo_set, 1)
            nc.vector.tensor_copy(token_id[:], tab[:, C_TOKEN:C_BASE]).then_inc(id_next, 1)
            nc.vector.tensor_copy(filled[:], tab[:, C_BASE:C_IOTA]).then_inc(filled_set, 1)
            dve.wait_ge(pad_zero, 1)
            nc.vector.tensor_copy(pad_rows[:, :, COL_ID], tab[:, C_PAD:C_END])
            nc.vector.memset(pad_rows[:, :, COL_EXPERT], -1.0).then_inc(pad_set, 1)
            dve.wait_ge(mask_set, 2)

            def a_statistics(g):
                dve.wait_ge(x_loaded, g * 16 + 16)
                dve.nop(nofuse=True)
                for t in range(G):
                    last = nc.vector.bn_stats(a_st[:, t, :], resid[:, bass.ds(g * G + t, 1), :].rearrange("p a d -> p (a d)"))
                last.then_inc(a_stats, 1)
                dve.wait_ge(a_stats, g + 1)
                dve.nop(nofuse=True)
                for t in range(G):
                    last = nc.vector.bn_aggr(a_mv[:, t, :], a_st[:, t, :])
                last.then_inc(a_aggr, 1)
                dve.wait_ge(a_aggr, g + 1)
                nc.vector.tensor_scalar(a_var[:], a_mv[:, :, 1], EPS_LN, None, ALU.add).then_inc(a_var_set, 1)

            def a_normalise(g):
                dve.wait_ge(a_rstd_set, g + 1)
                if later(g):
                    dve.wait_ge(a_hT_ps, g)
                dve.nop(nofuse=True)
                for t in range(G):
                    last = nc.vector.tensor_scalar(
                        a_h[:, t, :], resid[:, bass.ds(g * G + t, 1), :].rearrange("p a d -> p (a d)"),
                        a_mv[:, t, 0:1], a_rstd[:, t:t + 1], ALU.subtract, ALU.mult)
                last.then_inc(a_norm, 1)

            def a_floor(g):
                dve.wait_ge(sql_ps, g + 1)
                if later(g):
                    dve.wait_ge(guard_set, g)
                nc.vector.tensor_scalar(sq_l[:], bank_a[2][:, 0:G], EPS * EPS, None, ALU.max).then_inc(sql_set, 1)

            def a_adj_l(g):
                dve.wait_ge(gl_ps, g + 1)
                if later(g):
                    dve.wait_ge(outl_ps1, g)
                nc.vector.scalar_tensor_tensor(adj_l[:], tiles(bank_a[1]), 0.0, mask_l[:].unsqueeze(1).broadcast_to([P, G, P]),
                                               ALU.max, ALU.mult).then_inc(adj_l_set, 1)

            def a_values_l(g):
                dve.wait_ge(v_ps, g + 1)
                dve.wait_ge(vg_set, g + 1)
                dve.wait_ge(inv_set, g + 1)
                if later(g):
                    dve.wait_ge(outl_ps1, g)
                nc.vector.scalar_tensor_tensor(v_l[:, :, 0:D], tiles(bank_a[0]), 1.0 - T_WAKE,
                                               inv_norm[:].unsqueeze(2).broadcast_to([P, G, D]), ALU.mult,
                                               ALU.mult).then_inc(vl_set, 1)

            def a_arg_g(g):
                dve.wait_ge(gg_ps, g + 1)
                if later(g):
                    dve.wait_ge(adj_g_set, g)
                nc.vector.tensor_tensor(arg_g[:], tiles(bank_a[2]), mask_g[:].unsqueeze(1).broadcast_to([P, G, P]),
                                        ALU.min).then_inc(arg_g_set, 1)

            def halves(bank):
                return bank[:, 0:2 * (D + 1)].rearrange("p (t d) -> p t d", t=2)

            def a_scale_l(g):
                for h in range(2):
                    dve.wait_ge([outl_ps0, outl_ps1][h], g + 1)
                    if h == 0:
                        dve.wait_ge(guard_set, g + 1)
                    last = nc.vector.scalar_tensor_tensor(
                        den_l[:, 2 * h:2 * h + 2], guard[:, 2 * h:2 * h + 2], EPS, halves(bank_a[h])[:, :, D],
                        ALU.mult, ALU.max)
                last.then_inc(denl_set, 1)
                dve.wait_ge(denl_set, g + 1)
                nc.vector.reciprocal(rec_l[:], den_l[:]).then_inc(recl_set, 1)
                dve.wait_ge(recl_set, g + 1)
                dve.nop(nofuse=True)
                for h in range(2):
                    for t in (2 * h, 2 * h + 1):
                        x_t = resid[:, bass.ds(g * G + t, 1), :].rearrange("p a d -> p (a d)")
                        last = nc.vector.scalar_tensor_tensor(x_t, halves(bank_a[h])[:, t % 2, 0:D], rec_l[:, t:t + 1], x_t,
                                                              ALU.mult, ALU.add)
                    last.then_inc([xl_set0, xl_set1][h], 1)

            def a_scale_g(g):
                for h in range(2):
                    dve.wait_ge([outg_ps0, outg_ps1][h], g + 1)
                    last = nc.vector.tensor_scalar(den_g[:, 2 * h:2 * h + 2], halves(bank_a[2 - 2 * h])[:, :, D], EPS, None,
                                                   ALU.max)
                last.then_inc(deng_set, 1)
                dve.wait_ge(deng_set, g + 1)
                nc.vector.reciprocal(rec_g[:], den_g[:]).then_inc(recg_set, 1)
                dve.wait_ge(recg_set, g + 1)
                dve.wait_ge(xl_set1, g + 1)
                dve.nop(nofuse=True)
                for h in range(2):
                    for t in (2 * h, 2 * h + 1):
                        x_t = resid[:, bass.ds(g * G + t, 1), :].rearrange("p a d -> p (a d)")
                        last = nc.vector.scalar_tensor_tensor(x_t, halves(bank_a[2 - 2 * h])[:, t % 2, 0:D],
                                                              rec_g[:, t:t + 1], x_t, ALU.mult, ALU.add)
                    last.then_inc([x1_half, x1_set][h], 1)

            def b_statistics(g):
                dve.wait_ge(x1_set, g + 1)
                dve.nop(nofuse=True)
                for t in range(G):
                    last = nc.vector.bn_stats(b_st[:, t, :], resid[:, bass.ds(g * G + t, 1), :].rearrange("p a d -> p (a d)"))
                last.then_inc(b_stats, 1)
                dve.wait_ge(b_stats, g + 1)
                dve.nop(nofuse=True)
                for t in range(G):
                    last = nc.vector.bn_aggr(b_mv[:, t, :], b_st[:, t, :])
                last.then_inc(b_aggr, 1)
                dve.wait_ge(b_aggr, g + 1)
                nc.vector.tensor_scalar(b_var[:, 0, :], b_mv[:, :, 1], EPS_LN, None, ALU.add)
                nc.vector.tensor_scalar(b_var[:, 1, :], b_mv[:, :, 1], 1.0 + EPS_RMS, EPS_RMS * EPS_LN,
                                        ALU.mult, ALU.add).then_inc(b_var_set, 1)

            def b_normalise(g):
                dve.wait_ge(b_rs_set, g + 1)
                if later(g):
                    dve.wait_ge(b_ratio_set, g)
                nc.vector.reciprocal(b_rec[:], b_rs[:, 1, :]).then_inc(b_rec_set, 1)
                if later(g):
                    dve.wait_ge(b_hT_ps, g)
                    dve.wait_ge(h2_set, g)
                dve.nop(nofuse=True)
                for t in range(G):
                    last = nc.vector.tensor_scalar(
                        b_h[:, t, :], resid[:, bass.ds(g * G + t, 1), :].rearrange("p a d -> p (a d)"),
                        b_mv[:, t, 0:1], b_rs[:, 1, t:t + 1], ALU.subtract, ALU.mult)
                last.then_inc(b_norm, 1)

            def b_rope_cos(g, half):
                dve.wait_ge([qkv_ps0, qkv_ps1][half], g + 1)
                dve.wait_ge([swap_set0, swap_set1][half], g + 1)
                qk = tiles(bank_b[1 - half], 2)[:, :, 0:QK]
                cos = tab[:, C_COS:C_SIN].unsqueeze(1).broadcast_to([P, 2, QK])
                last = nc.vector.tensor_tensor(rope_c[:, 2 * half:2 * half + 2, :], qk, cos, ALU.mult)
                last.then_inc(rope_c_set, 1)

            def b_rope_add(g):
                dve.wait_ge(rope_c_set, g * 2 + 2)
                dve.wait_ge(rope_s_set, g * 2 + 2)
                if later(g):
                    dve.wait_ge(kT_ps, g)
                nc.vector.tensor_tensor(roped[:], rope_c[:], rope_s[:], ALU.add).then_inc(roped_set, 1)

            def b_row_min(g, h):
                dve.wait_ge(s_ps, g * NH + h + 1)
                if later(g):
                    dve.wait_ge(prob_set, g * NH - NH + h + 1)
                nc.vector.tensor_reduce(row_min[:, h, :], tiles(bank_b[1 - h % 2]), AX_X, ALU.min).then_inc(min_set, 1)

            def c_sum_rec(g):
                dve.wait_ge(prob_set, g * NH + NH)
                if later(g):
                    dve.wait_ge(rec_rows_set, g)
                nc.vector.reciprocal(sum_rec[:], sums[:]).then_inc(sum_rec_set, 1)

            def c_normalise_y(g):
                dve.wait_ge(recT_set, g + 1)
                dve.wait_ge(y_ps, g + 1)
                if later(g):
                    dve.wait_ge(attn_ps, g)
                nc.vector.tensor_tensor(yT[:], tiles(bank_c[0]), rec_t[:], ALU.mult).then_inc(yT_set, 1)

            def c_block_input(g):
                dve.wait_ge(attn_ps, g + 1)
                dve.wait_ge(h2_set, g + 1)
                if later(g):
                    dve.wait_ge(resid_set, g)
                    dve.wait_ge(sq_set, g)
                nc.vector.tensor_tensor(xf[:], tiles(bank_c[1]), h2[:], ALU.add).then_inc(xf_set, 1)

            def c_mean_square(g):
                dve.wait_ge(sq_set, g + 1)
                if later(g):
                    dve.wait_ge(rms_set, g)
                nc.vector.tensor_scalar(ms[:], sum_sq[:], 1.0 / D, EPS_RMS, ALU.mult, ALU.add).then_inc(ms_set, 1)

            def c_flat(g):
                dve.wait_ge(rms_set, g + 1)
                if later(g):
                    dve.wait_ge(scattered, g * (G * 2 * 16))
                    dve.wait_ge(flat_ps, g)
                dve.nop(nofuse=True)
                for t in range(G):
                    last = nc.vector.scalar_tensor_tensor(flat_rows[:, t, 0:D], xf[:, t, :], rms[:, t:t + 1], ln2_row[:],
                                                          ALU.mult, ALU.mult)
                last.then_inc(flat_set, 1)
                dve.wait_ge(id_next, g + 1)
                nc.vector.tensor_copy(flat_rows[:, :, COL_ID], token_id[:]).then_inc(id_set, 1)
                dve.wait_ge(id_set, g + 1)
                nc.vector.tensor_scalar(token_id[:], token_id[:], float(G), None, ALU.add).then_inc(id_next, 1)

            def c_choose(g):
                logits = bank_d[:, 0:G * NE].rearrange("p (t e) -> p t e", t=G)
                dve.wait_ge(router_ps, g + 1)
                dve.nop(nofuse=True)
                for t in range(G):
                    last = nc.vector.max(best[:, t, :], logits[:, t, :])
                last.then_inc(best_set, 1)
                dve.wait_ge(best_set, g + 1)
                dve.nop(nofuse=True)
                for t in range(G):
                    last = nc.vector.max_index(best_at[:, t, :], best[:, t, :], logits[:, t, :])
                last.then_inc(best_at_set, 1)
                dve.wait_ge(best_at_set, g + 1)
                nc.vector.tensor_copy(choice[:].rearrange("p (t n) -> p t n", n=2), best_at[:, :, 0:2]).then_inc(choice_set, 1)
                dve.wait_ge(choice_set, g + 1)
                nc.vector.tensor_tensor(
                    pick[:].rearrange("p t n e -> p (t n) e"), tab[:, C_IOTA:C_UPTO].unsqueeze(1).broadcast_to([P, 2 * G, NE]),
                    choice[:].unsqueeze(2).broadcast_to([P, 2 * G, NE]), ALU.is_equal).then_inc(pick_set, 1)
                nc.vector.tensor_copy(flat_rows[:, :, COL_EXPERT], choice[:].rearrange("p (t n) -> p t n", n=2)[:, :, 0]).then_inc(
                    expert_set, 1)
                dve.wait_ge(pick_set, g + 1)
                if later(g):
                    dve.wait_ge(rank_ps, g)
                nc.vector.tensor_tensor(chosen_b[:], pick[:, :, 0, :], pick[:, :, 1, :], ALU.add).then_inc(chosen_set, 1)
                if later(g):
                    dve.wait_ge(weight_set, g)
                nc.vector.tensor_tensor(below[:], best[:], best[:, :, 0:1].broadcast_to([P, G, NE]), ALU.subtract).then_inc(
                    below_set, 1)

            def c_gates(g):
                dve.wait_ge(weight_set, g + 1)
                nc.vector.tensor_reduce(total[:], weight[:], AX_X, ALU.add).then_inc(total_set, 1)
                nc.vector.tensor_tensor(pair[:], weight[:, :, 0], weight[:, :, 1], ALU.add).then_inc(pair_set, 1)
                dve.wait_ge(total_set, g + 1)
                dve.wait_ge(pair_set, g + 1)
                nc.vector.scalar_tensor_tensor(denom[:], total[:], 1e-9, pair[:], ALU.mult, ALU.add).then_inc(denom_set, 1)
                dve.wait_ge(denom_set, g + 1)
                nc.vector.reciprocal(denom_rec[:], denom[:]).then_inc(denom_rec_set, 1)
                dve.wait_ge(denom_rec_set, g + 1)
                nc.vector.tensor_tensor(flat_rows[:, :, COL_GATE:COL_GATE + 2], weight[:, :, 0:2],
                                        denom_rec[:].unsqueeze(2).broadcast_to([P, G, 2]), ALU.mult).then_inc(gates_set, 1)

            def c_places(g):
                dve.wait_ge(rank_ps, g + 1)
                dve.wait_ge(filled_set, g + 1)
                nc.vector.tensor_tensor(place[:], bank_d[:, RANKS:RANKS + (G + 1) * NE].rearrange("p (t e) -> p t e", e=NE),
                                        filled[:].unsqueeze(1).broadcast_to([P, G + 1, NE]), ALU.add).then_inc(place_set, 1)
                dve.wait_ge(place_set, g + 1)
                nc.vector.tensor_copy(filled[:], place[:, G, :]).then_inc(filled_set, 1)
                nc.vector.tensor_tensor(picked[:], pick[:], place[:, 0:G, :].unsqueeze(2).broadcast_to([P, G, 2, NE]),
                                        ALU.mult).then_inc(picked_set, 1)
                dve.wait_ge(picked_set, g + 1)
                nc.vector.tensor_reduce(place_f[:], picked[:].rearrange("p t n e -> p (t n) e"), AX_X, ALU.add).then_inc(
                    place_f_set, 1)
                dve.wait_ge(place_f_set, g + 1)
                nc.vector.tensor_copy(place_i[:], place_f[:]).then_inc(place_i_set, 1)

            def step(k):
                at(k, a_statistics)
                at(k - 4, c_choose)
                at(k, a_normalise)
                at(k - 2, b_rope_cos, 0)
                at(k - 1, a_floor)
                at(k - 4, c_places)
                at(k - 3, c_sum_rec)
                at(k - 2, b_rope_cos, 1)
                at(k - 4, c_gates)
                at(k - 2, b_rope_add)
                at(k - 1, a_adj_l)
                at(k - 1, a_values_l)
                at(k - 1, a_arg_g)
                at(k - 3, c_normalise_y)
                at(k - 1, a_scale_l)
                at(k - 2, b_row_min, 0)
                at(k - 2, b_row_min, 1)
                at(k - 3, c_block_input)
                at(k - 1, a_scale_g)
                at(k - 2, b_row_min, 2)
                at(k - 3, c_mean_square)
                at(k - 1, b_statistics)
                at(k - 2, b_row_min, 3)
                at(k - 3, c_flat)
                at(k - 1, b_normalise)

            for k in range(LAG + 1):
                step(k)
            with dve.Fori(LAG + 1, NG) as k:
                step(k)
            for k in range(NG, NG + LAG):
                step(k)

            dve.wait_ge(filled_set, NG + 1)
            nc.vector.tensor_tensor(counts[:], filled[:], tab[:, C_BASE:C_IOTA], ALU.subtract).then_inc(table_step, 1)
            nc.vector.tensor_copy(region_end_i[:], filled[:])
            dve.wait_ge(table_step, 1)
            n_steps = N_TOK // ROWS
            nc.vector.tensor_tensor(over[:], counts[:].unsqueeze(2).broadcast_to([P, NE, n_steps]),
                                    tab[:, C_STEP:C_TILE].unsqueeze(1).broadcast_to([P, NE, n_steps]), ALU.is_gt).then_inc(
                table_step, 1)
            dve.wait_ge(table_step, 2)
            nc.vector.tensor_reduce(n_tiles[:], over[:], AX_X, ALU.add).then_inc(table_step, 1)
            dve.wait_ge(table_step, 3)
            nc.vector.tensor_tensor(upto[:], tab[:, C_UPTO:C_STEP].rearrange("p (e j) -> p e j", e=NE),
                                    n_tiles[:].unsqueeze(1).broadcast_to([P, NE, NE]), ALU.mult).then_inc(table_step, 1)
            dve.wait_ge(table_step, 4)
            nc.vector.tensor_reduce(tiles_upto[:], upto[:], AX_X, ALU.add).then_inc(table_step, 1)
            dve.wait_ge(table_step, 5)
            numbers = tab[:, C_TILE:C_PAD]
            nc.vector.tensor_tensor(passed[:], numbers.unsqueeze(2).broadcast_to([P, N_TILES, NE]),
                                    tiles_upto[:].unsqueeze(1).broadcast_to([P, N_TILES, NE]), ALU.is_ge).then_inc(table_step, 1)
            dve.wait_ge(table_step, 6)
            nc.vector.tensor_reduce(tile_expert[:], passed[:], AX_X, ALU.add).then_inc(table_step, 1)
            nc.vector.tensor_tensor(passed_n[:], passed[:], n_tiles[:].unsqueeze(1).broadcast_to([P, N_TILES, NE]),
                                    ALU.mult).then_inc(table_step, 1)
            dve.wait_ge(table_step, 8)
            nc.vector.tensor_reduce(tile_first[:], passed_n[:], AX_X, ALU.add).then_inc(table_step, 1)
            dve.wait_ge(table_step, 9)
            nc.vector.tensor_tensor(tile_at[:], numbers, tile_first[:], ALU.subtract).then_inc(table_step, 1)
            dve.wait_ge(table_step, 10)
            nc.vector.tensor_scalar(tile_first[:], tile_expert[:], float(REGION), None, ALU.mult).then_inc(table_step, 1)
            dve.wait_ge(table_step, 11)
            nc.vector.scalar_tensor_tensor(tile_row[:], tile_at[:], float(ROWS), tile_first[:], ALU.mult, ALU.add).then_inc(
                table_step, 1)
            dve.wait_ge(table_step, 12)
            nc.vector.tensor_scalar(tile_weights_i[:], tile_expert[:], float(NE - 1), None, ALU.min)
            nc.vector.tensor_scalar(tile_row_i[:], tile_row[:], float(NE * REGION), None, ALU.min).then_inc(table_set, 1)

            def gates(pair_no, u):
                j = pair_no * 2 + u
                rows = in_rows[:, u, :, :]
                dve.wait_ge([rows_loaded0, rows_loaded1][u], pair_no * 16 + 16)
                dve.nop(nofuse=True)
                nc.vector.tensor_scalar(second[:, u, :], rows[:, :, COL_EXPERT], tile_expert[:, bass.ds(j, 1)], None,
                                        ALU.not_equal).then_inc(second_set, 1)
                nc.vector.tensor_tensor(gate_diff[:, u, :], rows[:, :, COL_GATE + 1], rows[:, :, COL_GATE],
                                        ALU.subtract).then_inc(gdiff_set, 1)
                dve.wait_ge(second_set, j + 1)
                if later(pair_no):
                    dve.wait_ge(dest_set, j - 1)
                nc.vector.scalar_tensor_tensor(dest_f[:, u, :], second[:, u, :], float(N_TOK), rows[:, :, COL_ID],
                                               ALU.mult, ALU.add).then_inc(destf_set, 1)
                dve.wait_ge(gdiff_set, j + 1)
                nc.vector.tensor_tensor(gate_step[:, u, :], second[:, u, :], gate_diff[:, u, :], ALU.mult).then_inc(gstep_set, 1)
                dve.wait_ge(gstep_set, j + 1)
                nc.vector.tensor_tensor(gate[:, u, :], gate_step[:, u, :], rows[:, :, COL_GATE], ALU.add).then_inc(gate_set, 1)

            def places(pair_no, u):
                j = pair_no * 2 + u
                dve.wait_ge(destf_set, j + 1)
                if later(pair_no):
                    dve.wait_ge([placed0, placed1][u], pair_no * (SUB * 16))
                nc.vector.tensor_copy(dest_i[:, u, :], dest_f[:, u, :]).then_inc(dest_set, 1)

            def rows_rest(pair_no, u):
                j = pair_no * 2 + u
                dve.wait_ge(in_hi_set, j + 1)
                if later(pair_no):
                    dve.wait_ge(gate_ps, j * NC - NC)
                nc.vector.tensor_tensor(in_lo[:, u, :], bank_in[:], in_hi[:, u, :], ALU.subtract).then_inc(in_lo_set, 1)

            def weights_rest(pair_no, u):
                j = pair_no * 2 + u
                dve.wait_ge(w_hi_set, j + 1)
                if later(pair_no):
                    dve.wait_ge(gate_ps, j * NC - NC)
                nc.vector.tensor_tensor(w_lo[:, u, :], w13[:, u, :], w_hi[:, u, :], ALU.subtract).then_inc(w_lo_set, 1)

            def hidden_chunk(pair_no, u, c):
                j = pair_no * 2 + u
                n = CHUNKS[c][1]
                dve.wait_ge(gate_ps, j * NC + c + 1)
                dve.wait_ge(silu_set, j * NC + c + 1)
                if later(pair_no):
                    dve.wait_ge(down_ps, j - 1)
                nc.vector.tensor_tensor(hidden[0:n, u, c, :], bank_gate[(u * NC + c) % 2][0:n, :], silu[0:n, (u * NC + c) % 2, :],
                                        ALU.mult).then_inc(hidden_set, 1)

            def scale_rows(pair_no, u):
                j = pair_no * 2 + u
                dve.wait_ge(down_ps, j + 1)
                dve.wait_ge(gate_set, j + 1)
                if later(pair_no):
                    dve.wait_ge([placed0, placed1][u], pair_no * (SUB * 16))
                nc.vector.tensor_tensor(out_rows[:, u, :, :], tiles(bank_down[u]), gate[:, u, :].unsqueeze(2).broadcast_to([P, SUB, D]),
                                        ALU.mult).then_inc(outrows_set, 1)

            def tile(pair_no, u, *next_tile):
                if next_tile:
                    weights_rest(*next_tile)
                    rows_rest(*next_tile)
                hidden_chunk(pair_no, u, 1)
                hidden_chunk(pair_no, u, 2)
                if next_tile:
                    gates(*next_tile)
                    hidden_chunk(*next_tile, 0)
                places(pair_no, u)
                scale_rows(pair_no, u)

            def tile_pair(pair_no):
                tile(pair_no, 0, pair_no, 1)
                tile(pair_no, 1, pair_no + 1, 0)

            weights_rest(0, 0)
            rows_rest(0, 0)
            gates(0, 0)
            hidden_chunk(0, 0, 0)
            tile_pair(0)
            with dve.Fori(1, N_TILES // 2 - 1) as k:
                tile_pair(k)
            tile(N_TILES // 2 - 1, 0, N_TILES // 2 - 1, 1)
            tile(N_TILES // 2 - 1, 1)

            for i in range(NB // FINAL):
                r = resid[:, i * FINAL:(i + 1) * FINAL, :]
                dve.wait_ge([final_loaded0, final_loaded1][i % 2], (i // 2 + 1) * 32)
                if i == 0:
                    dve.wait_ge(resid_set, NG)
                nc.vector.tensor_tensor(r, r, final_in[:, i % 2, 0, :, :], ALU.add).then_inc(sum_half, 1)
                dve.wait_ge(sum_half, i + 1)
                nc.vector.tensor_tensor(r, r, final_in[:, i % 2, 1, :, :], ALU.add).then_inc(sum_set, 1)

        @block.scalar
        def _(act):
            act.wait_ge(ones_set, 1)

            def copy_bank(dst, bank):
                return nc.scalar.activation(dst, bank, ACT.Copy)

            def a_copy_hT(g):
                act.wait_ge(a_hT_ps, g + 1)
                if later(g):
                    act.wait_ge(v_ps, g)
                copy_bank(a_hT[:], tiles(bank_a[0])).then_inc(a_hT_set, 1)

            def a_copy_zl(g):
                act.wait_ge(zl_ps, g + 1)
                if later(g):
                    act.wait_ge(gl_ps, g)
                copy_bank(zl[:], tiles(bank_a[1])).then_inc(zl_set, 1)

            def a_square_zl(g):
                act.wait_ge(zl_ps, g + 1)
                if later(g):
                    act.wait_ge(sql_ps, g)
                nc.scalar.activation(zl2[:], tiles(bank_a[1]), ACT.Square).then_inc(zl_sq, 1)

            def a_copy_zg(g):
                act.wait_ge(zg_ps, g + 1)
                if later(g):
                    act.wait_ge(gg_ps, g)
                copy_bank(zg[:], tiles(bank_a[2])).then_inc(zg_set, 1)

            def a_square_zg(g):
                act.wait_ge(zg_ps, g + 1)
                if later(g):
                    act.wait_ge(gg_ps, g)
                nc.scalar.activation(zg2[:], tiles(bank_a[2]), ACT.Square).then_inc(zg_sq, 1)

            def a_copy_values(g):
                act.wait_ge(v_ps, g + 1)
                if later(g):
                    act.wait_ge(outg_ps1, g)
                nc.scalar.activation(v_g[:, :, 0:D], tiles(bank_a[0]), ACT.Copy, scale=T_WAKE).then_inc(vg_set, 1)

            def a_exp(g):
                act.wait_ge(arg_g_set, g + 1)
                if later(g):
                    act.wait_ge(outg_ps1, g)
                nc.scalar.activation(adj_g[:], arg_g[:], ACT.Exp).then_inc(adj_g_set, 1)

            def b_copy_hT(g):
                act.wait_ge(b_hT_ps, g + 1)
                if later(g):
                    act.wait_ge(qkv_ps1, g)
                copy_bank(b_hT[:], tiles(bank_b[0])).then_inc(b_hT_set, 1)

            def b_copy_qkv(g, half):
                qkv = tiles(bank_b[1 - half], 2)
                t = slice(2 * half, 2 * half + 2)
                act.wait_ge([qkv_ps0, qkv_ps1][half], g + 1)
                if later(g):
                    act.wait_ge(rope_s_set, g * 2 - 1 + half)
                    act.wait_ge(y_ps, g)
                src = qkv[:, :, 0:QK].rearrange("p t (h two e) -> p t h two e", two=2, e=HD // 2)
                dst = swapped[:, t, :].rearrange("p t (h two e) -> p t h two e", two=2, e=HD // 2)
                for part in range(2):
                    copy_bank(dst[:, :, :, part, :], src[:, :, :, 1 - part, :])
                copy_bank(v_attn[:, t, :, :], qkv[:, :, QK:QKV].rearrange("p t (k d) -> p t k d", k=NKV)).then_inc(
                    [swap_set0, swap_set1][half], 1)

            def b_copy_q(g):
                act.wait_ge(qT_ps, g + 1)
                if later(g):
                    act.wait_ge(s_ps, g * NH)
                copy_bank(qT[:], tiles(bank_b[1])).then_inc(qT_set, 1)

            def b_copy_k(g):
                act.wait_ge(kT_ps, g + 1)
                if later(g):
                    act.wait_ge(s_ps, g * NH)
                for r in range(NREP):
                    last = copy_bank(kT[r * NKV * HD:(r + 1) * NKV * HD, :, :], tiles(bank_b[0])[0:NKV * HD, :, :])
                last.then_inc(kT_set, 1)

            def b_exp(g, h):
                act.wait_ge(min_set, g * NH + h + 1)
                if later(g):
                    act.wait_ge(pT_ps, g * NH - NH + h + 1)
                    act.wait_ge(sum_rec_set, g)
                act.nop(nofuse=True)
                for t in range(G):
                    last = nc.scalar.activation(probs[:, h, t, :], tiles(bank_b[1 - h % 2])[:, t, :], ACT.Exp,
                                                bias=row_min[:, h, t:t + 1], scale=-1.0, accum_out=sums[:, h, t:t + 1])
                last.then_inc(prob_set, 1)

            def c_spread_rec(g):
                act.wait_ge(sum_rec_set, g + 1)
                if later(g):
                    act.wait_ge(recT_ps, g)
                copy_bank(rec_rows[:], sum_rec[:].rearrange("p h t -> p t h").unsqueeze(3).broadcast_to(
                    [P, G, NH, HD])).then_inc(rec_rows_set, 1)

            def c_copy_rec(g):
                act.wait_ge(recT_ps, g + 1)
                if later(g):
                    act.wait_ge(yT_set, g)
                copy_bank(rec_t[:], tiles(bank_c[1])).then_inc(recT_set, 1)

            def c_copy_probs(g, h):
                act.wait_ge(pT_ps, g * NH + h + 1)
                if later(g):
                    act.wait_ge(y_ps, g)
                copy_bank(probs_t[:, h, :, :], tiles(bank_c[h % 2])).then_inc(pT_set, 1)

            def c_square(g):
                act.wait_ge(xf_set, g + 1)
                if later(g):
                    act.wait_ge(ms_set, g)
                for t in range(G):
                    last = nc.scalar.activation(sq_junk[:, t, :], xf[:, t, :], ACT.Square, accum_out=sum_sq[:, t:t + 1])
                last.then_inc(sq_set, 1)

            def c_copy_flatT(g):
                act.wait_ge(flat_ps, g + 1)
                if later(g):
                    act.wait_ge(router_ps, g)
                copy_bank(flatT[:], tiles(bank_d)).then_inc(flatT_set, 1)

            def c_weights(g):
                act.wait_ge(below_set, g + 1)
                if later(g):
                    act.wait_ge(gates_set, g)
                nc.scalar.activation(weight[:], below[:], ACT.Exp).then_inc(weight_set, 1)

            def step(k):
                at(k - 3, c_copy_probs, 2)
                at(k - 4, c_copy_flatT)
                at(k - 3, c_copy_probs, 3)
                at(k - 2, b_copy_hT)
                at(k - 1, a_copy_zg)
                at(k - 1, a_square_zg)
                at(k - 1, a_copy_values)
                at(k - 1, a_square_zl)
                at(k - 2, b_copy_qkv, 0)
                at(k - 1, a_copy_zl)
                at(k - 2, b_copy_qkv, 1)
                at(k - 4, c_weights)
                at(k - 3, c_spread_rec)
                at(k - 2, b_copy_q)
                at(k - 3, c_copy_rec)
                at(k - 2, b_copy_k)
                at(k - 1, a_exp)
                at(k - 2, b_exp, 0)
                at(k - 2, b_exp, 1)
                at(k - 3, c_square)
                at(k - 2, c_copy_probs, 0)
                at(k, a_copy_hT)
                at(k - 2, b_exp, 2)
                at(k - 2, c_copy_probs, 1)
                at(k - 2, b_exp, 3)

            for k in range(LAG + 1):
                step(k)
            with act.Fori(LAG + 1, NG) as k:
                step(k)
            for k in range(NG, NG + LAG):
                step(k)

            def weights_upper(pair_no, u):
                j = pair_no * 2 + u
                act.wait_ge([w13_loaded0, w13_loaded1][u], pair_no * 16 + 16)
                if later(pair_no):
                    act.wait_ge(gate_ps, j * NC - NC)
                copy_bank(w_hi[:, u, :], w13[:, u, :]).then_inc(w_hi_set, 1)

            def rows_upper(pair_no, u):
                j = pair_no * 2 + u
                act.wait_ge(inT_ps, j + 1)
                if later(pair_no):
                    act.wait_ge(gate_ps, j * NC - NC)
                copy_bank(in_hi[:, u, :], bank_in[:]).then_inc(in_hi_set, 1)

            def silu_chunk(pair_no, u, c):
                j = pair_no * 2 + u
                m, n = u * NC + c, CHUNKS[c][1]
                act.wait_ge(up_ps, j * NC + c + 1)
                if later(pair_no) or m >= 2:
                    act.wait_ge(hidden_set, j * NC + c - 1)
                nc.scalar.activation(silu[0:n, m % 2, :], bank_up[m % 2][0:n, :], ACT.Silu).then_inc(silu_set, 1)

            def tile(pair_no, u, *next_tile):
                if next_tile:
                    weights_upper(*next_tile)
                    rows_upper(*next_tile)
                silu_chunk(pair_no, u, 1)
                silu_chunk(pair_no, u, 2)
                if next_tile:
                    silu_chunk(*next_tile, 0)

            def tile_pair(pair_no):
                tile(pair_no, 0, pair_no, 1)
                tile(pair_no, 1, pair_no + 1, 0)

            weights_upper(0, 0)
            rows_upper(0, 0)
            silu_chunk(0, 0, 0)
            tile_pair(0)
            with act.Fori(1, N_TILES // 2 - 1) as k:
                tile_pair(k)
            tile(N_TILES // 2 - 1, 0, N_TILES // 2 - 1, 1)
            tile(N_TILES // 2 - 1, 1)

            for i in range(NB // FINAL):
                act.wait_ge(sum_set, i + 1)
                act.dma_start(out[:, i * FINAL:(i + 1) * FINAL, :], resid[:, i * FINAL:(i + 1) * FINAL, :]).then_inc(
                    out_stored, 16)
            act.wait_ge(out_stored, NB // FINAL * 16)

        @block.tensor
        def _(pe):
            pe.wait_ge(w_loaded, W_LOADED)
            nc.tensor.matmul(bank_a[0][:, 0:D], w_v_t[:], w_o_gnn[:], start=True, stop=True).then_inc(wvo_ps, 1)
            pe.wait_ge(const_loaded, 16)
            pe.wait_ge(consts_set, 1)
            pe.wait_ge(ones_set, 1)
            pe.wait_ge(w_qkv_set, 1)
            pe.wait_ge(wvo_set, 1)

            def transposes(bank, srcs):
                for t, src in enumerate(srcs):
                    last = nc.tensor.transpose(bank[:, t * P:(t + 1) * P], src, ident)
                return last

            def a_transpose(g):
                pe.wait_ge(a_norm, g + 1)
                if later(g):
                    pe.wait_ge(x1_set, g)
                transposes(bank_a[0], [a_h[:, t, :] for t in range(G)]).then_inc(a_hT_ps, 1)

            def a_project(g):
                pe.wait_ge(a_hT_set, g + 1)
                if later(g):
                    pe.wait_ge(xl_set1, g)
                hT = a_hT[:].rearrange("p t d -> p (t d)")
                nc.tensor.matmul(bank_a[1][:], w_l[:], hT, start=True, stop=True).then_inc(zl_ps, 1)
                if later(g):
                    pe.wait_ge(x1_half, g)
                nc.tensor.matmul(bank_a[2][:], w_g[:], hT, start=True, stop=True).then_inc(zg_ps, 1)

            def a_project_v(g):
                pe.wait_ge(a_hT_set, g + 1)
                for t in range(G):
                    last = nc.tensor.matmul(bank_a[0][:, t * P:(t + 1) * P], a_hT[:, t, :], w_vo[:], start=True, stop=True)
                last.then_inc(v_ps, 1)

            def a_gram_l(g):
                pe.wait_ge(zl_set, g + 1)
                pe.wait_ge(zl_sq, g + 1)
                for t in range(G):
                    last = nc.tensor.matmul(bank_a[1][:, t * P:(t + 1) * P], zl[:, t, :], zl[:, t, :], start=True, stop=True)
                last.then_inc(gl_ps, 1)

            def a_norms(g):
                pe.wait_ge(zl_sq, g + 1)
                pe.wait_ge(zg_set, g + 1)
                pe.wait_ge(zg_sq, g + 1)
                for t in range(G):
                    last = nc.tensor.matmul(bank_a[2][:, t:t + 1], zl2[:, t, :], v_g[:, 0, D:D + 1], start=True, stop=True)
                last.then_inc(sql_ps, 1)

            def a_gram_g(g):
                pe.wait_ge(zg_sq, g + 1)
                pe.wait_ge(sql_set, g + 1)
                for t in range(G):
                    o = bank_a[2][:, t * P:(t + 1) * P]
                    nc.tensor.matmul(o, zg[:, t, :], zg[:, t, :], start=True, stop=False)
                    nc.tensor.matmul(o, minus_half[:], zg2[:, t, :], start=False, stop=False)
                    last = nc.tensor.matmul(o, zg2[:, t, :], minus_half[:], start=False, stop=True)
                last.then_inc(gg_ps, 1)

            def a_apply(g, kernel, values, banks, ready):
                for h in range(2):
                    for t in range(2):
                        last = nc.tensor.matmul(banks[h][:, t * (D + 1):(t + 1) * (D + 1)], kernel[:, 2 * h + t, :],
                                                values[:, 2 * h + t, :], start=True, stop=True)
                    last.then_inc(ready[h], 1)

            def a_apply_l(g):
                pe.wait_ge(adj_l_set, g + 1)
                pe.wait_ge(vl_set, g + 1)
                pe.wait_ge(vl_col_set, g + 1)
                a_apply(g, adj_l, v_l, [bank_a[0], bank_a[1]], [outl_ps0, outl_ps1])

            def a_apply_g(g, h):
                if h == 0:
                    pe.wait_ge(adj_g_set, g + 1)
                    pe.wait_ge(arg_g_set, g + 1)
                    pe.wait_ge(vg_set, g + 1)
                else:
                    pe.wait_ge(xl_set0, g + 1)
                for t in range(2):
                    last = nc.tensor.matmul(bank_a[2 - 2 * h][:, t * (D + 1):(t + 1) * (D + 1)], adj_g[:, 2 * h + t, :],
                                            v_g[:, 2 * h + t, :], start=True, stop=True)
                last.then_inc([outg_ps0, outg_ps1][h], 1)

            def b_transpose(g):
                pe.wait_ge(b_norm, g + 1)
                if later(g):
                    pe.wait_ge(prob_set, g * NH)
                transposes(bank_b[0], [b_h[:, t, :] for t in range(G)]).then_inc(b_hT_ps, 1)

            def b_project(g, half):
                pe.wait_ge(b_hT_set, g + 1)
                if half == 0 and later(g):
                    pe.wait_ge(prob_set, g * NH - 1)
                for t in range(2):
                    last = nc.tensor.matmul(bank_b[1 - half][:, t * QKV:(t + 1) * QKV], b_hT[:, 2 * half + t, :], w_qkv[:],
                                            start=True, stop=True)
                last.then_inc([qkv_ps0, qkv_ps1][half], 1)

            def b_transpose_q(g):
                pe.wait_ge(roped_set, g + 1)
                transposes(bank_b[1], [roped[:, t, 0:NH * HD] for t in range(G)]).then_inc(qT_ps, 1)

            def b_transpose_k(g):
                for t in range(G):
                    last = nc.tensor.transpose(bank_b[0][0:NKV * HD, t * P:(t + 1) * P], roped[:, t, NH * HD:QK], ident)
                last.then_inc(kT_ps, 1)

            def b_scores(g, h):
                bank = bank_b[1 - h % 2]
                if h == 0:
                    pe.wait_ge(qT_set, g + 1)
                    pe.wait_ge(kT_set, g + 1)
                if h >= 2:
                    pe.wait_ge(prob_set, g * NH + h - 1)
                nc.tensor.matmul(bank[:], ident_b[:], causal_b[:].unsqueeze(1).broadcast_to([P, G, P]), start=True, stop=False,
                                 skip_group_check=True)
                heads = slice(h * HD, (h + 1) * HD)
                for t in range(G):
                    last = nc.tensor.matmul(bank[:, t * P:(t + 1) * P], qT[heads, t, :], kT[heads, t, :], start=False, stop=True,
                                            skip_group_check=True)
                last.then_inc(s_ps, 1)

            def c_transpose_probs(g, h):
                pe.wait_ge(prob_set, g * NH + h + 1)
                if h >= 2:
                    pe.wait_ge(pT_set, g * NH + h - 1)
                elif later(g):
                    pe.wait_ge([yT_set, xf_set][h], g)
                transposes(bank_c[h % 2], [probs[:, h, t, :] for t in range(G)]).then_inc(pT_ps, 1)

            def c_transpose_rec(g):
                pe.wait_ge(rec_rows_set, g + 1)
                pe.wait_ge(pT_set, g * NH + NH)
                transposes(bank_c[1], [rec_rows[:, t, :, :].rearrange("p h d -> p (h d)") for t in range(G)]).then_inc(recT_ps, 1)

            def c_values(g):
                pe.wait_ge(pT_set, g * NH + NH)
                for t in range(G):
                    for h in range(NH):
                        last = nc.tensor.matmul(bank_c[0][h * HD:(h + 1) * HD, t * P:(t + 1) * P], v_attn[:, t, h % NKV, :],
                                                probs_t[:, h, t, :], start=True, stop=True)
                last.then_inc(y_ps, 1)

            def c_output(g):
                pe.wait_ge(yT_set, g + 1)
                for t in range(G):
                    last = nc.tensor.matmul(bank_c[1][:, t * P:(t + 1) * P], yT[:, t, :], w_o[:], start=True, stop=True)
                last.then_inc(attn_ps, 1)

            def c_transpose_flat(g):
                pe.wait_ge(flat_set, g + 1)
                if later(g):
                    pe.wait_ge(place_set, g)
                transposes(bank_d, [flat_rows[:, t, 0:D] for t in range(G)]).then_inc(flat_ps, 1)

            def c_router(g):
                pe.wait_ge(flatT_set, g + 1)
                for t in range(G):
                    last = nc.tensor.matmul(bank_d[:, t * NE:(t + 1) * NE], flatT[:, t, :], w_router[:], start=True, stop=True)
                last.then_inc(router_ps, 1)

            def c_rank(g):
                pe.wait_ge(chosen_set, g + 1)
                o = bank_d[:, RANKS:RANKS + (G + 1) * NE]
                last = nc.tensor.matmul(o[:, 0:G * NE], upper_b[:], chosen_b[:].rearrange("p t e -> p (t e)"), start=True,
                                        stop=False, skip_group_check=True)
                for t in range(G):
                    n = G - t
                    last = nc.tensor.matmul(o[:, (t + 1) * NE:(G + 1) * NE], ones_b[:],
                                            chosen_b[:, t:t + 1, :].broadcast_to([P, n, NE]), start=False, stop=t == G - 1,
                                            skip_group_check=True)
                last.then_inc(rank_ps, 1)

            def step(k):
                at(k - 4, c_router)
                at(k - 3, c_values)
                at(k - 2, b_project, 0)
                at(k - 4, c_rank)
                at(k - 1, a_norms)
                at(k - 2, b_project, 1)
                at(k - 1, a_gram_l)
                at(k - 1, a_gram_g)
                at(k - 2, b_transpose_q)
                at(k - 3, c_transpose_rec)
                at(k - 2, b_transpose_k)
                at(k - 1, a_apply_l)
                at(k - 2, b_scores, 0)
                at(k - 1, a_apply_g, 0)
                at(k - 2, b_scores, 1)
                at(k - 3, c_output)
                at(k - 1, a_apply_g, 1)
                at(k - 2, c_transpose_probs, 0)
                at(k - 2, b_scores, 2)
                at(k - 2, c_transpose_probs, 1)
                at(k, a_transpose)
                at(k - 2, b_scores, 3)
                at(k, a_project)
                at(k - 2, c_transpose_probs, 2)
                at(k, a_project_v)
                at(k - 3, c_transpose_flat)
                at(k - 2, c_transpose_probs, 3)
                at(k - 1, b_transpose)

            for k in range(LAG + 1):
                step(k)
            with pe.Fori(LAG + 1, NG) as k:
                step(k)
            for k in range(NG, NG + LAG):
                step(k)

            def turn_rows(pair_no, u):
                pe.wait_ge([rows_loaded0, rows_loaded1][u], pair_no * 16 + 16)
                if u or later(pair_no):
                    pe.wait_ge(in_lo_set, pair_no * 2 + u)
                for i in range(SUB):
                    last = nc.tensor.transpose(bank_in[:, i * P:(i + 1) * P], in_rows[:, u, i, 0:D], ident)
                last.then_inc(inT_ps, 1)

            def up_and_gate(pair_no, u, c):
                j = pair_no * 2 + u
                if c == 0:
                    pe.wait_ge(in_hi_set, j + 1)
                    pe.wait_ge(w_lo_set, j + 1)
                    pe.wait_ge(in_lo_set, j + 1)

                def product(bank, cols):
                    nc.tensor.matmul(bank, w_hi[:, u, cols], in_hi[:, u, :], start=True, stop=False)
                    nc.tensor.matmul(bank, w_hi[:, u, cols], in_lo[:, u, :], start=False, stop=False)
                    return nc.tensor.matmul(bank, w_lo[:, u, cols], in_hi[:, u, :], start=False, stop=True)

                c0, n = CHUNKS[c]
                m = u * NC + c
                full = later(pair_no) or m >= 2
                if full:
                    pe.wait_ge(silu_set, j * NC + c - 1)
                product(bank_up[m % 2][0:n, :], slice(c0, c0 + n)).then_inc(up_ps, 1)
                if full:
                    pe.wait_ge(hidden_set, j * NC + c - 1)
                product(bank_gate[m % 2][0:n, :], slice(HID + c0, HID + c0 + n)).then_inc(gate_ps, 1)

            def down(pair_no, u):
                j = pair_no * 2 + u
                pe.wait_ge(hidden_set, j * NC + NC)
                pe.wait_ge([w2_loaded0, w2_loaded1][u], pair_no * 16 + 16)
                if later(pair_no):
                    pe.wait_ge(outrows_set, j - 1)
                for i in range(SUB):
                    for c, (_, n) in enumerate(CHUNKS):
                        last = nc.tensor.matmul(bank_down[u][:, i * P:(i + 1) * P], hidden[0:n, u, c, i * P:(i + 1) * P],
                                                w2[0:n, u, c * D:(c + 1) * D], start=c == 0, stop=c == NC - 1)
                last.then_inc(down_ps, 1)

            def tile(pair_no, u, *next_tile):
                if next_tile:
                    turn_rows(*next_tile)
                up_and_gate(pair_no, u, 1)
                up_and_gate(pair_no, u, 2)
                if next_tile:
                    up_and_gate(*next_tile, 0)
                down(pair_no, u)

            def tile_pair(pair_no):
                tile(pair_no, 0, pair_no, 1)
                tile(pair_no, 1, pair_no + 1, 0)

            turn_rows(0, 0)
            up_and_gate(0, 0, 0)
            tile_pair(0)
            with pe.Fori(1, N_TILES // 2 - 1) as k:
                tile_pair(k)
            tile(N_TILES // 2 - 1, 0, N_TILES // 2 - 1, 1)
            tile(N_TILES // 2 - 1, 1)


def kernel(**inputs):
    import numpy as _np
    import concourse.bacc as _bacc
    from concourse import mybir as _mybir
    from concourse.bass_utils import run_bass_kernel_spmd as _run

    nc = _bacc.Bacc("TRN2", target_bir_lowering=False, num_devices=1)
    f = {k: _np.asarray(v) for k, v in inputs.items()}
    wq = f["L0_ffn_wq"].reshape(NH, HD, D)[HEADS].reshape(NH * HD, D)
    wo = f["L0_ffn_wo"].reshape(D, NH, HD)[:, HEADS].reshape(D, NH * HD)
    laid = {
        "x": f["x"].transpose(1, 0, 2),
        "adj_t": _np.ascontiguousarray(f["adj"].T).view(_np.int32),
        "wl": f["L0_gnn_Wl"],
        "wg": f["L0_gnn_Wg"],
        "wv_t": f["L0_gnn_Wv"].T,
        "wo_gnn": f["L0_gnn_Wo"],
        "ln1": f["L0_ffn_ln1_w"].reshape(D, 1),
        "ln2": f["L0_ffn_ln2_w"],
        "wqkv_t": _np.concatenate([wq, f["L0_ffn_wk"], f["L0_ffn_wv"]], 0).T,
        "wo_t": wo.T,
        "router_t": f["L0_ffn_router_w"].T,
        "w1_t": f["L0_ffn_w1"].transpose(2, 0, 1),
        "w2_t": f["L0_ffn_w2"].transpose(2, 0, 1),
        "w3_t": f["L0_ffn_w3"].transpose(2, 0, 1),
        "table": constants(),
    }
    arrays, args = {}, []
    for name, a in laid.items():
        a = _np.ascontiguousarray(a)
        arrays[f"in_{name}"] = a
        args.append(nc.dram_tensor(f"in_{name}", a.shape, _mybir.dt.from_np(a.dtype), kind="ExternalInput").ap())
    args.append(nc.dram_tensor("out_0", (P, NB, D), _mybir.dt.float32, kind="ExternalOutput").ap())
    build(nc, *args)
    r = _run(nc, [arrays], core_ids=[0])
    return _np.ascontiguousarray(r.results[0]["out_0"].transpose(1, 0, 2))
```
